# Optimizing a Trainium2 kernel written in Bass

```python
import numpy as np
import jax
import jax.numpy as jnp

def _softmax(x, axis=-1):
    return jax.nn.softmax(x, axis=axis)

def _gelu(x):
    return jax.nn.gelu(x, approximate=True)

def _silu(x):
    return jax.nn.silu(x)

def _sigmoid(x):
    return jax.nn.sigmoid(x)

def _layernorm(x, axis=-1, eps=1e-05):
    m = jnp.mean(x, axis=axis, keepdims=True)
    v = jnp.var(x, axis=axis, keepdims=True)
    return (x - m) / jnp.sqrt(v + eps)

def _scatter_add(tgt, idx, src, axis=0):
    return tgt.at[idx].add(src)

def _segment_sum(src, seg, n):
    return jax.ops.segment_sum(src, seg, n)
kernel_name = 'mk_perceiver_d4_seqx_r4_21770a'

def setup_inputs(seed: int=0):
    np.random.seed(seed)
    _w = jnp.asarray

    def _rec_inputs():
        import jax
        import jax.numpy as jnp
        _rk = jax.random.key(seed)
        x = -0.0002928 + 1 * jax.random.normal(jax.random.fold_in(_rk, 1), (16, 64, 256), jnp.float32)
        _lenS = 64 - jax.random.randint(jax.random.fold_in(_rk, 7), (16,), 0, max(1, 64 // 4) + 1, jnp.int32)
        _lenS2 = 1601 - jax.random.randint(jax.random.fold_in(_rk, 8), (16,), 0, max(1, 1601 // 4) + 1, jnp.int32)
        _ctx_1024P = jax.random.normal(jax.random.fold_in(_rk, 11), (16, 16, 256), jnp.float32)
        _ctx_1024c = jax.random.dirichlet(jax.random.fold_in(_rk, 511), 0.3 * jnp.ones((16,), jnp.float32), (16, 1601))
        _ctx_1024t = jnp.einsum('bsk,bkd->bsd', _ctx_1024c, _ctx_1024P)
        _ctx_1024t = _ctx_1024t * jax.lax.rsqrt(jnp.mean(jnp.square(_ctx_1024t)) + 1e-12) * 0.953939
        ctx_1024 = -1.39393e-06 + 0.999914 * (_ctx_1024t + 0.3 * jax.random.normal(jax.random.fold_in(_rk, 611), (16, 1601, 256), jnp.float32))
        itok_BxS2_0_2047 = jax.random.randint(jax.random.fold_in(_rk, 12), (16, 1601), 0, 512, jnp.int32)
        _validS = jnp.arange(64)[None, :] < _lenS[:, None]
        _validS2 = jnp.arange(1601)[None, :] < _lenS2[:, None]
        _causal = jnp.tril(jnp.ones((64, 64), dtype=bool))
        mask_SxS2_ik0 = jnp.where(jnp.broadcast_to(_validS2[0:1, :], (64, 1601)), 0, 1).astype(jnp.int32)
        return (x, ctx_1024, itok_BxS2_0_2047, mask_SxS2_ik0)
    x, ctx_1024, itok_BxS2_0_2047, mask_SxS2_ik0 = _rec_inputs()

    def _L0_xattn_setup():
        import jax, jax.numpy as jnp
        import numpy as np
        import math
        EMBED_DIM = 256
        NUM_HEADS = 16
        HEAD_DIM = EMBED_DIM // NUM_HEADS
        SUB_HEAD_DIM = HEAD_DIM // 2
        SCALING = 1.0 / math.sqrt(SUB_HEAD_DIM)
        LAMBDA_INIT = 0.8 - 0.6 * math.exp(-0.3 * 0)
        key = jax.random.key(seed)
        ks = jax.random.split(key, 10)
        B, T, D = (2, 512, EMBED_DIM)
        xav = math.sqrt(6.0 / (D + D))
        return {'query': jax.random.normal(ks[0], (B, T, D), jnp.float32), 'key': jax.random.normal(ks[1], (B, T, D), jnp.float32), 'value': jax.random.normal(ks[2], (B, T, D), jnp.float32), 'in_proj_weight': jax.random.uniform(ks[3], (3 * D, D), jnp.float32, -xav, xav), 'in_proj_bias': jnp.zeros((3 * D,), jnp.float32), 'out_proj_weight': jax.random.uniform(ks[4], (D, D), jnp.float32, -xav, xav), 'out_proj_bias': jnp.zeros((D,), jnp.float32), 'lambda_q1': 0.1 * jax.random.normal(ks[5], (SUB_HEAD_DIM,), jnp.float32), 'lambda_k1': 0.1 * jax.random.normal(ks[6], (SUB_HEAD_DIM,), jnp.float32), 'lambda_q2': 0.1 * jax.random.normal(ks[7], (SUB_HEAD_DIM,), jnp.float32), 'lambda_k2': 0.1 * jax.random.normal(ks[8], (SUB_HEAD_DIM,), jnp.float32)}
    _L0_xattn_all = _L0_xattn_setup()
    _L0_xattn_in = {k: v for k, v in _L0_xattn_all.items() if k in ('in_proj_weight', 'in_proj_bias', 'out_proj_weight', 'out_proj_bias', 'lambda_q1', 'lambda_k1', 'lambda_q2', 'lambda_k2')}
    del _L0_xattn_all

    def _L0_attn_setup():
        import jax, jax.numpy as jnp
        import numpy as np
        HEADS = 16
        DIM_HEAD = 64
        SEG = 32
        SCALE = DIM_HEAD ** (-0.5)
        INNER = HEADS * DIM_HEAD

        def elu1(x):
            return jax.nn.elu(x) + 1.0

        def rope(t, pos):
            d = t.shape[-1]
            freqs = 10000.0 ** (-jnp.arange(0, d, 2, dtype=jnp.float32) / d)
            ang = pos[:, None] * freqs
            cos = jnp.repeat(jnp.cos(ang), 2, axis=-1)
            sin = jnp.repeat(jnp.sin(ang), 2, axis=-1)
            t2 = t.reshape(t.shape[:-1] + (d // 2, 2))
            rot = jnp.stack((-t2[..., 1], t2[..., 0]), axis=-1).reshape(t.shape)
            return t * cos + rot * sin

        def _reference_tuple_inner(x, w_qkv, w_out, ln_g, ln_b, mem_beta):
            B, N, D = x.shape
            mu = x.mean(-1, keepdims=True)
            var = x.var(-1, keepdims=True)
            xn = (x - mu) / jnp.sqrt(var + 1e-05) * ln_g + ln_b
            qkv = xn @ w_qkv
            q, k, v = jnp.split(qkv, 3, axis=-1)

            def to_heads(t):
                return t.reshape(B, N, HEADS, DIM_HEAD).transpose(0, 2, 1, 3)
            q, k, v = map(to_heads, (q, k, v))
            next_k, next_v = (k, v)
            pos = jnp.arange(N, dtype=jnp.float32)
            qr, kr = (rope(q, pos), rope(k, pos))
            W = N // SEG

            def to_segs(t):
                return t.reshape(B, HEADS, W, SEG, DIM_HEAD).transpose(2, 0, 1, 3, 4)
            qs, ks, vs, qnope, knope = map(to_segs, (qr, kr, v, q, k))
            mask = jnp.tril(jnp.ones((SEG, SEG), bool))
            beta = jax.nn.sigmoid(mem_beta)
            mem0 = jnp.zeros((B, HEADS, DIM_HEAD, DIM_HEAD), x.dtype)
            z0 = jnp.full((B, HEADS, DIM_HEAD), 1e-06, x.dtype)

            def step(carry, inp):
                mem, z = carry
                q_s, k_s, v_s, qn_s, kn_s = inp
                scores = jnp.einsum('bhnd,bhmd->bhnm', q_s, k_s) * SCALE
                scores = jnp.where(mask, scores, -jnp.inf)
                sdpa = jnp.einsum('bhnm,bhmd->bhnd', jax.nn.softmax(scores, axis=-1), v_s)
                sq = elu1(qn_s)
                num = jnp.einsum('bhnk,bhkv->bhnv', sq, mem)
                den = jnp.einsum('bhnk,bhk->bhn', sq, z)[..., None]
                mem_out = num / (den + 1e-06)
                out = beta * mem_out + (1.0 - beta) * sdpa
                sk = elu1(kn_s)
                prev_v = jnp.einsum('bhnk,bhkv->bhnv', sk, mem) / jnp.einsum('bhnk,bhk->bhn', sk, z)[..., None]
                mem = mem + jnp.einsum('bhnk,bhnv->bhkv', sk, v_s - prev_v)
                z = z + sk.sum(axis=2)
                return ((mem, z), out)
            _, outs = jax.lax.scan(step, (mem0, z0), (qs, ks, vs, qnope, knope))
            o = outs.transpose(1, 0, 3, 2, 4).reshape(B, N, INNER)
            out = o @ w_out
            return (out, next_k, next_v)
        key = jax.random.key(seed)
        k1, k2, k3 = jax.random.split(key, 3)
        B, N, D = (4, 1024, 256)
        x = jax.random.normal(k1, (B, N, D), dtype=jnp.float32)
        w_qkv = jax.random.normal(k2, (D, 3 * INNER), dtype=jnp.float32) * 0.02
        w_out = jax.random.normal(k3, (INNER, D), dtype=jnp.float32) * 0.02
        ln_g = jnp.ones((D,), jnp.float32)
        ln_b = jnp.zeros((D,), jnp.float32)
        mem_beta = jnp.zeros((1, HEADS, 1, 1), jnp.float32)
        return {'x': x, 'w_qkv': w_qkv, 'w_out': w_out, 'ln_g': ln_g, 'ln_b': ln_b, 'mem_beta': mem_beta}
    _L0_attn_all = _L0_attn_setup()
    _L0_attn_in = {k: v for k, v in _L0_attn_all.items() if k in ('w_qkv', 'w_out', 'ln_g', 'ln_b', 'mem_beta')}
    del _L0_attn_all

    def _L0_ffn_setup():
        import jax, jax.numpy as jnp
        import numpy as np
        H = 256
        M = 128
        E = 16
        TOP_K = 4
        N_GROUP = 4
        TOPK_GROUP = 2
        SCALE = 2.5
        B, S = (2, 256)

        def _gate(x2d, gate_kernel, gate_bias):
            n = x2d.shape[0]
            logits = jnp.dot(x2d.astype(jnp.float32), gate_kernel.astype(jnp.float32))
            scores = jax.nn.sigmoid(logits)
            scores_for_choice = scores + gate_bias
            group_scores = scores_for_choice.reshape(n, N_GROUP, E // N_GROUP)
            top2 = jax.lax.top_k(group_scores, k=2)[0]
            group_sum = jnp.sum(top2, axis=-1)
            group_idx = jax.lax.top_k(group_sum, k=TOPK_GROUP)[1]
            group_mask = jnp.zeros_like(group_sum).at[jnp.arange(n)[:, None], group_idx].set(1.0)
            score_mask = jnp.repeat(group_mask[:, :, None], E // N_GROUP, axis=2).reshape(n, E)
            masked_scores = jnp.where(score_mask > 0, scores_for_choice, 0.0)
            topk_weight, topk_idx = jax.lax.top_k(masked_scores, k=TOP_K)
            topk_weight = topk_weight / (jnp.sum(topk_weight, axis=-1, keepdims=True) + 1e-20)
            topk_weight = topk_weight * SCALE
            return (topk_idx, topk_weight)
        key = jax.random.key(seed)
        ks = jax.random.split(key, 9)
        sc_h = 1.0 / np.sqrt(H)
        sc_m = 1.0 / np.sqrt(M)
        return {'hidden_states': jax.random.normal(ks[0], (B, S, H), jnp.float32), 'gate_kernel': jax.random.normal(ks[1], (H, E), jnp.float32) * sc_h, 'gate_bias': jax.random.normal(ks[2], (E,), jnp.float32) * 0.01, 'w_gate': jax.random.normal(ks[3], (E, H, M), jnp.float32) * sc_h, 'w_up': jax.random.normal(ks[4], (E, H, M), jnp.float32) * sc_h, 'w_down': jax.random.normal(ks[5], (E, M, H), jnp.float32) * sc_m, 'sw_gate': jax.random.normal(ks[6], (H, 2 * M), jnp.float32) * sc_h, 'sw_up': jax.random.normal(ks[7], (H, 2 * M), jnp.float32) * sc_h, 'sw_down': jax.random.normal(ks[8], (2 * M, H), jnp.float32) * (1.0 / np.sqrt(2 * M))}
    _L0_ffn_all = _L0_ffn_setup()
    _L0_ffn_in = {k: v for k, v in _L0_ffn_all.items() if k in ('gate_kernel', 'gate_bias', 'w_gate', 'w_up', 'w_down', 'sw_gate', 'sw_up', 'sw_down')}
    del _L0_ffn_all

    def _L1_xattn_setup():
        import jax, jax.numpy as jnp
        import numpy as np
        DIM = 256
        HEADS = 16
        HEAD_DIM = DIM // HEADS
        SCALE = HEAD_DIM ** (-0.5)
        key = jax.random.key(seed)
        ks = jax.random.split(key, 13)
        B, Nq, Nk = (4, 512, 512)
        s = DIM ** (-0.5)
        return {'query': jax.random.normal(ks[0], (B, Nq, DIM), jnp.float32), 'key': jax.random.normal(ks[1], (B, Nk, DIM), jnp.float32), 'value': jax.random.normal(ks[2], (B, Nk, DIM), jnp.float32), 'qpos': jax.random.randint(ks[3], (B, Nq), 0, Nq), 'kpos': jax.random.randint(ks[4], (B, Nk), 0, Nk), 'Wq': jax.random.normal(ks[5], (DIM, DIM), jnp.float32) * s, 'bq': jnp.zeros((DIM,), jnp.float32), 'Wk': jax.random.normal(ks[6], (DIM, DIM), jnp.float32) * s, 'bk': jnp.zeros((DIM,), jnp.float32), 'Wv': jax.random.normal(ks[7], (DIM, DIM), jnp.float32) * s, 'bv': jnp.zeros((DIM,), jnp.float32), 'Wo': jax.random.normal(ks[8], (DIM, DIM), jnp.float32) * s, 'bo': jnp.zeros((DIM,), jnp.float32)}
    _L1_xattn_all = _L1_xattn_setup()
    _L1_xattn_in = {k: v for k, v in _L1_xattn_all.items() if k in ('Wq', 'bq', 'Wk', 'bk', 'Wv', 'bv', 'Wo', 'bo')}
    del _L1_xattn_all

    def _L1_attn_setup():
        import jax, jax.numpy as jnp
        import numpy as np
        import math
        B, S, D = (4, 512, 256)
        H = 16
        HD = D // H
        DL = 64
        LAMBDA_DECAY = 0.01
        key = jax.random.key(seed)
        ks = jax.random.split(key, 8)
        sc = lambda fan_in: 1.0 / math.sqrt(fan_in)
        return {'x': jax.random.normal(ks[0], (B, S, D), dtype=jnp.float32), 'W_q': jax.random.normal(ks[1], (D, D), dtype=jnp.float32) * sc(D), 'W_k': jax.random.normal(ks[2], (D, D), dtype=jnp.float32) * sc(D), 'W_v': jax.random.normal(ks[3], (D, D), dtype=jnp.float32) * sc(D), 'W_o': jax.random.normal(ks[4], (D, D), dtype=jnp.float32) * sc(D), 'W_down_kv': jax.random.normal(ks[5], (D, DL), dtype=jnp.float32) * sc(D), 'W_up_k': jax.random.normal(ks[6], (DL, D), dtype=jnp.float32) * sc(DL), 'W_up_v': jax.random.normal(ks[7], (DL, D), dtype=jnp.float32) * sc(DL)}
    _L1_attn_all = _L1_attn_setup()
    _L1_attn_in = {k: v for k, v in _L1_attn_all.items() if k in ('W_q', 'W_k', 'W_v', 'W_o', 'W_down_kv', 'W_up_k', 'W_up_v')}
    del _L1_attn_all

    def _L1_ffn_setup():
        import jax, jax.numpy as jnp
        import numpy as np
        B, S, D_MODEL, D_HIDDEN = (4, 512, 256, 1024)

        def act_quant(x):
            scale = 127.0 / jnp.clip(jnp.max(jnp.abs(x), axis=-1, keepdims=True), 1e-05)
            return jnp.clip(jnp.round(x * scale), -128, 127) / scale

        def weight_quant(w):
            scale = 1.0 / jnp.clip(jnp.mean(jnp.abs(w)), 1e-05)
            return jnp.clip(jnp.round(w * scale), -1, 1) / scale

        def bit_linear(x, w):
            xq = x + jax.lax.stop_gradient(act_quant(x) - x)
            wq = w + jax.lax.stop_gradient(weight_quant(w) - w)
            return jnp.einsum('bsd,hd->bsh', xq, wq)

        def depthwise_conv1d(x_bcl, w, b):
            y = jax.lax.conv_general_dilated(x_bcl, w, window_strides=(1,), padding=[(1, 1)], dimension_numbers=('NCH', 'OIH', 'NCH'), feature_group_count=x_bcl.shape[1])
            return y + b[None, :, None]
        key = jax.random.key(seed)
        ks = jax.random.split(key, 5)
        lim1 = 1.0 / np.sqrt(D_MODEL)
        lim2 = 1.0 / np.sqrt(D_HIDDEN)
        limc = 1.0 / np.sqrt(3.0)
        return {'x': jax.random.normal(ks[0], (B, S, D_MODEL), dtype=jnp.float32), 'w1': jax.random.uniform(ks[1], (D_HIDDEN, D_MODEL), jnp.float32, -lim1, lim1), 'conv_w': jax.random.uniform(ks[2], (D_HIDDEN, 1, 3), jnp.float32, -limc, limc), 'conv_b': jax.random.uniform(ks[3], (D_HIDDEN,), jnp.float32, -limc, limc), 'w2': jax.random.uniform(ks[4], (D_MODEL, D_HIDDEN), jnp.float32, -lim2, lim2)}
    _L1_ffn_all = _L1_ffn_setup()
    _L1_ffn_in = {k: v for k, v in _L1_ffn_all.items() if k in ('w1', 'conv_w', 'conv_b', 'w2')}
    del _L1_ffn_all

    def _L2_xattn_setup():
        import jax, jax.numpy as jnp
        import numpy as np
        D_MODEL = 256
        N_HEADS = 16
        D_K = D_MODEL // N_HEADS
        B, L = (4, 512)
        key = jax.random.key(seed)
        ks = jax.random.split(key, 12)
        s_in = 1.0 / np.sqrt(D_MODEL)
        inp = {'Q': jax.random.normal(ks[0], (B, L, D_MODEL), jnp.float32), 'K': jax.random.normal(ks[1], (B, L, D_MODEL), jnp.float32), 'V': jax.random.normal(ks[2], (B, L, D_MODEL), jnp.float32), 'attn_mask': jnp.tril(jnp.ones((L, L), jnp.int32)), 'Wq': jax.random.normal(ks[3], (D_MODEL, D_MODEL), jnp.float32) * s_in, 'bq': jnp.zeros((D_MODEL,), jnp.float32), 'Wk': jax.random.normal(ks[4], (D_MODEL, D_MODEL), jnp.float32) * s_in, 'bk': jnp.zeros((D_MODEL,), jnp.float32), 'Wv': jax.random.normal(ks[5], (D_MODEL, D_MODEL), jnp.float32) * s_in, 'bv': jnp.zeros((D_MODEL,), jnp.float32), 'Wo': jax.random.normal(ks[6], (D_MODEL, D_MODEL), jnp.float32) * s_in, 'bo': jnp.zeros((D_MODEL,), jnp.float32)}
        return inp
    _L2_xattn_all = _L2_xattn_setup()
    _L2_xattn_in = {k: v for k, v in _L2_xattn_all.items() if k in ('Wq', 'bq', 'Wk', 'bk', 'Wv', 'bv', 'Wo', 'bo')}
    del _L2_xattn_all

    def _L2_attn_setup():
        import jax, jax.numpy as jnp
        import numpy as np
        B, L, D = (16, 512, 256)
        LN_EPS = 1e-05
        key = jax.random.key(seed)
        ks = jax.random.split(key, 4)
        x = jax.random.normal(ks[0], (B, L, D), dtype=jnp.float32)
        gamma = jnp.ones((D,), jnp.float32)
        beta = jnp.zeros((D,), jnp.float32)
        A = jax.random.normal(ks[1], (D,), dtype=jnp.float32) * 0.1
        W_in = jax.random.normal(ks[2], (D, 2 * D), dtype=jnp.float32) * (1.0 / np.sqrt(D))
        b_in = jnp.zeros((2 * D,), jnp.float32)
        W_out = jax.random.normal(ks[3], (D, D), dtype=jnp.float32) * (1.0 / np.sqrt(D))
        b_out = jnp.zeros((D,), jnp.float32)
        return {'x': x, 'gamma': gamma, 'beta': beta, 'A': A, 'W_in': W_in, 'b_in': b_in, 'W_out': W_out, 'b_out': b_out}
    _L2_attn_all = _L2_attn_setup()
    _L2_attn_in = {k: v for k, v in _L2_attn_all.items() if k in ('gamma', 'beta', 'A', 'W_in', 'b_in', 'W_out', 'b_out')}
    del _L2_attn_all

    def _L2_ffn_setup():
        import jax, jax.numpy as jnp
        import numpy as np
        TOP_K = 2
        key = jax.random.key(seed)
        ks = jax.random.split(key, 5)
        B, N, C, FF, E = (2, 512, 256, 1024, 8)
        x = jax.random.normal(ks[0], (B, N, C), dtype=jnp.float32)
        router_w = jax.random.normal(ks[1], (E, C), dtype=jnp.float32) * 0.02
        lim1 = np.sqrt(6.0 / (FF + C))
        expert_w1 = jax.random.uniform(ks[2], (E, FF, C), dtype=jnp.float32, minval=-lim1, maxval=lim1)
        expert_b1 = jnp.zeros((E, FF), dtype=jnp.float32)
        expert_w2 = jax.random.uniform(ks[3], (E, C, FF), dtype=jnp.float32, minval=-lim1, maxval=lim1)
        expert_b2 = jnp.zeros((E, C), dtype=jnp.float32)
        return {'x': x, 'router_w': router_w, 'expert_w1': expert_w1, 'expert_b1': expert_b1, 'expert_w2': expert_w2, 'expert_b2': expert_b2}
    _L2_ffn_all = _L2_ffn_setup()
    _L2_ffn_in = {k: v for k, v in _L2_ffn_all.items() if k in ('router_w', 'expert_w1', 'expert_b1', 'expert_w2', 'expert_b2')}
    del _L2_ffn_all

    def _L3_xattn_setup():
        import jax, jax.numpy as jnp
        import numpy as np
        DIM = 256
        NUM_HEADS = 16
        HEAD_DIM = DIM // NUM_HEADS
        key = jax.random.key(seed)
        ks = jax.random.split(key, 11)
        B, N, C = (2, 512, DIM)
        s = 1.0 / np.sqrt(C)
        inp = {'q': jax.random.normal(ks[0], (B, N, C), jnp.float32), 'k': jax.random.normal(ks[1], (B, N, C), jnp.float32), 'v': jax.random.normal(ks[2], (B, N, C), jnp.float32), 'Wq': jax.random.normal(ks[3], (C, C), jnp.float32) * s, 'bq': jnp.zeros((C,), jnp.float32), 'Wk': jax.random.normal(ks[4], (C, C), jnp.float32) * s, 'bk': jnp.zeros((C,), jnp.float32), 'Wv': jax.random.normal(ks[5], (C, C), jnp.float32) * s, 'bv': jnp.zeros((C,), jnp.float32), 'Wo': jax.random.normal(ks[6], (C, C), jnp.float32) * s, 'bo': jnp.zeros((C,), jnp.float32)}
        return inp
    _L3_xattn_all = _L3_xattn_setup()
    _L3_xattn_in = {k: v for k, v in _L3_xattn_all.items() if k in ('Wq', 'bq', 'Wk', 'bk', 'Wv', 'bv', 'Wo', 'bo')}
    del _L3_xattn_all

    def _L3_attn_setup():
        import jax, jax.numpy as jnp
        import numpy as np
        D_MODEL = 256
        D_STATE = 16
        D_CONV = 4
        EXPAND = 2
        D_INNER = EXPAND * D_MODEL
        DT_RANK = (D_MODEL + 15) // 16
        BATCH = 2
        SEQLEN = 512

        def _mefi_forward(x, W_in, conv_w, conv_b, W_x, W_dt, b_dt, A_log, Dp, W_out1, W_out2):
            B, L, _ = x.shape
            xz = jnp.einsum('bld,ed->bel', x, W_in)
            xi, z = (xz[:, :D_INNER, :], xz[:, D_INNER:, :])
            xc = jax.lax.conv_general_dilated(xi, conv_w[:, None, :], window_strides=(1,), padding=[(D_CONV - 1, 0)], dimension_numbers=('NCH', 'OIH', 'NCH'), feature_group_count=D_INNER)
            u = jax.nn.silu(xc + conv_b[None, :, None])
            x_dbl = jnp.einsum('bdl,ed->ble', u, W_x)
            dt_r = x_dbl[..., :DT_RANK]
            Bm = x_dbl[..., DT_RANK:DT_RANK + D_STATE].transpose(0, 2, 1)
            Cm = x_dbl[..., DT_RANK + D_STATE:].transpose(0, 2, 1)
            dt = jnp.einsum('blr,dr->bdl', dt_r, W_dt)
            A = -jnp.exp(A_log)
            delta = jax.nn.softplus(dt + b_dt[None, :, None])

            def step(s, inp):
                d_t, u_t, B_t, C_t = inp
                dA = jnp.exp(d_t[:, :, None] * A[None, :, :])
                s = dA * s + (d_t * u_t)[:, :, None] * B_t[:, None, :]
                y_t = jnp.einsum('bdn,bn->bd', s, C_t)
                return (s, y_t)
            s0 = jnp.zeros((B, D_INNER, D_STATE), delta.dtype)
            xs = (delta.transpose(2, 0, 1), u.transpose(2, 0, 1), Bm.transpose(2, 0, 1), Cm.transpose(2, 0, 1))
            _, ys = jax.lax.scan(step, s0, xs)
            y = ys.transpose(1, 2, 0)
            y = (y + Dp[None, :, None] * u) * jax.nn.silu(z)
            y_t = jnp.einsum('bnl,dn->bld', Cm, A) + jnp.einsum('d,bdl->bl', Dp, u)[..., None]
            y_cat = jnp.concatenate([y.transpose(0, 2, 1), y_t], axis=-1)
            h = jnp.maximum(y_cat @ W_out1.T, 0.0)
            return h @ W_out2.T
        key = jax.random.key(seed)
        ks = jax.random.split(key, 10)

        def rn(k, shape, scale=0.02):
            return (jax.random.normal(k, shape, jnp.float32) * scale).astype(jnp.float32)
        x = jax.random.normal(ks[0], (BATCH, SEQLEN, D_MODEL), jnp.float32)
        W_in = rn(ks[1], (2 * D_INNER, D_MODEL))
        conv_w = rn(ks[2], (D_INNER, D_CONV), 0.1)
        conv_b = jnp.zeros((D_INNER,), jnp.float32)
        W_x = rn(ks[3], (DT_RANK + 2 * D_STATE, D_INNER))
        dt_std = DT_RANK ** (-0.5)
        W_dt = jax.random.uniform(ks[4], (D_INNER, DT_RANK), jnp.float32, -dt_std, dt_std)
        dt = jnp.exp(jax.random.uniform(ks[5], (D_INNER,), jnp.float32) * (np.log(0.1) - np.log(0.001)) + np.log(0.001))
        dt = jnp.clip(dt, 0.0001, None)
        b_dt = dt + jnp.log(-jnp.expm1(-dt))
        A_log = jnp.log(jnp.tile(jnp.arange(1, D_STATE + 1, dtype=jnp.float32)[None, :], (D_INNER, 1)))
        Dp = jnp.ones((D_INNER,), jnp.float32)
        W_out1 = rn(ks[6], (D_INNER, 2 * D_INNER))
        W_out2 = rn(ks[7], (D_MODEL, D_INNER))
        return {'x': x, 'W_in': W_in, 'conv_w': conv_w, 'conv_b': conv_b, 'W_x': W_x, 'W_dt': W_dt, 'b_dt': b_dt, 'A_log': A_log, 'Dp': Dp, 'W_out1': W_out1, 'W_out2': W_out2}
    _L3_attn_all = _L3_attn_setup()
    _L3_attn_in = {k: v for k, v in _L3_attn_all.items() if k in ('W_in', 'conv_w', 'conv_b', 'W_x', 'W_dt', 'b_dt', 'A_log', 'Dp', 'W_out1', 'W_out2')}
    del _L3_attn_all

    def _L3_ffn_setup():
        import jax, jax.numpy as jnp
        import numpy as np
        E = 8
        K = 2
        key = jax.random.key(seed)
        ks = jax.random.split(key, 6)
        B, S, D, F = (4, 512, 256, 1024)
        s_d = 1.0 / np.sqrt(D).astype(np.float32)
        s_f = 1.0 / np.sqrt(F).astype(np.float32)
        return {'x': jax.random.normal(ks[0], (B, S, D), jnp.float32), 'ln_w': jnp.ones((D,), jnp.float32), 'Wg': jax.random.normal(ks[1], (D, E), jnp.float32) * s_d, 'bg': jnp.zeros((E,), jnp.float32), 'W1a': jax.random.normal(ks[2], (E, D, F), jnp.float32) * s_d, 'b1a': jnp.zeros((E, F), jnp.float32), 'W1b': jax.random.normal(ks[3], (E, D, F), jnp.float32) * s_d, 'b1b': jnp.zeros((E, F), jnp.float32), 'W2': jax.random.normal(ks[4], (E, F, D), jnp.float32) * s_f, 'b2': jnp.zeros((E, D), jnp.float32)}
    _L3_ffn_all = _L3_ffn_setup()
    _L3_ffn_in = {k: v for k, v in _L3_ffn_all.items() if k in ('ln_w', 'Wg', 'bg', 'W1a', 'b1a', 'W1b', 'b1b', 'W2', 'b2')}
    del _L3_ffn_all
    return {'x': x, 'ctx_1024': ctx_1024, 'itok_BxS2_0_2047': itok_BxS2_0_2047, 'mask_SxS2_ik0': mask_SxS2_ik0, 'L0_xattn_in_proj_weight': _L0_xattn_in['in_proj_weight'], 'L0_xattn_in_proj_bias': _L0_xattn_in['in_proj_bias'], 'L0_xattn_out_proj_weight': _L0_xattn_in['out_proj_weight'], 'L0_xattn_out_proj_bias': _L0_xattn_in['out_proj_bias'], 'L0_xattn_lambda_q1': _L0_xattn_in['lambda_q1'], 'L0_xattn_lambda_k1': _L0_xattn_in['lambda_k1'], 'L0_xattn_lambda_q2': _L0_xattn_in['lambda_q2'], 'L0_xattn_lambda_k2': _L0_xattn_in['lambda_k2'], 'L0_attn_w_qkv': _L0_attn_in['w_qkv'], 'L0_attn_w_out': _L0_attn_in['w_out'], 'L0_attn_ln_g': _L0_attn_in['ln_g'], 'L0_attn_ln_b': _L0_attn_in['ln_b'], 'L0_attn_mem_beta': _L0_attn_in['mem_beta'], 'L0_ffn_gate_kernel': _L0_ffn_in['gate_kernel'], 'L0_ffn_gate_bias': _L0_ffn_in['gate_bias'], 'L0_ffn_w_gate': _L0_ffn_in['w_gate'], 'L0_ffn_w_up': _L0_ffn_in['w_up'], 'L0_ffn_w_down': _L0_ffn_in['w_down'], 'L0_ffn_sw_gate': _L0_ffn_in['sw_gate'], 'L0_ffn_sw_up': _L0_ffn_in['sw_up'], 'L0_ffn_sw_down': _L0_ffn_in['sw_down'], 'L1_xattn_Wq': _L1_xattn_in['Wq'], 'L1_xattn_bq': _L1_xattn_in['bq'], 'L1_xattn_Wk': _L1_xattn_in['Wk'], 'L1_xattn_bk': _L1_xattn_in['bk'], 'L1_xattn_Wv': _L1_xattn_in['Wv'], 'L1_xattn_bv': _L1_xattn_in['bv'], 'L1_xattn_Wo': _L1_xattn_in['Wo'], 'L1_xattn_bo': _L1_xattn_in['bo'], 'L1_attn_W_q': _L1_attn_in['W_q'], 'L1_attn_W_k': _L1_attn_in['W_k'], 'L1_attn_W_v': _L1_attn_in['W_v'], 'L1_attn_W_o': _L1_attn_in['W_o'], 'L1_attn_W_down_kv': _L1_attn_in['W_down_kv'], 'L1_attn_W_up_k': _L1_attn_in['W_up_k'], 'L1_attn_W_up_v': _L1_attn_in['W_up_v'], 'L1_ffn_w1': _L1_ffn_in['w1'], 'L1_ffn_conv_w': _L1_ffn_in['conv_w'], 'L1_ffn_conv_b': _L1_ffn_in['conv_b'], 'L1_ffn_w2': _L1_ffn_in['w2'], 'L2_xattn_Wq': _L2_xattn_in['Wq'], 'L2_xattn_bq': _L2_xattn_in['bq'], 'L2_xattn_Wk': _L2_xattn_in['Wk'], 'L2_xattn_bk': _L2_xattn_in['bk'], 'L2_xattn_Wv': _L2_xattn_in['Wv'], 'L2_xattn_bv': _L2_xattn_in['bv'], 'L2_xattn_Wo': _L2_xattn_in['Wo'], 'L2_xattn_bo': _L2_xattn_in['bo'], 'L2_attn_gamma': _L2_attn_in['gamma'], 'L2_attn_beta': _L2_attn_in['beta'], 'L2_attn_A': _L2_attn_in['A'], 'L2_attn_W_in': _L2_attn_in['W_in'], 'L2_attn_b_in': _L2_attn_in['b_in'], 'L2_attn_W_out': _L2_attn_in['W_out'], 'L2_attn_b_out': _L2_attn_in['b_out'], 'L2_ffn_router_w': _L2_ffn_in['router_w'], 'L2_ffn_expert_w1': _L2_ffn_in['expert_w1'], 'L2_ffn_expert_b1': _L2_ffn_in['expert_b1'], 'L2_ffn_expert_w2': _L2_ffn_in['expert_w2'], 'L2_ffn_expert_b2': _L2_ffn_in['expert_b2'], 'L3_xattn_Wq': _L3_xattn_in['Wq'], 'L3_xattn_bq': _L3_xattn_in['bq'], 'L3_xattn_Wk': _L3_xattn_in['Wk'], 'L3_xattn_bk': _L3_xattn_in['bk'], 'L3_xattn_Wv': _L3_xattn_in['Wv'], 'L3_xattn_bv': _L3_xattn_in['bv'], 'L3_xattn_Wo': _L3_xattn_in['Wo'], 'L3_xattn_bo': _L3_xattn_in['bo'], 'L3_attn_W_in': _L3_attn_in['W_in'], 'L3_attn_conv_w': _L3_attn_in['conv_w'], 'L3_attn_conv_b': _L3_attn_in['conv_b'], 'L3_attn_W_x': _L3_attn_in['W_x'], 'L3_attn_W_dt': _L3_attn_in['W_dt'], 'L3_attn_b_dt': _L3_attn_in['b_dt'], 'L3_attn_A_log': _L3_attn_in['A_log'], 'L3_attn_Dp': _L3_attn_in['Dp'], 'L3_attn_W_out1': _L3_attn_in['W_out1'], 'L3_attn_W_out2': _L3_attn_in['W_out2'], 'L3_ffn_ln_w': _L3_ffn_in['ln_w'], 'L3_ffn_Wg': _L3_ffn_in['Wg'], 'L3_ffn_bg': _L3_ffn_in['bg'], 'L3_ffn_W1a': _L3_ffn_in['W1a'], 'L3_ffn_b1a': _L3_ffn_in['b1a'], 'L3_ffn_W1b': _L3_ffn_in['W1b'], 'L3_ffn_b1b': _L3_ffn_in['b1b'], 'L3_ffn_W2': _L3_ffn_in['W2'], 'L3_ffn_b2': _L3_ffn_in['b2']}

def reference(x, ctx_1024, itok_BxS2_0_2047, mask_SxS2_ik0, L0_xattn_in_proj_weight, L0_xattn_in_proj_bias, L0_xattn_out_proj_weight, L0_xattn_out_proj_bias, L0_xattn_lambda_q1, L0_xattn_lambda_k1, L0_xattn_lambda_q2, L0_xattn_lambda_k2, L0_attn_w_qkv, L0_attn_w_out, L0_attn_ln_g, L0_attn_ln_b, L0_attn_mem_beta, L0_ffn_gate_kernel, L0_ffn_gate_bias, L0_ffn_w_gate, L0_ffn_w_up, L0_ffn_w_down, L0_ffn_sw_gate, L0_ffn_sw_up, L0_ffn_sw_down, L1_xattn_Wq, L1_xattn_bq, L1_xattn_Wk, L1_xattn_bk, L1_xattn_Wv, L1_xattn_bv, L1_xattn_Wo, L1_xattn_bo, L1_attn_W_q, L1_attn_W_k, L1_attn_W_v, L1_attn_W_o, L1_attn_W_down_kv, L1_attn_W_up_k, L1_attn_W_up_v, L1_ffn_w1, L1_ffn_conv_w, L1_ffn_conv_b, L1_ffn_w2, L2_xattn_Wq, L2_xattn_bq, L2_xattn_Wk, L2_xattn_bk, L2_xattn_Wv, L2_xattn_bv, L2_xattn_Wo, L2_xattn_bo, L2_attn_gamma, L2_attn_beta, L2_attn_A, L2_attn_W_in, L2_attn_b_in, L2_attn_W_out, L2_attn_b_out, L2_ffn_router_w, L2_ffn_expert_w1, L2_ffn_expert_b1, L2_ffn_expert_w2, L2_ffn_expert_b2, L3_xattn_Wq, L3_xattn_bq, L3_xattn_Wk, L3_xattn_bk, L3_xattn_Wv, L3_xattn_bv, L3_xattn_Wo, L3_xattn_bo, L3_attn_W_in, L3_attn_conv_w, L3_attn_conv_b, L3_attn_W_x, L3_attn_W_dt, L3_attn_b_dt, L3_attn_A_log, L3_attn_Dp, L3_attn_W_out1, L3_attn_W_out2, L3_ffn_ln_w, L3_ffn_Wg, L3_ffn_bg, L3_ffn_W1a, L3_ffn_b1a, L3_ffn_W1b, L3_ffn_b1b, L3_ffn_W2, L3_ffn_b2):
    import jax
    import jax.numpy as jnp

    def _L0_xattn_ref(query, key, value, in_proj_weight, in_proj_bias, out_proj_weight, out_proj_bias, lambda_q1, lambda_k1, lambda_q2, lambda_k2):
        import jax, jax.numpy as jnp
        import numpy as np
        import math
        EMBED_DIM = 256
        NUM_HEADS = 16
        HEAD_DIM = EMBED_DIM // NUM_HEADS
        SUB_HEAD_DIM = HEAD_DIM // 2
        SCALING = 1.0 / math.sqrt(SUB_HEAD_DIM)
        LAMBDA_INIT = 0.8 - 0.6 * math.exp(-0.3 * 0)
        B, T, D = query.shape
        S = key.shape[1]
        H, hd, sd = (NUM_HEADS, HEAD_DIM, SUB_HEAD_DIM)
        qw, kw, vw = jnp.split(in_proj_weight, 3, axis=0)
        qb, kb, vb = jnp.split(in_proj_bias, 3, axis=0)
        q = query @ qw.T + qb
        k = key @ kw.T + kb
        v = value @ vw.T + vb
        q = q.reshape(B, T, H, hd).transpose(0, 2, 1, 3)
        k = k.reshape(B, S, H, hd).transpose(0, 2, 1, 3)
        v = v.reshape(B, S, H, hd).transpose(0, 2, 1, 3)
        q1, q2 = (q[..., :sd], q[..., sd:])
        k1, k2 = (k[..., :sd], k[..., sd:])
        logits_1 = jnp.einsum('bhtd,bhsd->bhts', q1, k1) * SCALING
        logits_2 = jnp.einsum('bhtd,bhsd->bhts', q2, k2) * SCALING
        a1 = jax.nn.softmax(logits_1, axis=-1)
        a2 = jax.nn.softmax(logits_2, axis=-1)
        lam = jnp.exp(jnp.dot(lambda_q1, lambda_k1)) - jnp.exp(jnp.dot(lambda_q2, lambda_k2)) + LAMBDA_INIT
        diff_weights = a1 - lam * a2
        attn_output = jnp.einsum('bhts,bhsd->bhtd', diff_weights, v)
        attn_output = attn_output * (1.0 - LAMBDA_INIT)
        attn_output = attn_output.transpose(0, 2, 1, 3).reshape(B, T, D)
        output = attn_output @ out_proj_weight.T + out_proj_bias
        return output

    def _L0_attn_ref(x, w_qkv, w_out, ln_g, ln_b, mem_beta):
        import jax, jax.numpy as jnp
        import numpy as np
        HEADS = 16
        DIM_HEAD = 64
        SEG = 32
        SCALE = DIM_HEAD ** (-0.5)
        INNER = HEADS * DIM_HEAD

        def elu1(x):
            return jax.nn.elu(x) + 1.0

        def rope(t, pos):
            d = t.shape[-1]
            freqs = 10000.0 ** (-jnp.arange(0, d, 2, dtype=jnp.float32) / d)
            ang = pos[:, None] * freqs
            cos = jnp.repeat(jnp.cos(ang), 2, axis=-1)
            sin = jnp.repeat(jnp.sin(ang), 2, axis=-1)
            t2 = t.reshape(t.shape[:-1] + (d // 2, 2))
            rot = jnp.stack((-t2[..., 1], t2[..., 0]), axis=-1).reshape(t.shape)
            return t * cos + rot * sin

        def _reference_tuple_inner(x, w_qkv, w_out, ln_g, ln_b, mem_beta):
            B, N, D = x.shape
            mu = x.mean(-1, keepdims=True)
            var = x.var(-1, keepdims=True)
            xn = (x - mu) / jnp.sqrt(var + 1e-05) * ln_g + ln_b
            qkv = xn @ w_qkv
            q, k, v = jnp.split(qkv, 3, axis=-1)

            def to_heads(t):
                return t.reshape(B, N, HEADS, DIM_HEAD).transpose(0, 2, 1, 3)
            q, k, v = map(to_heads, (q, k, v))
            next_k, next_v = (k, v)
            pos = jnp.arange(N, dtype=jnp.float32)
            qr, kr = (rope(q, pos), rope(k, pos))
            W = N // SEG

            def to_segs(t):
                return t.reshape(B, HEADS, W, SEG, DIM_HEAD).transpose(2, 0, 1, 3, 4)
            qs, ks, vs, qnope, knope = map(to_segs, (qr, kr, v, q, k))
            mask = jnp.tril(jnp.ones((SEG, SEG), bool))
            beta = jax.nn.sigmoid(mem_beta)
            mem0 = jnp.zeros((B, HEADS, DIM_HEAD, DIM_HEAD), x.dtype)
            z0 = jnp.full((B, HEADS, DIM_HEAD), 1e-06, x.dtype)

            def step(carry, inp):
                mem, z = carry
                q_s, k_s, v_s, qn_s, kn_s = inp
                scores = jnp.einsum('bhnd,bhmd->bhnm', q_s, k_s) * SCALE
                scores = jnp.where(mask, scores, -jnp.inf)
                sdpa = jnp.einsum('bhnm,bhmd->bhnd', jax.nn.softmax(scores, axis=-1), v_s)
                sq = elu1(qn_s)
                num = jnp.einsum('bhnk,bhkv->bhnv', sq, mem)
                den = jnp.einsum('bhnk,bhk->bhn', sq, z)[..., None]
                mem_out = num / (den + 1e-06)
                out = beta * mem_out + (1.0 - beta) * sdpa
                sk = elu1(kn_s)
                prev_v = jnp.einsum('bhnk,bhkv->bhnv', sk, mem) / jnp.einsum('bhnk,bhk->bhn', sk, z)[..., None]
                mem = mem + jnp.einsum('bhnk,bhnv->bhkv', sk, v_s - prev_v)
                z = z + sk.sum(axis=2)
                return ((mem, z), out)
            _, outs = jax.lax.scan(step, (mem0, z0), (qs, ks, vs, qnope, knope))
            o = outs.transpose(1, 0, 3, 2, 4).reshape(B, N, INNER)
            out = o @ w_out
            return (out, next_k, next_v)
        return _reference_tuple_inner(x, w_qkv, w_out, ln_g, ln_b, mem_beta)[0]

    def _L0_ffn_ref(hidden_states, gate_kernel, gate_bias, w_gate, w_up, w_down, sw_gate, sw_up, sw_down):
        import jax, jax.numpy as jnp
        import numpy as np
        H = 256
        M = 128
        E = 16
        TOP_K = 4
        N_GROUP = 4
        TOPK_GROUP = 2
        SCALE = 2.5
        B, S = (2, 256)

        def _gate(x2d, gate_kernel, gate_bias):
            n = x2d.shape[0]
            logits = jnp.dot(x2d.astype(jnp.float32), gate_kernel.astype(jnp.float32))
            scores = jax.nn.sigmoid(logits)
            scores_for_choice = scores + gate_bias
            group_scores = scores_for_choice.reshape(n, N_GROUP, E // N_GROUP)
            top2 = jax.lax.top_k(group_scores, k=2)[0]
            group_sum = jnp.sum(top2, axis=-1)
            group_idx = jax.lax.top_k(group_sum, k=TOPK_GROUP)[1]
            group_mask = jnp.zeros_like(group_sum).at[jnp.arange(n)[:, None], group_idx].set(1.0)
            score_mask = jnp.repeat(group_mask[:, :, None], E // N_GROUP, axis=2).reshape(n, E)
            masked_scores = jnp.where(score_mask > 0, scores_for_choice, 0.0)
            topk_weight, topk_idx = jax.lax.top_k(masked_scores, k=TOP_K)
            topk_weight = topk_weight / (jnp.sum(topk_weight, axis=-1, keepdims=True) + 1e-20)
            topk_weight = topk_weight * SCALE
            return (topk_idx, topk_weight)
        orig_shape = hidden_states.shape
        x = hidden_states.reshape(-1, orig_shape[-1])
        topk_idx, topk_weight = _gate(x, gate_kernel, gate_bias)
        onehot = (topk_idx[:, :, None] == jnp.arange(E)[None, None, :]).astype(topk_weight.dtype)
        combine = jnp.einsum('nke,nk->ne', onehot, topk_weight)
        g = jnp.einsum('nh,ehm->enm', x, w_gate)
        u = jnp.einsum('nh,ehm->enm', x, w_up)
        inter = jax.nn.silu(g) * u
        y_e = jnp.einsum('enm,emh->enh', inter, w_down)
        y = jnp.einsum('ne,enh->nh', combine, y_e)
        shared = jnp.dot(jax.nn.silu(jnp.dot(x, sw_gate)) * jnp.dot(x, sw_up), sw_down)
        return (y + shared).reshape(orig_shape)

    def _L1_xattn_ref(query, key, value, qpos, kpos, Wq, bq, Wk, bk, Wv, bv, Wo, bo):
        import jax, jax.numpy as jnp
        import numpy as np
        DIM = 256
        HEADS = 16
        HEAD_DIM = DIM // HEADS
        SCALE = HEAD_DIM ** (-0.5)
        B, Nq, C = query.shape

        def split_heads(x):
            return x.reshape(x.shape[0], x.shape[1], HEADS, HEAD_DIM).transpose(0, 2, 1, 3)
        q = split_heads(query @ Wq + bq)
        k = split_heads(key @ Wk + bk)
        v = split_heads(value @ Wv + bv)
        attn = jnp.einsum('bhqd,bhkd->bhqk', q, k) * SCALE
        attn = jax.nn.softmax(attn, axis=-1)
        x = jnp.einsum('bhqk,bhkd->bhqd', attn, v)
        x = x.transpose(0, 2, 1, 3).reshape(B, Nq, C)
        return x @ Wo + bo

    def _L1_attn_ref(x, W_q, W_k, W_v, W_o, W_down_kv, W_up_k, W_up_v):
        import jax, jax.numpy as jnp
        import numpy as np
        import math
        B, S, D = (4, 512, 256)
        H = 16
        HD = D // H
        DL = 64
        LAMBDA_DECAY = 0.01
        b, s, d = x.shape
        q = x @ W_q
        k = x @ W_k
        v = x @ W_v
        latent_kv = (k + v) @ W_down_kv
        k_rec = (latent_kv @ W_up_k).reshape(b, s, H, HD).transpose(0, 2, 1, 3)
        v_rec = (latent_kv @ W_up_v).reshape(b, s, H, HD).transpose(0, 2, 1, 3)
        qh = q.reshape(b, s, H, HD).transpose(0, 2, 1, 3)
        scores = jnp.einsum('bhqd,bhkd->bhqk', qh, k_rec) / math.sqrt(d)
        t = jnp.arange(s, dtype=jnp.float32)
        decay = jnp.exp(-LAMBDA_DECAY * jnp.abs(t[:, None] - t[None, :]))
        scores = scores * decay[None, None, :, :]
        attn = jax.nn.softmax(scores, axis=-1)
        out = jnp.einsum('bhqk,bhkd->bhqd', attn, v_rec)
        out = out.transpose(0, 2, 1, 3).reshape(b, s, d)
        return out @ W_o

    def _L1_ffn_ref(x, w1, conv_w, conv_b, w2):
        import jax, jax.numpy as jnp
        import numpy as np
        B, S, D_MODEL, D_HIDDEN = (4, 512, 256, 1024)

        def act_quant(x):
            scale = 127.0 / jnp.clip(jnp.max(jnp.abs(x), axis=-1, keepdims=True), 1e-05)
            return jnp.clip(jnp.round(x * scale), -128, 127) / scale

        def weight_quant(w):
            scale = 1.0 / jnp.clip(jnp.mean(jnp.abs(w)), 1e-05)
            return jnp.clip(jnp.round(w * scale), -1, 1) / scale

        def bit_linear(x, w):
            xq = x + jax.lax.stop_gradient(act_quant(x) - x)
            wq = w + jax.lax.stop_gradient(weight_quant(w) - w)
            return jnp.einsum('bsd,hd->bsh', xq, wq)

        def depthwise_conv1d(x_bcl, w, b):
            y = jax.lax.conv_general_dilated(x_bcl, w, window_strides=(1,), padding=[(1, 1)], dimension_numbers=('NCH', 'OIH', 'NCH'), feature_group_count=x_bcl.shape[1])
            return y + b[None, :, None]
        h = bit_linear(x, w1)
        h = depthwise_conv1d(h.transpose(0, 2, 1), conv_w, conv_b)
        h = h.transpose(0, 2, 1)
        h = jax.nn.silu(h)
        return bit_linear(h, w2)

    def _L2_xattn_ref(Q, K, V, Wq, bq, Wk, bk, Wv, bv, Wo, bo, attn_mask):
        import jax, jax.numpy as jnp
        import numpy as np
        D_MODEL = 256
        N_HEADS = 16
        D_K = D_MODEL // N_HEADS
        B, L = (4, 512)
        Bq, Lq, D = Q.shape
        Lk = K.shape[1]
        q = (Q @ Wq.T + bq).reshape(Bq, Lq, N_HEADS, D_K).transpose(0, 2, 1, 3)
        k = (K @ Wk.T + bk).reshape(Bq, Lk, N_HEADS, D_K).transpose(0, 2, 1, 3)
        v = (V @ Wv.T + bv).reshape(Bq, Lk, N_HEADS, D_K).transpose(0, 2, 1, 3)
        scores = jnp.einsum('bhqd,bhkd->bhqk', q, k) / jnp.sqrt(jnp.float32(D_K))
        mask = attn_mask[None, None, :, :]
        scores = jnp.where(mask == 0, jnp.float32(-jnp.inf), scores)
        attn = jax.nn.softmax(scores, axis=-1)
        out = jnp.einsum('bhqk,bhkd->bhqd', attn, v)
        out = out.transpose(0, 2, 1, 3).reshape(Bq, Lq, D)
        return out @ Wo.T + bo

    def _L2_attn_ref(x, gamma, beta, A, W_in, b_in, W_out, b_out):
        import jax, jax.numpy as jnp
        import numpy as np
        B, L, D = (16, 512, 256)
        LN_EPS = 1e-05
        mu = jnp.mean(x, axis=-1, keepdims=True)
        var = jnp.mean(jnp.square(x - mu), axis=-1, keepdims=True)
        z = (x - mu) * jax.lax.rsqrt(var + LN_EPS) * gamma + beta
        ug = jnp.einsum('bld,de->ble', z, W_in) + b_in
        d = x.shape[-1]
        u = ug[..., :d]
        g = jax.nn.sigmoid(ug[..., d:])

        def step(h, ug_t):
            u_t, g_t = ug_t
            h = g_t * h + (1.0 - g_t) * jnp.tanh(A * h + u_t)
            return (h, h)
        h0 = jnp.zeros((x.shape[0], d), x.dtype)
        _, hs = jax.lax.scan(step, h0, (jnp.swapaxes(u, 0, 1), jnp.swapaxes(g, 0, 1)))
        hs = jnp.swapaxes(hs, 0, 1)
        out = jnp.einsum('bld,de->ble', hs, W_out) + b_out
        return x + out

    def _L2_ffn_ref(x, router_w, expert_w1, expert_b1, expert_w2, expert_b2):
        import jax, jax.numpy as jnp
        import numpy as np
        TOP_K = 2
        router_logits = jnp.einsum('bnc,ec->bne', x, router_w)
        router_probs = jax.nn.softmax(router_logits, axis=-1)
        expert_weights, expert_idx = jax.lax.top_k(router_probs, TOP_K)
        expert_weights = expert_weights / (expert_weights.sum(axis=-1, keepdims=True) + 1e-09)
        h = jnp.einsum('bnc,efc->bnef', x, expert_w1) + expert_b1
        h = jax.nn.gelu(h, approximate=False)
        out_all = jnp.einsum('bnef,ecf->bnec', h, expert_w2) + expert_b2
        out_k = jnp.take_along_axis(out_all, expert_idx[..., None], axis=2)
        return (out_k * expert_weights[..., None]).sum(axis=2)

    def _L3_xattn_ref(q, k, v, Wq, bq, Wk, bk, Wv, bv, Wo, bo):
        import jax, jax.numpy as jnp
        import numpy as np
        DIM = 256
        NUM_HEADS = 16
        HEAD_DIM = DIM // NUM_HEADS
        B, Nq, C = q.shape
        Nkv = k.shape[1]
        H, D = (NUM_HEADS, HEAD_DIM)
        qh = (q @ Wq.T + bq).reshape(B, Nq, H, D).transpose(0, 2, 1, 3)
        kh = (k @ Wk.T + bk).reshape(B, Nkv, H, D).transpose(0, 2, 1, 3)
        vh = (v @ Wv.T + bv).reshape(B, Nkv, H, D).transpose(0, 2, 1, 3)
        scale = D ** (-0.5)
        attn = jax.nn.softmax(jnp.einsum('bhqd,bhkd->bhqk', qh, kh) * scale, axis=-1)
        out = jnp.einsum('bhqk,bhkd->bhqd', attn, vh)
        out = out.transpose(0, 2, 1, 3).reshape(B, Nq, C)
        return out @ Wo.T + bo

    def _L3_attn_ref(x, W_in, conv_w, conv_b, W_x, W_dt, b_dt, A_log, Dp, W_out1, W_out2):
        import jax, jax.numpy as jnp
        import numpy as np
        D_MODEL = 256
        D_STATE = 16
        D_CONV = 4
        EXPAND = 2
        D_INNER = EXPAND * D_MODEL
        DT_RANK = (D_MODEL + 15) // 16
        BATCH = 2
        SEQLEN = 512

        def _mefi_forward(x, W_in, conv_w, conv_b, W_x, W_dt, b_dt, A_log, Dp, W_out1, W_out2):
            B, L, _ = x.shape
            xz = jnp.einsum('bld,ed->bel', x, W_in)
            xi, z = (xz[:, :D_INNER, :], xz[:, D_INNER:, :])
            xc = jax.lax.conv_general_dilated(xi, conv_w[:, None, :], window_strides=(1,), padding=[(D_CONV - 1, 0)], dimension_numbers=('NCH', 'OIH', 'NCH'), feature_group_count=D_INNER)
            u = jax.nn.silu(xc + conv_b[None, :, None])
            x_dbl = jnp.einsum('bdl,ed->ble', u, W_x)
            dt_r = x_dbl[..., :DT_RANK]
            Bm = x_dbl[..., DT_RANK:DT_RANK + D_STATE].transpose(0, 2, 1)
            Cm = x_dbl[..., DT_RANK + D_STATE:].transpose(0, 2, 1)
            dt = jnp.einsum('blr,dr->bdl', dt_r, W_dt)
            A = -jnp.exp(A_log)
            delta = jax.nn.softplus(dt + b_dt[None, :, None])

            def step(s, inp):
                d_t, u_t, B_t, C_t = inp
                dA = jnp.exp(d_t[:, :, None] * A[None, :, :])
                s = dA * s + (d_t * u_t)[:, :, None] * B_t[:, None, :]
                y_t = jnp.einsum('bdn,bn->bd', s, C_t)
                return (s, y_t)
            s0 = jnp.zeros((B, D_INNER, D_STATE), delta.dtype)
            xs = (delta.transpose(2, 0, 1), u.transpose(2, 0, 1), Bm.transpose(2, 0, 1), Cm.transpose(2, 0, 1))
            _, ys = jax.lax.scan(step, s0, xs)
            y = ys.transpose(1, 2, 0)
            y = (y + Dp[None, :, None] * u) * jax.nn.silu(z)
            y_t = jnp.einsum('bnl,dn->bld', Cm, A) + jnp.einsum('d,bdl->bl', Dp, u)[..., None]
            y_cat = jnp.concatenate([y.transpose(0, 2, 1), y_t], axis=-1)
            h = jnp.maximum(y_cat @ W_out1.T, 0.0)
            return h @ W_out2.T
        return _mefi_forward(x, W_in, conv_w, conv_b, W_x, W_dt, b_dt, A_log, Dp, W_out1, W_out2)

    def _L3_ffn_ref(x, ln_w, Wg, bg, W1a, b1a, W1b, b1b, W2, b2):
        import jax, jax.numpy as jnp
        import numpy as np
        E = 8
        K = 2
        B, S, D = x.shape
        eps = jnp.finfo(x.dtype).eps
        xn = x * jax.lax.rsqrt(jnp.mean(x * x, axis=-1, keepdims=True) + eps) * ln_w
        logits = xn @ Wg + bg
        vals, idx = jax.lax.top_k(logits, K)
        topk_w = jax.nn.softmax(vals, axis=-1)
        we = jnp.sum(jax.nn.one_hot(idx, E, dtype=x.dtype) * topk_w[..., None], axis=-2)
        T = B * S
        xf = xn.reshape(T, D)
        wef = we.reshape(T, E).T

        def step(acc, params):
            W1a_e, b1a_e, W1b_e, b1b_e, W2_e, b2_e, w_e = params
            a = xf @ W1a_e + b1a_e
            b = xf @ W1b_e + b1b_e
            y = jax.nn.silu(a) * b @ W2_e + b2_e
            return (acc + w_e[:, None] * y, None)
        out0 = jnp.zeros_like(xf)
        out, _ = jax.lax.scan(step, out0, (W1a, b1a, W1b, b1b, W2, b2, wef))
        return out.reshape(B, S, D)
    x = x + _L0_xattn_ref(_layernorm(x, axis=-1), ctx_1024, ctx_1024, L0_xattn_in_proj_weight, L0_xattn_in_proj_bias, L0_xattn_out_proj_weight, L0_xattn_out_proj_bias, L0_xattn_lambda_q1, L0_xattn_lambda_k1, L0_xattn_lambda_q2, L0_xattn_lambda_k2)
    x = x + _L0_attn_ref(_layernorm(x, axis=-1), L0_attn_w_qkv, L0_attn_w_out, L0_attn_ln_g, L0_attn_ln_b, L0_attn_mem_beta)
    x = x + _L0_ffn_ref(_layernorm(x, axis=-1), L0_ffn_gate_kernel, L0_ffn_gate_bias, L0_ffn_w_gate, L0_ffn_w_up, L0_ffn_w_down, L0_ffn_sw_gate, L0_ffn_sw_up, L0_ffn_sw_down)
    x = x + _L1_xattn_ref(_layernorm(x, axis=-1), ctx_1024, ctx_1024, itok_BxS2_0_2047, itok_BxS2_0_2047, L1_xattn_Wq, L1_xattn_bq, L1_xattn_Wk, L1_xattn_bk, L1_xattn_Wv, L1_xattn_bv, L1_xattn_Wo, L1_xattn_bo)
    x = x + _L1_attn_ref(_layernorm(x, axis=-1), L1_attn_W_q, L1_attn_W_k, L1_attn_W_v, L1_attn_W_o, L1_attn_W_down_kv, L1_attn_W_up_k, L1_attn_W_up_v)
    x = x + _L1_ffn_ref(_layernorm(x, axis=-1), L1_ffn_w1, L1_ffn_conv_w, L1_ffn_conv_b, L1_ffn_w2)
    x = x + _L2_xattn_ref(_layernorm(x, axis=-1), ctx_1024, ctx_1024, L2_xattn_Wq, L2_xattn_bq, L2_xattn_Wk, L2_xattn_bk, L2_xattn_Wv, L2_xattn_bv, L2_xattn_Wo, L2_xattn_bo, mask_SxS2_ik0)
    x = x + _L2_attn_ref(_layernorm(x, axis=-1), L2_attn_gamma, L2_attn_beta, L2_attn_A, L2_attn_W_in, L2_attn_b_in, L2_attn_W_out, L2_attn_b_out)
    x = x + _L2_ffn_ref(_layernorm(x, axis=-1), L2_ffn_router_w, L2_ffn_expert_w1, L2_ffn_expert_b1, L2_ffn_expert_w2, L2_ffn_expert_b2)
    x = x + _L3_xattn_ref(_layernorm(x, axis=-1), ctx_1024, ctx_1024, L3_xattn_Wq, L3_xattn_bq, L3_xattn_Wk, L3_xattn_bk, L3_xattn_Wv, L3_xattn_bv, L3_xattn_Wo, L3_xattn_bo)
    x = x + _L3_attn_ref(_layernorm(x, axis=-1), L3_attn_W_in, L3_attn_conv_w, L3_attn_conv_b, L3_attn_W_x, L3_attn_W_dt, L3_attn_b_dt, L3_attn_A_log, L3_attn_Dp, L3_attn_W_out1, L3_attn_W_out2)
    x = x + _L3_ffn_ref(_layernorm(x, axis=-1), L3_ffn_ln_w, L3_ffn_Wg, L3_ffn_bg, L3_ffn_W1a, L3_ffn_b1a, L3_ffn_W1b, L3_ffn_b1b, L3_ffn_W2, L3_ffn_b2)
    return x

_drawn_inputs = setup_inputs


def setup_inputs(seed=0):
    import zlib

    import numpy as np

    out = dict(_drawn_inputs(seed))
    spreads = {'L0_xattn_in_proj_bias': (0.0, 0.1),
     'L0_xattn_out_proj_bias': (0.0, 0.1),
     'L0_attn_ln_g': (1.0, 0.2),
     'L0_attn_ln_b': (0.0, 0.1),
     'L0_attn_mem_beta': (0.0, 0.1),
     'L1_xattn_bq': (0.0, 0.29),
     'L1_xattn_bk': (0.0, 2.0),
     'L1_xattn_bv': (0.0, 0.1),
     'L1_xattn_bo': (0.0, 0.1),
     'L2_xattn_bq': (0.0, 0.345),
     'L2_xattn_bk': (0.0, 2.0),
     'L2_xattn_bv': (0.0, 0.1),
     'L2_xattn_bo': (0.0, 0.1),
     'L2_attn_gamma': (1.0, 0.2),
     'L2_attn_beta': (0.0, 0.1),
     'L2_attn_b_in': (0.0, 0.1),
     'L2_attn_b_out': (0.0, 0.1),
     'L2_ffn_expert_b1': (0.0, 0.288),
     'L2_ffn_expert_b2': (0.0, 0.1),
     'L3_xattn_bq': (0.0, 0.8),
     'L3_xattn_bk': (0.0, 2.0),
     'L3_xattn_bv': (0.0, 0.1),
     'L3_xattn_bo': (0.0, 0.1),
     'L3_attn_conv_b': (0.0, 0.1),
     'L3_attn_Dp': (1.0, 0.6),
     'L3_ffn_ln_w': (1.0, 0.2),
     'L3_ffn_bg': (0.0, 0.1),
     'L3_ffn_b1a': (0.0, 0.514),
     'L3_ffn_b1b': (0.0, 0.534),
     'L3_ffn_b2': (0.0, 0.336)}
    factors = {'L2_attn_A': 3.115, 'L3_attn_W_dt': 64.0, 'L3_attn_b_dt': 64.0}
    for name, (base, spread) in spreads.items():
        noise = np.random.default_rng([zlib.crc32(name.encode()), seed]).standard_normal(out[name].shape)
        drawn = base * np.exp(spread * noise) if base else spread * noise
        out[name] = jnp.asarray(drawn.astype(out[name].dtype))
    for name, factor in factors.items():
        out[name] = (out[name] * factor).astype(out[name].dtype)
    return out
```

```python
from contextlib import ExitStack

import numpy as np

import concourse.bass as bass
from concourse import mybir

F32 = mybir.dt.float32
BF16 = mybir.dt.bfloat16
I32 = mybir.dt.int32
U32 = mybir.dt.uint32
ALU = mybir.AluOpType
ACT = mybir.ActivationFunctionType
AX = mybir.AxisListType

P = 128
B, S, D = 16, 64, 256
T = B * S
NT = T // P
DC = D // P
HALF = 512
NKEY = 1601
KT = -(-NKEY // P)
HEADS = 16
HD = D // HEADS
LAST_KEYS = NKEY - (KT - 1) * P
MASKED = -1e30


class Chain:

    def __init__(self, engine, sem, base=0):
        self.engine, self.sem, self.base, self.n = engine, sem, base, 0

    def __call__(self, instruction):
        self.n += 1
        instruction.then_inc(self.sem, 1)
        self.engine.wait_ge(self.sem, self.base + self.n)
        return instruction


class Env:

    def __init__(self, nc, ctx, dram):
        self.nc, self.ctx, self.dram = nc, ctx, dram
        self.serial = 0
        self.stage_sems = []
        self.x = self.sbuf("x_stream", [P, NT, D])
        self.xn = self.sbuf("x_normed", [P, NT, D])
        self.xt = self.sbuf("x_normed_T", [P, DC, T])
        self.ident = self.sbuf("identity", [P, P])
        self.psum = ctx.enter_context(nc.psum_tensor("psum_all", [P, 8, 512], F32))

    def sbuf(self, name, shape, dtype=F32, ctx=None):
        self.serial += 1
        return (ctx or self.ctx).enter_context(self.nc.sbuf_tensor(f"{name}_{self.serial}", shape, dtype))

    def sem(self, name):
        self.serial += 1
        handle = self.nc.alloc_semaphore(f"{name}_{self.serial}")
        self.stage_sems.append(handle)
        return handle

    def end_stage(self):
        nc, sems = self.nc, self.stage_sems
        with nc.Block() as block:

            @block.sync
            def _(sp):
                for handle in sems:
                    sp.sem_clear(handle)

        for handle in sems:
            nc.release_semaphore(handle)
        self.stage_sems = []

    def bank(self, k):
        return self.psum[:, k, :]


def load_stream(env):
    nc = env.nc
    loaded = env.sem("stream_loaded")
    with nc.Block() as block:

        @block.sync
        def _(sp):
            sp.dma_start(env.x[:, :, :], env.dram["x"].rearrange("(n p) d -> p n d", p=P)).then_inc(loaded, 16)
            sp.dma_start(env.ident[:, :], env.dram["identity"]).then_inc(loaded, 16)
            sp.wait_ge(loaded, 32)


def store_stream(env):
    nc = env.nc
    stored = env.sem("stream_stored")
    with nc.Block() as block:

        @block.sync
        def _(sp):
            sp.dma_start(env.dram["out"].rearrange("(n p) d -> p n d", p=P), env.x[:, :, :]).then_inc(stored, 16)
            sp.wait_ge(stored, 16)


def normalise(env, src, transpose=True, gain=None, shift=None, rms=False, eps=1e-5):
    nc = env.nc
    chain_s, normed, turned, loaded = (env.sem(n) for n in ("norm_chain", "tile_normed", "tile_turned", "gain_loaded"))
    var_ready, deviation_ready = env.sem("var_ready"), env.sem("deviation_ready")
    with ExitStack() as ctx:
        stats = env.sbuf("stats", [P, NT, 6], ctx=ctx)
        moments = env.sbuf("moments", [P, NT, 2], ctx=ctx)
        rstd = env.sbuf("rstd", [P, NT], ctx=ctx)
        deviation = env.sbuf("deviation", [P, NT], ctx=ctx)
        affine = env.sbuf("affine", [P, 2, DC], ctx=ctx)
        rows = (gain is not None) + (shift is not None)
        with nc.Block() as block:

            @block.sync
            def _(sp):
                for i, row in enumerate((gain, shift)):
                    if row is not None:
                        sp.dma_start(affine[:, i, :], env.dram[row]).then_inc(loaded, 16)

            @block.vector
            def _(dve):
                chain = Chain(dve, chain_s)
                for t in range(NT):
                    nc.vector.bn_stats(stats[:, t, :], src[:, t, :]).then_inc(chain_s, 1)
                chain.n = NT
                dve.wait_ge(chain_s, NT)
                for t in range(NT):
                    nc.vector.bn_aggr(moments[:, t, :], stats[:, t, :]).then_inc(chain_s, 1)
                chain.n = 2 * NT
                dve.wait_ge(chain_s, 2 * NT)
                if rms:
                    chain(nc.vector.tensor_tensor(rstd[:, :], moments[:, :, 0], moments[:, :, 0], ALU.mult))
                    chain(nc.vector.tensor_tensor(moments[:, :, 1], moments[:, :, 1], rstd[:, :], ALU.add))
                    chain(nc.vector.memset(moments[:, :, 0], 0.0))
                nc.vector.tensor_scalar(rstd[:, :], moments[:, :, 1], eps, None, ALU.add).then_inc(var_ready, 1)
                dve.wait_ge(deviation_ready, 1)
                chain(nc.vector.reciprocal(rstd[:, :], deviation[:, :]))
                for t in range(NT):
                    nc.vector.tensor_scalar(env.xn[:, t, :], src[:, t, :], moments[:, t, 0:1], rstd[:, t:t + 1],
                                            ALU.subtract, ALU.mult).then_inc(normed, 1)

            if transpose:

                @block.tensor
                def _(pe):
                    for t in range(NT):
                        pe.wait_ge(normed, t + 1)
                        for c in range(DC):
                            mm = nc.tensor.transpose(env.psum[:, t, c * P:(c + 1) * P],
                                                     env.xn[:, t, c * P:(c + 1) * P], env.ident[:, :])
                        mm.then_inc(turned, 1)

            @block.scalar
            def _(act):
                act.wait_ge(var_ready, 1)
                nc.scalar.activation(deviation[:, :], rstd[:, :], ACT.Sqrt).then_inc(deviation_ready, 1)
                if not transpose:
                    return
                if rows:
                    act.wait_ge(loaded, 16 * rows)
                for t in range(NT):
                    act.wait_ge(turned, t + 1)
                    here = slice(t * P, (t + 1) * P)
                    if not rows:
                        nc.scalar.copy(env.xt[:, :, here],
                                       env.psum[:, t, 0:D].rearrange("p (c n) -> p c n", c=DC))
                        continue
                    for c in range(DC):
                        nc.scalar.activation(env.xt[:, c, here], env.psum[:, t, c * P:(c + 1) * P], ACT.Identity,
                                             scale=affine[:, 0, c:c + 1],
                                             bias=affine[:, 1, c:c + 1] if shift is not None else 0.0)


def add_projected(env, o_rows, w_o, scale=1.0):
    nc = env.nc
    o_turned, o_ready, out_filled, out_free = (env.sem(n) for n in ("o_turned", "o_ready", "out_filled", "out_free"))
    with ExitStack() as ctx:
        o_t = env.sbuf("o_t", [P, DC, T], ctx=ctx)
        with nc.Block() as block:

            @block.tensor
            def _(pe):
                for b in range(B):
                    if b >= 4:
                        pe.wait_ge(o_ready, b - 3)
                    for c in range(DC):
                        mm = nc.tensor.transpose(env.psum[:, b % 4, c * S:(c + 1) * S],
                                                 o_rows[:, b, c * P:(c + 1) * P], env.ident[0:S, 0:S])
                    mm.then_inc(o_turned, 1)
                for t in range(NT):
                    pe.wait_ge(o_ready, 2 * t + 2)
                    if t >= 4:
                        pe.wait_ge(out_free, t - 3)
                    for k in range(DC):
                        mm = nc.tensor.matmul(env.psum[:, 4 + t % 4, 0:D], o_t[:, k, t * P:(t + 1) * P], w_o[:, k, :],
                                              start=(k == 0), stop=(k == DC - 1))
                    mm.then_inc(out_filled, 1)

            @block.scalar
            def _(act):
                for b in range(B):
                    act.wait_ge(o_turned, b + 1)
                    nc.scalar.mul(o_t[:, :, b * S:(b + 1) * S],
                                  env.psum[:, b % 4, 0:DC * S].rearrange("p (c q) -> p c q", c=DC),
                                  scale).then_inc(o_ready, 1)

            @block.vector
            def _(dve):
                for t in range(NT):
                    dve.wait_ge(out_filled, t + 1)
                    nc.vector.tensor_tensor(env.x[:, t, :], env.x[:, t, :], env.psum[:, 4 + t % 4, 0:D],
                                            ALU.add).then_inc(out_free, 1)


def cross_attention(env, pre, wq, wk, wv, wo, bq, bk, bv, bo, lambdas=None, mask=None):
    nc = env.nc
    subs = 2 if lambdas is None else 4
    R = HEADS * subs // 4
    W = D // R
    GK, GV = 2 * 4, -(-KT // 2)
    C5, C4 = GK + 2 * R, GV + 2 * R
    key_cut = [(k * 512, min(512, NKEY - k * 512)) for k in range(4)]
    EXP_CUT = [(0, 1024), (1024, NKEY)]

    weights_loaded, const_ready = env.sem("weights_loaded"), env.sem("const_ready")
    q_filled, q_ready, qd_ready = env.sem("q_filled"), env.sem("q_ready"), env.sem("q_diag_ready")
    ctx_loaded = env.sem("ctx_loaded")
    bank4_filled, bank4_free = env.sem("bank4_filled"), env.sem("bank4_free")
    bank5_filled, bank5_free = env.sem("bank5_filled"), env.sem("bank5_free")
    scored, max_ready, exp_done = env.sem("scored"), env.sem("max_ready"), env.sem("exp_done")
    pv_done, o_taken = env.sem("pv_done"), env.sem("o_taken")
    sum_s, end_s = env.sem("sum_chain"), env.sem("end_chain")
    dve_out = env.sem("o_first_ready")

    with ExitStack() as ctx:
        def sb(name, shape, dtype=F32):
            return env.sbuf(pre + name, shape, dtype, ctx)

        w_q, w_k, w_v, w_o = (sb(n, [P, DC, D]) for n in ("wq", "wk", "wv", "wo"))
        b_q, b_k = sb("bq", [P, DC]), sb("bk", [P, DC])
        b_v, b_o = sb("bv", [P, D]), sb("bo", [P, D])
        head_mask = sb("head_mask", [P, subs])
        q_t = sb("q_t", [P, DC, T])
        q_diag = sb("q_diag", [P, DC, subs, S])
        ctx_t = sb("ctx_t", [P, DC, NKEY])
        k_t = sb("k_t", [P, DC, NKEY])
        v = sb("v", [P, KT, D])
        probs = sb("probs", [P, 2, NKEY])
        probs_t = sb("probs_t", [P, 2, KT, P])
        neg_max = sb("neg_max", [P, 2])
        sums = sb("sums", [P, 2, R, 2])
        total = sb("total", [P, R])
        inverse = sb("inverse", [P, R])
        o_rows = sb("o_rows", [S, B, D])
        if lambdas:
            lam_in = sb("lam_in", [P, 4, 8])
            lam_prod = sb("lam_prod", [P, 2, 8])
            lam = sb("lam", [P, 4])
            o_second = sb("o_second", [S, R, W])
        if mask:
            mask_in = sb("mask_in", [S, NKEY], I32)
            mask_add = sb("mask_add", [S, NKEY], BF16)
            twice = sb("twice", [S, 2, S], BF16)
            twice_in = sb("twice_in", [S, 2, S])
        loads = [(w_q[:, :, :], env.dram[wq]), (w_k[:, :, :], env.dram[wk]), (w_v[:, :, :], env.dram[wv]),
                 (w_o[:, :, :], env.dram[wo]), (b_q[:, :], env.dram[bq]), (b_k[:, :], env.dram[bk]),
                 (b_v[:, :], env.dram[bv].partition_broadcast(P)), (b_o[:, :], env.dram[bo].partition_broadcast(P)),
                 (head_mask[:, :], env.dram[f"head_mask_{subs}"])]
        if lambdas:
            loads += [(lam_in[:, i, :], env.dram[n].partition_broadcast(P)) for i, n in enumerate(lambdas)]
        if mask:
            loads += [(mask_in[:, :], env.dram[mask])]
            loads += [(twice_in[:, s, :], env.dram["identity"][0:S, 0:S]) for s in range(2)]
        s_all = env.psum[:, 0:4, :].rearrange("p k n -> p (k n)")
        o_psum = env.psum[:, 6, 0:D].rearrange("p (r w) -> p r w", r=R)

        with nc.Block() as block:

            @block.sync
            def _(sp):
                for dst, src in loads:
                    sp.dma_start(dst, src).then_inc(weights_loaded, 16)
                sp.dma_start(ctx_t[:, :, :], env.dram["ctx_t"][0]).then_inc(ctx_loaded, 16)
                with sp.Fori(0, B - 1) as b:
                    sp.wait_ge(bank5_filled, b * C5 + GK)
                    sp.dma_start(ctx_t[:, :, :], env.dram["ctx_t"][bass.ds(b + 1, 1)].rearrange(
                        "o p c n -> p (o c) n")).then_inc(ctx_loaded, 16)

            @block.gpsimd
            def _(pool):
                pool.wait_ge(weights_loaded, 16 * len(loads))
                for t in range(NT):
                    nc.gpsimd.tensor_tensor(env.x[:, t, :], env.x[:, t, :], b_o[:, :], ALU.add)

            @block.tensor
            def _(pe):
                pe.wait_ge(weights_loaded, 16 * len(loads))
                for m in range(DC):
                    for h in range(2):
                        for k in range(DC):
                            mm = nc.tensor.matmul(env.bank(2 * m + h), w_q[:, k, m * P:(m + 1) * P],
                                                  env.xt[:, k, h * HALF:(h + 1) * HALF],
                                                  start=(k == 0), stop=(k == DC - 1))
                        mm.then_inc(q_filled, 1)
                pe.wait_ge(q_ready, 4)
                if mask:
                    pe.wait_ge(const_ready, 1)

                with pe.Fori(0, B) as b:
                    pe.wait_ge(ctx_loaded, 16 * b + 16)

                    def free(sem, per_batch, n):
                        pe.wait_ge(sem, b * per_batch + n)

                    for g in range(GK):
                        m, (at, width) = g // 4, key_cut[g % 4]
                        free(bank5_free, C5, g)
                        for k in range(DC):
                            mm = nc.tensor.matmul(env.psum[:, 5, 0:width], w_k[:, k, m * P:(m + 1) * P],
                                                  ctx_t[:, k, at:at + width], start=(k == 0), stop=(k == DC - 1))
                        mm.then_inc(bank5_filled, 1)
                        if g >= GV:
                            continue
                        free(bank4_free, C4, g)
                        for j in range(2 * g, min(2 * g + 2, KT)):
                            rows = P if j < KT - 1 else LAST_KEYS
                            for k in range(DC):
                                mm = nc.tensor.matmul(env.psum[0:rows, 4, (j % 2) * D:(j % 2 + 1) * D],
                                                      ctx_t[:, k, j * P:j * P + rows], w_v[:, k, :],
                                                      start=(k == 0), stop=(k == DC - 1))
                        mm.then_inc(bank4_filled, 1)

                    def scores(r):
                        if r == 0:
                            pe.wait_ge(qd_ready, b * subs + subs)
                            free(bank5_free, C5, GK)
                        c, j = (r // 4, r % 4) if subs == 2 else (r // 8, r % 8 // 2)
                        first = 0 if subs == 2 else 2 * (r % 2)
                        rows = slice(32 * j, 32 * j + 32)
                        for n, (at, width) in enumerate(key_cut):
                            if n % 2 == 0:
                                pe.wait_ge(exp_done, b * (2 * R) + 2 * r - 1 + n // 2) if r else \
                                    pe.wait_ge(exp_done, b * (2 * R))
                            mm = nc.tensor.matmul(s_all[:, at:at + width],
                                                  q_diag[rows, c, first:first + 2, :].rearrange("p s q -> p (s q)"),
                                                  k_t[rows, c, at:at + width], start=True, stop=mask is None,
                                                  tile_position=(32 * j, 0))
                            if mask:
                                mm = nc.tensor.matmul(s_all[:, at:at + width], twice[:, :, :].rearrange(
                                    "p s q -> p (s q)"), mask_add[:, at:at + width], start=False, stop=True)
                        mm.then_inc(scored, 1)

                    def turn(r):
                        for f in range(4):
                            if f % 2 == 0:
                                free(bank4_free, C4, GV + 2 * r + f // 2)
                            else:
                                free(bank5_free, C5, GK + 2 * r + f // 2)
                            if f in (0, 2):
                                pe.wait_ge(exp_done, b * (2 * R) + 2 * r + 1 + f // 2)
                            for j in range(4 * f, min(4 * f + 4, KT)):
                                rows = P if j < KT - 1 else LAST_KEYS
                                mm = nc.tensor.transpose(env.psum[0:rows, 4 + f % 2, (j % 4) * P:(j % 4 + 1) * P],
                                                         probs[:, r % 2, j * P:j * P + rows], env.ident[:, :])
                            mm.then_inc(bank4_filled if f % 2 == 0 else bank5_filled, 1)

                    def weigh(r):
                        if r == 0:
                            pe.wait_ge(o_taken, b)
                        free(bank4_free, C4, GV + 2 * r + 2)
                        free(bank5_free, C5, GK + 2 * r + 2)
                        for j in range(KT):
                            rows = P if j < KT - 1 else LAST_KEYS
                            mm = nc.tensor.matmul(o_psum[:, r, :], probs_t[0:rows, r % 2, j, :],
                                                  v[0:rows, j, r * W:(r + 1) * W], start=(j == 0), stop=(j == KT - 1))
                        mm.then_inc(pv_done, 1)

                    for r in range(R + 2):
                        if r < R:
                            scores(r)
                        if 1 <= r <= R:
                            turn(r - 1)
                        if r >= 2:
                            weigh(r - 2)

            @block.scalar
            def _(act):
                act.wait_ge(weights_loaded, 16 * len(loads))
                for m in range(DC):
                    for h in range(2):
                        act.wait_ge(q_filled, 2 * m + h + 1)
                        nc.scalar.activation(q_t[:, m, h * HALF:(h + 1) * HALF], env.bank(2 * m + h), ACT.Identity,
                                             bias=b_q[:, m:m + 1]).then_inc(q_ready, 1)
                if lambdas:
                    act.wait_ge(const_ready, 1)
                    nc.scalar.activation(lam[:, 2:4], lam[:, 0:2], ACT.Exp).then_inc(const_ready, 1)

                with act.Fori(0, B) as b:
                    for g in range(GK):
                        m, (at, width) = g // 4, key_cut[g % 4]
                        act.wait_ge(bank5_filled, b * C5 + g + 1)
                        nc.scalar.activation(k_t[:, m, at:at + width], env.psum[:, 5, 0:width], ACT.Identity,
                                             bias=b_k[:, m:m + 1]).then_inc(bank5_free, 1)

                    def take(r, f):
                        tiles = min(4, KT - 4 * f)
                        rows = P if tiles == 4 else LAST_KEYS
                        act.wait_ge(bank5_filled, b * C5 + GK + 2 * r + f // 2 + 1)
                        if f == 1 and r >= 2:
                            act.wait_ge(pv_done, b * R + r - 1)
                        nc.scalar.copy(probs_t[0:rows, r % 2, 4 * f:4 * f + tiles, :],
                                       env.psum[0:rows, 5, 0:tiles * P].rearrange("p (j n) -> p j n", n=P)
                                       ).then_inc(bank5_free, 1)

                    for r in range(R + 1):
                        if r >= 1:
                            take(r - 1, 1)
                        if r < R:
                            act.wait_ge(max_ready, b * R + r + 1)
                            if r >= 2:
                                act.wait_ge(bank5_filled, b * C5 + GK + 2 * (r - 1))
                            for n, (at, end) in enumerate(EXP_CUT):
                                nc.scalar.activation(probs[:, r % 2, at:end], s_all[:, at:end], ACT.Exp,
                                                     bias=neg_max[:, r % 2:r % 2 + 1],
                                                     accum_out=sums[:, 0, r, n:n + 1]).then_inc(exp_done, 1)
                        if r >= 1:
                            take(r - 1, 3)

            @block.vector
            def _(dve):
                dve.wait_ge(weights_loaded, 16 * len(loads))
                chain = Chain(dve, end_s)
                if lambdas:
                    for i in range(2):
                        chain(nc.vector.tensor_tensor(lam_prod[:, i, :], lam_in[:, 2 * i, :], lam_in[:, 2 * i + 1, :],
                                                      ALU.mult))
                    nc.vector.tensor_reduce(lam[:, 0:2], lam_prod[:, :, :], AX.X, ALU.add).then_inc(const_ready, 1)
                    dve.wait_ge(const_ready, 2)
                    chain(nc.vector.tensor_tensor(lam[:, 0:1], lam[:, 3:4], lam[:, 2:3], ALU.subtract))
                    chain(nc.vector.tensor_scalar(lam[:, 0:1], lam[:, 0:1], -0.2, None, ALU.add))
                if mask:
                    for s in range(2):
                        chain(nc.vector.tensor_copy(twice[:, s, :], twice_in[:, s, :]))
                    nc.vector.tensor_scalar(mask_add[:, :], mask_in[:, :], 0.0, MASKED, ALU.is_equal,
                                            ALU.mult).then_inc(const_ready, 1)
                dve.wait_ge(q_ready, 4)

                with dve.Fori(0, B) as b:
                    for s in range(subs):
                        nc.vector.tensor_scalar(q_diag[:, :, s, :], q_t[:, :, bass.ds(b * S, S)],
                                                head_mask[:, s:s + 1], None, ALU.mult).then_inc(qd_ready, 1)
                    for g in range(GV):
                        tiles = min(2, KT - 2 * g)
                        rows = P if tiles == 2 else LAST_KEYS
                        dve.wait_ge(bank4_filled, b * C4 + g + 1)
                        nc.vector.tensor_tensor(v[0:rows, 2 * g:2 * g + tiles, :],
                                                env.psum[0:rows, 4, 0:tiles * D].rearrange("p (j d) -> p j d", d=D),
                                                b_v[0:rows, None, :].to_broadcast([rows, tiles, D]),
                                                ALU.add).then_inc(bank4_free, 1)

                    def take(r, f):
                        dve.wait_ge(bank4_filled, b * C4 + GV + 2 * r + f // 2 + 1)
                        if f == 0 and r >= 2:
                            dve.wait_ge(pv_done, b * R + r - 1)
                        nc.vector.tensor_copy(probs_t[:, r % 2, 4 * f:4 * f + 4, :],
                                              env.psum[:, 4, :].rearrange("p (j n) -> p j n", n=P)
                                              ).then_inc(bank4_free, 1)

                    for r in range(R + 1):
                        if r < R:
                            dve.wait_ge(scored, b * R + r + 1)
                            if r >= 2:
                                dve.wait_ge(exp_done, b * (2 * R) + 2 * (r - 1))
                            nc.vector.tensor_reduce(neg_max[:, r % 2:r % 2 + 1], s_all[:, 0:NKEY], AX.X, ALU.max,
                                                    negate=True).then_inc(max_ready, 1)
                        if r >= 1:
                            take(r - 1, 0)
                            take(r - 1, 2)

                    L = 4 if lambdas else 2
                    done = Chain(dve, sum_s, b * L)
                    dve.wait_ge(exp_done, b * (2 * R) + 2 * R)
                    done(nc.vector.tensor_tensor(total[:, :], sums[:, 0, :, 0], sums[:, 0, :, 1], ALU.add))
                    done(nc.vector.reciprocal(inverse[:, :], total[:, :]))
                    if lambdas:
                        done(nc.vector.tensor_scalar(inverse[S:P, :], inverse[S:P, :], lam[S:P, 0:1], None, ALU.mult))
                    dve.wait_ge(pv_done, b * R + R)
                    out = o_rows[:, bass.ds(b, 1), :]
                    if lambdas:
                        done(nc.vector.tensor_tensor(o_second[:, :, :], o_psum[S:P, :, :],
                                                     inverse[S:P, :, None].to_broadcast([S, R, W]), ALU.mult))
                        out = out.rearrange("p o (r w) -> p (o r) w", w=W)
                        nc.vector.tensor_tensor(out, o_psum[0:S, :, :],
                                                inverse[0:S, :, None].to_broadcast([S, R, W]), ALU.mult
                                                ).then_inc(dve_out, 1)
                        dve.wait_ge(dve_out, b + 1)
                        nc.vector.tensor_tensor(out, out, o_second[:, :, :], ALU.add).then_inc(o_taken, 1)
                    else:
                        out = out.rearrange("p o (r s w) -> p (o r) s w", s=2, w=HD)
                        nc.vector.tensor_tensor(out[:, :, 0, :], o_psum[0:S, :, 0:HD],
                                                inverse[0:S, :, None].to_broadcast([S, R, HD]), ALU.mult)
                        nc.vector.tensor_tensor(out[:, :, 1, :], o_psum[S:P, :, HD:2 * HD],
                                                inverse[S:P, :, None].to_broadcast([S, R, HD]), ALU.mult
                                                ).then_inc(o_taken, 1)

        add_projected(env, o_rows, w_o, 0.8 if lambdas else 1.0)


def rank_of(env, chain, values, ties, rank, scratch, shape):
    nc = env.nc
    rows, n = shape
    full = [P, rows, n, n]
    left = values[:, :, None, :].to_broadcast(full)
    own = values[:, :, :, None].to_broadcast(full)
    greater, equal = scratch
    chain(nc.vector.tensor_tensor(greater, left, own, ALU.is_gt))
    chain(nc.vector.tensor_tensor(equal, left, own, ALU.is_equal))
    chain(nc.vector.tensor_tensor(equal, equal, ties[:, None, :, :].to_broadcast(full), ALU.mult))
    chain(nc.vector.tensor_tensor(greater, greater, equal, ALU.add))
    chain(nc.vector.tensor_reduce(rank, greater, AX.X, ALU.add))


def route(env, kind, experts, weights, gate, add, steps):
    nc = env.nc
    filled, loaded, chain_s = env.sem("logits_filled"), env.sem("gate_loaded"), env.sem("route_chain")
    scored, exp_ready = env.sem("scores_ready"), env.sem("exp_ready")
    n_all = weights.shape[2]
    with ExitStack() as ctx:
        def sb(name, shape):
            return env.sbuf(name, shape, ctx=ctx)

        w = sb("router_w", [P, DC, experts])
        ties = sb("ties", [P, experts, experts])
        ties4 = sb("ties4", [P, 4, 4])
        bias = sb("router_bias", [P, experts])
        score = sb("score", [P, NT, experts])
        prob = sb("prob", [P, NT, experts])
        rank = sb("rank", [P, NT, experts])
        big = [sb(f"pairs{i}", [P, NT * experts * experts]) for i in range(2)]
        row = sb("row", [P, NT * 4])
        group_rank = sb("group_rank", [P, NT * 4])
        total = sb("total", [P, NT])
        loads = [(w[:, :, :], env.dram[gate]), (ties[:, :, :], env.dram[f"ties_{experts}"]),
                 (ties4[:, :, :], env.dram["ties_4"])]
        if add:
            loads.append((bias[:, :], env.dram[add].partition_broadcast(P)))
        logits = env.psum[:, 0, 0:NT * experts].rearrange("p (t e) -> p t e", t=NT)

        def pairs(rows, n):
            return [t[:, 0:rows * n * n].rearrange("p (r a b) -> p r a b", r=rows, a=n) for t in big]

        def wide(v):
            return v[:, :, None].to_broadcast([P, NT, experts])

        bias_all = bias[:, None, :].to_broadcast([P, NT, experts])
        with nc.Block() as block:

            @block.sync
            def _(sp):
                for dst, src in loads:
                    sp.dma_start(dst, src).then_inc(loaded, 16)

            @block.tensor
            def _(pe):
                pe.wait_ge(loaded, 16 * len(loads))
                for t in range(NT):
                    for k in range(DC):
                        mm = nc.tensor.matmul(logits[:, t, :], env.xt[:, k, t * P:(t + 1) * P], w[:, k, :],
                                              start=(k == 0), stop=(k == DC - 1))
                mm.then_inc(filled, 1)

            @block.scalar
            def _(act):
                if kind == "groups":
                    act.wait_ge(filled, 1)
                    nc.scalar.activation(score[:, :, :], logits, ACT.Sigmoid).then_inc(exp_ready, 1)
                else:
                    act.wait_ge(scored, 1)
                    nc.scalar.activation(prob[:, :, :], prob[:, :, :], ACT.Exp).then_inc(exp_ready, 1)

            @block.vector
            def _(dve):
                chain = Chain(dve, chain_s)
                dve.wait_ge(loaded, 16 * len(loads))
                if n_all > experts:
                    nc.vector.memset(weights[:, :, experts:n_all], 1.0)
                chosen = weights[:, :, 0:experts]
                if kind == "groups":
                    dve.wait_ge(exp_ready, 1)
                    chain(nc.vector.tensor_tensor(score[:, :, :], score[:, :, :], bias_all, ALU.add))
                    quads = score[:, :, :].rearrange("p t (g j) -> p (t g) j", j=4)
                    rank4 = rank[:, :, :].rearrange("p t (g j) -> p (t g) j", j=4)
                    prob4 = prob[:, :, :].rearrange("p t (g j) -> p (t g) j", j=4)
                    rank_of(env, chain, quads, ties4, rank4, pairs(NT * 4, 4), (NT * 4, 4))
                    chain(nc.vector.scalar_tensor_tensor(prob4, rank4, 2.0, quads, ALU.is_lt, ALU.mult))
                    chain(nc.vector.tensor_reduce(row[:, :], prob4, AX.X, ALU.add))
                    sums = row[:, :].rearrange("p (t g) -> p t g", t=NT)
                    ranks = group_rank[:, :].rearrange("p (t g) -> p t g", t=NT)
                    rank_of(env, chain, sums, ties4, ranks, pairs(NT, 4), (NT, 4))
                    chain(nc.vector.tensor_scalar(group_rank[:, :], group_rank[:, :], 2.0, None, ALU.is_lt))
                    chain(nc.vector.tensor_tensor(quads, quads, group_rank[:, :, None].to_broadcast([P, NT * 4, 4]),
                                                  ALU.mult))
                    best, values = 4.0, score
                else:
                    dve.wait_ge(filled, 1)
                    if add:
                        chain(nc.vector.tensor_tensor(score[:, :, :], logits, bias_all, ALU.add))
                    else:
                        chain(nc.vector.tensor_copy(score[:, :, :], logits))
                    chain(nc.vector.tensor_reduce(total[:, :], score[:, :, :], AX.X, ALU.max))
                    nc.vector.tensor_tensor(prob[:, :, :], score[:, :, :], wide(total),
                                            ALU.subtract).then_inc(scored, 1)
                    dve.wait_ge(exp_ready, 1)
                    best, values = 2.0, prob
                    if kind == "probs":
                        chain(nc.vector.tensor_reduce(total[:, :], prob[:, :, :], AX.X, ALU.add))
                        chain(nc.vector.reciprocal(total[:, :], total[:, :]))
                        chain(nc.vector.tensor_tensor(prob[:, :, :], prob[:, :, :], wide(total), ALU.mult))
                ranked = prob if kind == "probs" else score
                rank_of(env, chain, ranked[:, :, :], ties, rank[:, :, :], pairs(NT, experts), (NT, experts))
                chain(nc.vector.scalar_tensor_tensor(chosen, rank[:, :, :], best, values[:, :, :], ALU.is_lt, ALU.mult))
                chain(nc.vector.tensor_reduce(total[:, :], chosen, AX.X, ALU.add))
                tiny = {"groups": 1e-20, "probs": 1e-9, "logits": 0.0}[kind]
                chain(nc.vector.tensor_scalar(total[:, :], total[:, :], tiny, None, ALU.add))
                chain(nc.vector.reciprocal(total[:, :], total[:, :]))
                if kind == "groups":
                    chain(nc.vector.tensor_scalar(total[:, :], total[:, :], 2.5, None, ALU.mult))
                chain(nc.vector.tensor_tensor(chosen, chosen, wide(total), ALU.mult))


def expert_ffn(env, kind, routed, n_all, group, chunks, func, gate, add, up_a, up_b, down, bias_up, bias_down):
    nc = env.nc
    steps = n_all // group
    U = 2 * chunks
    DN = NT * group
    per = chunks // group
    gated = up_b is not None
    n_bias = (1 + gated) if bias_up else 0
    w1_loaded, w2_loaded, up_filled, act_ready = (env.sem(n) for n in ("up_loaded", "down_loaded", "up_filled",
                                                                      "act_ready"))
    h_ready, down_filled, down_free, column_s = (env.sem(n) for n in ("h_ready", "down_filled", "down_free", "column"))
    ones_ready = env.sem("ones_ready")
    with ExitStack() as ctx:
        def sb(name, shape):
            return env.sbuf(name, shape, ctx=ctx)

        combine = sb("combine", [P, NT, n_all])
        route(env, kind, routed, combine, gate, add, steps)
        w_a = sb("w_a", [P, DC, chunks * P])
        w_b = sb("w_b", [P, DC, chunks * P]) if gated else None
        w_2 = sb("w_2", [P, chunks, D])
        b_up = sb("b_up", [P, 2, chunks])
        b_down = sb("b_down", [1, D])
        ones = sb("ones", [1, P])
        hidden = sb("hidden", [P, chunks, T])
        column = sb("column", [P, NT, group])

        def up_loads(e):
            one = bass.ds(e, 1)
            out = [(w_a[:, :, :], env.dram[up_a][one].rearrange("o p k n -> p (o k) n"))]
            if gated:
                out.append((w_b[:, :, :], env.dram[up_b][one].rearrange("o p k n -> p (o k) n")))
            for i in range(n_bias):
                out.append((b_up[:, i, :], env.dram[bias_up[i]][one].rearrange("o p n -> p (o n)")))
            return out

        def down_loads(e):
            one = bass.ds(e, 1)
            out = [(w_2[:, :, :], env.dram[down][one].rearrange("o p k n -> p (o k) n"))]
            if bias_down:
                out.append((b_down[:, :], env.dram[bias_down][one, :]))
            return out

        n_up, n_down = 1 + gated + n_bias, 1 + bool(bias_down)

        with nc.Block() as block:

            @block.sync
            def _(sp):
                for dst, src in up_loads(0):
                    sp.dma_start(dst, src).then_inc(w1_loaded, 16)
                for dst, src in down_loads(0):
                    sp.dma_start(dst, src).then_inc(w2_loaded, 16)
                with sp.Fori(0, steps - 1) as e:
                    sp.wait_ge(h_ready, e * U + U)
                    for dst, src in up_loads(e + 1):
                        sp.dma_start(dst, src).then_inc(w1_loaded, 16)
                    sp.wait_ge(down_filled, e * DN + DN)
                    for dst, src in down_loads(e + 1):
                        sp.dma_start(dst, src).then_inc(w2_loaded, 16)

            @block.tensor
            def _(pe):
                pe.wait_ge(ones_ready, 1)
                with pe.Fori(0, steps) as e:
                    pe.wait_ge(w1_loaded, 16 * n_up * e + 16 * n_up)
                    for f in range(chunks):
                        for half in range(2):
                            u = 2 * f + half
                            depth = 2 if gated else 4
                            pe.wait_ge(h_ready, e * U + max(u - depth + 1, 0))
                            for i, w in enumerate((w_a, w_b) if gated else (w_a,)):
                                bank = 2 * (u % 2) + i if gated else u % 4
                                for k in range(DC):
                                    mm = nc.tensor.matmul(env.bank(bank), w[:, k, f * P:(f + 1) * P],
                                                          env.xt[:, k, half * HALF:(half + 1) * HALF],
                                                          start=(k == 0), stop=(k == DC - 1))
                            mm.then_inc(up_filled, 1)
                    pe.wait_ge(w2_loaded, 16 * n_down * e + 16 * n_down)
                    for g in range(group):
                        for t in range(NT):
                            d = NT * g + t
                            last = U if group == 1 else 2 * g + t // 4 + 1
                            pe.wait_ge(h_ready, e * U + last)
                            pe.wait_ge(down_free, e * DN + max(d - 3, 0))
                            out = env.psum[:, 4 + d % 4, 0:D]
                            for k in range(per):
                                mm = nc.tensor.matmul(out, hidden[:, g * per + k, t * P:(t + 1) * P],
                                                      w_2[:, g * per + k, :],
                                                      start=(k == 0), stop=(k == per - 1 and not bias_down))
                            if bias_down:
                                mm = nc.tensor.matmul(out, ones[:, :], b_down[:, :], start=False, stop=True)
                            mm.then_inc(down_filled, 1)

            @block.scalar
            def _(act):
                with act.Fori(0, steps) as e:
                    if n_bias:
                        act.wait_ge(w1_loaded, 16 * n_up * e + 16 * n_up)
                    for f in range(chunks):
                        for half in range(2):
                            u = 2 * f + half
                            act.wait_ge(up_filled, e * U + u + 1)
                            bank = 2 * (u % 2) if gated else u % 4
                            nc.scalar.activation(hidden[:, f, half * HALF:(half + 1) * HALF], env.bank(bank), func,
                                                 bias=b_up[:, 0, f:f + 1] if n_bias else 0.0
                                                 ).then_inc(act_ready if gated else h_ready, 1)

            @block.vector
            def _(dve):
                nc.vector.memset(ones[:, :], 1.0).then_inc(ones_ready, 1)
                with dve.Fori(0, steps) as e:
                    if gated:
                        for f in range(chunks):
                            for half in range(2):
                                u = 2 * f + half
                                here = hidden[:, f, half * HALF:(half + 1) * HALF]
                                dve.wait_ge(act_ready, e * U + u + 1)
                                if n_bias:
                                    nc.vector.scalar_tensor_tensor(here, env.bank(2 * (u % 2) + 1),
                                                                   b_up[:, 1, f:f + 1], here,
                                                                   ALU.add, ALU.mult).then_inc(h_ready, 1)
                                else:
                                    nc.vector.tensor_tensor(here, env.bank(2 * (u % 2) + 1), here,
                                                            ALU.mult).then_inc(h_ready, 1)
                    dve.wait_ge(down_free, e * DN)
                    nc.vector.tensor_copy(column[:, :, :], combine[:, :, bass.ds(e * group, group)]
                                          ).then_inc(column_s, 1)
                    dve.wait_ge(column_s, e + 1)
                    for g in range(group):
                        dve.wait_ge(down_free, e * DN + NT * g)
                        for t in range(NT):
                            d = NT * g + t
                            dve.wait_ge(down_filled, e * DN + d + 1)
                            nc.vector.scalar_tensor_tensor(env.x[:, t, :], env.psum[:, 4 + d % 4, 0:D],
                                                           column[:, t, g:g + 1], env.x[:, t, :],
                                                           ALU.mult, ALU.add).then_inc(down_free, 1)


def l0_ffn(env):
    normalise(env, env.x)
    expert_ffn(env, "groups", 16, 18, 6, 6, ACT.Silu, "l0f_router", "l0f_bias", "l0f_gate", "l0f_up", "l0f_down",
               None, None)


def l2_ffn(env):
    normalise(env, env.x)
    expert_ffn(env, "probs", 8, 8, 1, 8, ACT.Gelu, "l2f_router", None, "l2f_w1", None, "l2f_w2", ["l2f_b1"], "l2f_b2")


def l3_ffn(env):
    normalise(env, env.x, transpose=False)
    normalise(env, env.xn, gain="l3f_ln_w", rms=True, eps=float(np.finfo(np.float32).eps))
    expert_ffn(env, "logits", 8, 8, 1, 8, ACT.Silu, "l3f_router", "l3f_bias", "l3f_w1a", "l3f_w1b", "l3f_w2",
               ["l3f_b1a", "l3f_b1b"], "l3f_b2")


def l1_attn(env):
    nc = env.nc
    normalise(env, env.x)
    LAT = 64
    R = HEADS // 2
    filled, taken_a, taken_d, loaded = (env.sem(n) for n in ("filled", "taken_act", "taken_dve", "loaded"))
    lat_filled, lat_taken = env.sem("latent_filled"), env.sem("latent_taken")
    up_filled, up_a, up_d = env.sem("up_filled"), env.sem("up_taken_act"), env.sem("up_taken_dve")
    qd_ready, scored, decayed, shifted = (env.sem(n) for n in ("qd_ready", "scored", "decayed", "shifted"))
    turn_start = env.sem("turn_start")
    exp_done, turned, turned_taken, pv_done, o_taken, chain_s = (
        env.sem(n) for n in ("exp_done", "turned", "turned_taken", "pv_done", "o_taken", "chain"))
    with ExitStack() as ctx:
        def sb(name, shape, dtype=F32):
            return env.sbuf(name, shape, dtype, ctx)

        w_q, w_k, w_v, w_o = (sb(n, [P, DC, D]) for n in ("w_q", "w_k", "w_v", "w_o"))
        w_down = sb("w_down", [P, DC, LAT])
        w_up_k, w_up_v = sb("w_up_k", [LAT, D]), sb("w_up_v", [LAT, D])
        head_mask, decay = sb("head_mask", [P, 8]), sb("decay", [P, S])
        q_t, kv_t, k_t = (sb(n, [P, DC, T]) for n in ("q_t", "kv_t", "k_t"))
        lat_t = sb("lat_t", [LAT, T])
        v = sb("v", [S, B, D])
        q_diag = sb("q_diag", [P, 2, DC, 8, S])
        sc, probs = sb("sc", [P, 2, R, S]), sb("probs", [P, 2, R, S])
        probs_t = sb("probs_t", [S, 2, R, P])
        peak, total, inverse = (sb(n, [P, 2, R]) for n in ("peak", "total", "inverse"))
        o_rows = sb("o_rows", [S, B, D])
        loads = [(w_q[:, :, :], "l1a_wq"), (w_k[:, :, :], "l1a_wk"), (w_v[:, :, :], "l1a_wv"),
                 (w_down[:, :, :], "l1a_down"), (w_up_k[:, :], "l1a_up_k"), (w_up_v[:, :], "l1a_up_v"),
                 (head_mask[:, :], "pair_mask"), (decay[:, :], "decay"), (w_o[:, :, :], "l1a_wo")]

        with nc.Block() as block:

            @block.sync
            def _(sp):
                for dst, src in loads:
                    sp.dma_start(dst, env.dram[src]).then_inc(loaded, 16)

            @block.tensor
            def _(pe):
                pe.wait_ge(loaded, 16 * len(loads))
                for i, ws in enumerate(((w_q,), (w_k, w_v))):
                    for m in range(DC):
                        for h in range(2):
                            parts = [(w, k) for w in ws for k in range(DC)]
                            for n, (w, k) in enumerate(parts):
                                mm = nc.tensor.matmul(env.bank(4 * i + 2 * m + h), w[:, k, m * P:(m + 1) * P],
                                                      env.xt[:, k, h * HALF:(h + 1) * HALF],
                                                      start=(n == 0), stop=(n == len(parts) - 1))
                            mm.then_inc(filled, 1)
                pe.wait_ge(taken_d, 4)
                for h in range(2):
                    pe.wait_ge(taken_a, h + 1)
                    for k in range(DC):
                        mm = nc.tensor.matmul(env.psum[0:LAT, h, :], w_down[:, k, :], kv_t[:, k, h * HALF:(h + 1) * HALF],
                                              start=(k == 0), stop=(k == DC - 1))
                    mm.then_inc(lat_filled, 1)
                pe.wait_ge(taken_a, 4)
                pe.wait_ge(lat_taken, 2)
                for m in range(DC):
                    for h in range(2):
                        nc.tensor.matmul(env.bank(2 + 2 * m + h), w_up_k[:, m * P:(m + 1) * P],
                                         lat_t[:, h * HALF:(h + 1) * HALF], start=True, stop=True
                                         ).then_inc(up_filled, 1)
                for i in range(B // 2):
                    if i >= 4:
                        pe.wait_ge(up_d, i - 3)
                    for b in (2 * i, 2 * i + 1):
                        mm = nc.tensor.matmul(env.psum[0:S, (6 + i % 4) % 8, (b % 2) * D:(b % 2 + 1) * D],
                                              lat_t[:, b * S:(b + 1) * S], w_up_v[:, :], start=True, stop=True)
                    mm.then_inc(up_filled, 1)

            @block.scalar
            def _(act):
                for n in range(4):
                    act.wait_ge(filled, n + 1)
                    nc.scalar.copy(q_t[:, n // 2, n % 2 * HALF:(n % 2 + 1) * HALF], env.bank(n)).then_inc(taken_a, 1)
                for h in range(2):
                    act.wait_ge(lat_filled, h + 1)
                    nc.scalar.copy(lat_t[:, h * HALF:(h + 1) * HALF], env.psum[0:LAT, h, :]).then_inc(lat_taken, 1)
                for n in range(4):
                    act.wait_ge(up_filled, n + 1)
                    nc.scalar.copy(k_t[:, n // 2, n % 2 * HALF:(n % 2 + 1) * HALF], env.bank(2 + n)).then_inc(up_a, 1)

            @block.vector
            def _(dve):
                for n in range(4):
                    dve.wait_ge(filled, 4 + n + 1)
                    nc.vector.tensor_copy(kv_t[:, n // 2, n % 2 * HALF:(n % 2 + 1) * HALF],
                                          env.bank(4 + n)).then_inc(taken_d, 1)
                for i in range(B // 2):
                    dve.wait_ge(up_filled, 4 + i + 1)
                    nc.vector.tensor_copy(v[:, 2 * i:2 * i + 2, :],
                                          env.psum[0:S, (6 + i % 4) % 8, :].rearrange("p (b d) -> p b d", b=2)
                                          ).then_inc(up_d, 1)

        L = 3
        with nc.Block() as block:

            @block.gpsimd
            def _(pool):
                with pool.Fori(0, B // 2) as i:
                    for e in range(2):
                        pool.wait_ge(scored, 2 * i)
                        for c in range(DC):
                            now = q_t[:, c, bass.ds(i * (2 * S) + e * S, S)]
                            nc.gpsimd.tensor_tensor(q_diag[:, e, c, :, :], now[:, None, :].to_broadcast([P, 8, S]),
                                                    head_mask[:, :, None].to_broadcast([P, 8, S]), ALU.mult
                                                    ).then_inc(qd_ready, 1)

            @block.tensor
            def _(pe):
                with pe.Fori(0, B // 2) as i:
                    for e in range(2):
                        pe.wait_ge(qd_ready, i * 4 + 2 * e + 2)
                        pe.wait_ge(decayed, 2 * i)
                        for r in range(R):
                            pair = slice(2 * (r % 4), 2 * (r % 4) + 2)
                            mm = nc.tensor.matmul(env.psum[:, e, r * S:(r + 1) * S],
                                                  q_diag[:, e, r // 4, pair, :].rearrange("p s q -> p (s q)"),
                                                  k_t[:, r // 4, bass.ds(i * (2 * S) + e * S, S)],
                                                  start=True, stop=True)
                        mm.then_inc(scored, 1)
                    for e in range(2):
                        pe.wait_ge(exp_done, 2 * i + e + 1)
                        pe.wait_ge(turned_taken, 2 * i)
                        pe.sem_inc(turn_start, 1)
                        for r in range(R):
                            mm = nc.tensor.transpose(env.psum[0:S, 2 + 2 * e + r // 4, r % 4 * P:(r % 4 + 1) * P],
                                                     probs[:, e, r, :], env.ident[:, :])
                        mm.then_inc(turned, 1)
                    for e in range(2):
                        pe.wait_ge(turned_taken, 2 * i + e + 1)
                        pe.wait_ge(o_taken, 2 * i)
                        for r in range(R):
                            mm = nc.tensor.matmul(env.psum[:, 6 + e, r * 32:(r + 1) * 32], probs_t[:, e, r, :],
                                                  v[:, bass.ds(2 * i + e, 1), r * 32:(r + 1) * 32].rearrange(
                                                      "p o w -> p (o w)"), start=True, stop=True)
                        mm.then_inc(pv_done, 1)

            @block.scalar
            def _(act):
                with act.Fori(0, B // 2) as i:
                    for e in range(2):
                        act.wait_ge(shifted, 2 * i + e + 1)
                        act.wait_ge(turned, 2 * i)
                        nc.scalar.activation(probs[:, e, :, :], sc[:, e, :, :], ACT.Exp).then_inc(exp_done, 1)
                    for e in range(2):
                        act.wait_ge(turned, 2 * i + e + 1)
                        act.wait_ge(pv_done, 2 * i)
                        nc.scalar.copy(probs_t[:, e, :, :].rearrange("p r n -> p (r n)"),
                                       env.psum[0:S, 2 + 2 * e:4 + 2 * e, :].rearrange("p k n -> p (k n)")
                                       ).then_inc(turned_taken, 1)

            @block.vector
            def _(dve):
                with dve.Fori(0, B // 2) as i:
                    chain = Chain(dve, chain_s, i * (2 * L))
                    full = [P, R, S]
                    for e in range(2):
                        dve.wait_ge(scored, 2 * i + e + 1)
                        dve.wait_ge(exp_done, 2 * i)
                        nc.vector.tensor_tensor(sc[:, e, :, :], env.psum[:, e, :].rearrange("p (r m) -> p r m", r=R),
                                                decay[:, None, :].to_broadcast(full), ALU.mult).then_inc(decayed, 1)
                        dve.wait_ge(decayed, 2 * i + e + 1)
                        chain(nc.vector.tensor_reduce(peak[:, e, :], sc[:, e, :, :], AX.X, ALU.max))
                        nc.vector.tensor_tensor(sc[:, e, :, :], sc[:, e, :, :],
                                                peak[:, e, :, None].to_broadcast(full), ALU.subtract
                                                ).then_inc(shifted, 1)
                    for e in range(2):
                        dve.wait_ge(exp_done, 2 * i + e + 1)
                        dve.wait_ge(o_taken, 2 * i)
                        chain(nc.vector.tensor_reduce(total[:, e, :], probs[:, e, :, :], AX.X, ALU.add))
                        chain(nc.vector.reciprocal(inverse[:, e, :], total[:, e, :]))
                    for e in range(2):
                        dve.wait_ge(pv_done, 2 * i + e + 1)
                        out = o_rows[:, bass.ds(2 * i + e, 1), :].rearrange("p o (r s w) -> p (o r) s w", s=2, w=HD)
                        o_psum = env.psum[:, 6 + e, 0:D].rearrange("p (r w) -> p r w", r=R)
                        nc.vector.tensor_tensor(out[:, :, 0, :], o_psum[0:S, :, 0:HD],
                                                inverse[0:S, e, :, None].to_broadcast([S, R, HD]), ALU.mult)
                        nc.vector.tensor_tensor(out[:, :, 1, :], o_psum[S:P, :, HD:2 * HD],
                                                inverse[S:P, e, :, None].to_broadcast([S, R, HD]), ALU.mult
                                                ).then_inc(o_taken, 1)

        add_projected(env, o_rows, w_o)


def l2_attn(env):
    nc = env.nc
    normalise(env, env.x, transpose=False)
    base_loaded, loaded = env.sem("base_loaded"), env.sem("loaded")
    b_out_s, filled, u_ready, om_ready = (env.sem(n) for n in ("x_based", "filled", "gates_ready", "rest_ready"))
    summed, squashed, stepped, kept, mixed = (env.sem(n) for n in ("summed", "squashed", "stepped", "kept", "mixed"))
    out_filled, out_free = env.sem("out_filled"), env.sem("out_free")
    with ExitStack() as ctx:
        def sb(name, shape, dtype=F32):
            return env.sbuf(name, shape, dtype, ctx)

        b_out = sb("b_out", [P, D])
        with nc.Block() as block:

            @block.sync
            def _(sp):
                sp.dma_start(b_out[:, :], env.dram["l2a_b_out"].partition_broadcast(P)).then_inc(base_loaded, 16)

            @block.vector
            def _(dve):
                for t in range(NT):
                    nc.vector.tensor_tensor(env.x[:, t, :], env.x[:, t, :], env.xn[:, t, :],
                                            ALU.add).then_inc(b_out_s, 1)
                dve.wait_ge(base_loaded, 16)
                for t in range(NT):
                    dve.wait_ge(b_out_s, t + 1)
                    nc.vector.tensor_tensor(env.x[:, t, :], env.x[:, t, :], b_out[:, :], ALU.add)

        normalise(env, env.xn, gain="l2a_gamma", shift="l2a_beta")

        w_in, w_out = sb("w_in", [P, DC, 2 * D]), sb("w_out", [P, DC, D])
        b_in, a_col = sb("b_in", [P, 4]), sb("a_col", [P, DC])
        u, g, rest, hs = (sb(n, [P, DC, T]) for n in ("u", "g", "rest", "hs"))
        arg, squash, keep, mix = (sb(n, [P, DC, B]) for n in ("arg", "squash", "keep", "mix"))
        loads = [(w_in[:, :, :], "l2a_w_in"), (b_in[:, :], "l2a_b_in"), (a_col[:, :], "l2a_a"),
                 (w_out[:, :, :], "l2a_w_out")]

        def at(x, t):
            return x[:, :, :].rearrange("p c (b s) -> p c b s", s=S)[:, :, :, bass.ds(t, 1)].rearrange(
                "p c b o -> p c (b o)")

        with nc.Block() as block:

            @block.sync
            def _(sp):
                for dst, src in loads:
                    sp.dma_start(dst, env.dram[src]).then_inc(loaded, 16)

            @block.tensor
            def _(pe):
                pe.wait_ge(loaded, 16 * len(loads))
                for m in range(4):
                    for h in range(2):
                        for k in range(DC):
                            mm = nc.tensor.matmul(env.bank(2 * m + h), w_in[:, k, m * P:(m + 1) * P],
                                                  env.xt[:, k, h * HALF:(h + 1) * HALF],
                                                  start=(k == 0), stop=(k == DC - 1))
                        mm.then_inc(filled, 1)
                pe.wait_ge(stepped, S)
                for t in range(NT):
                    if t >= 4:
                        pe.wait_ge(out_free, t - 3)
                    for k in range(DC):
                        mm = nc.tensor.matmul(env.psum[:, t % 4, 0:D], hs[:, k, t * P:(t + 1) * P], w_out[:, k, :],
                                              start=(k == 0), stop=(k == DC - 1))
                    mm.then_inc(out_filled, 1)

            @block.scalar
            def _(act):
                act.wait_ge(loaded, 16 * len(loads))
                for m in range(4):
                    for h in range(2):
                        act.wait_ge(filled, 2 * m + h + 1)
                        dst = (u, g)[m // 2]
                        nc.scalar.activation(dst[:, m % 2, h * HALF:(h + 1) * HALF], env.bank(2 * m + h),
                                             (ACT.Identity, ACT.Sigmoid)[m // 2], bias=b_in[:, m:m + 1]
                                             ).then_inc(u_ready, 1)
                act.wait_ge(u_ready, 8)
                nc.scalar.activation(squash[:, :, :], at(u, 0), ACT.Tanh).then_inc(squashed, 1)
                with act.Fori(1, S) as t:
                    act.wait_ge(summed, 2 * t)
                    nc.scalar.activation(squash[:, :, :], arg[:, :, :], ACT.Tanh).then_inc(squashed, 1)

            @block.vector
            def _(dve):
                dve.wait_ge(u_ready, 8)
                for c in range(DC):
                    nc.vector.tensor_scalar(rest[:, c, :], g[:, c, :], -1.0, 1.0, ALU.mult, ALU.add
                                            ).then_inc(om_ready, 1)
                dve.wait_ge(om_ready, 2)
                dve.wait_ge(squashed, 1)
                nc.vector.tensor_tensor(at(hs, 0), at(rest, 0), squash[:, :, :], ALU.mult).then_inc(stepped, 1)
                with dve.Fori(1, S) as t:
                    dve.wait_ge(stepped, t)
                    for c in range(DC):
                        nc.vector.scalar_tensor_tensor(arg[:, c, :], at(hs, t - 1)[:, c, :], a_col[:, c:c + 1],
                                                       at(u, t)[:, c, :], ALU.mult, ALU.add).then_inc(summed, 1)
                    nc.vector.tensor_tensor(keep[:, :, :], at(g, t), at(hs, t - 1), ALU.mult).then_inc(kept, 1)
                    dve.wait_ge(squashed, t + 1)
                    nc.vector.tensor_tensor(mix[:, :, :], at(rest, t), squash[:, :, :], ALU.mult).then_inc(mixed, 1)
                    dve.wait_ge(mixed, t)
                    dve.wait_ge(kept, t)
                    nc.vector.tensor_tensor(at(hs, t), mix[:, :, :], keep[:, :, :], ALU.add).then_inc(stepped, 1)
                for t in range(NT):
                    dve.wait_ge(out_filled, t + 1)
                    nc.vector.tensor_tensor(env.x[:, t, :], env.x[:, t, :], env.psum[:, t % 4, 0:D],
                                            ALU.add).then_inc(out_free, 1)


def l1_ffn(env):
    nc = env.nc
    normalise(env, env.x, transpose=False)
    MAGIC = 1.5 * 2.0 ** 23
    FF = 4 * D
    FC = FF // P
    loaded, chain_s, w_chain = env.sem("loaded"), env.sem("chain"), env.sem("weight_chain")
    summed, sum_filled, w_ready, x_ready = (env.sem(n) for n in ("summed", "sum_filled", "weights_ready", "x_ready"))
    x_turned, x_taken, up_filled, scaled, conv_s, conved, h_ready, ones_ready = (
        env.sem(n) for n in ("x_turned", "x_taken", "up_filled", "scaled", "conv_step", "conved", "h_ready",
                             "ones_ready"))
    turned, quantised, int_turned, int_taken, out_filled, added, q_chain = (
        env.sem(n) for n in ("turned", "quantised", "int_turned", "int_taken", "out_filled", "added", "quant_chain"))
    with ExitStack() as ctx:
        def sb(name, shape, dtype=F32):
            return env.sbuf(name, shape, dtype, ctx)

        w1, w2 = sb("w1", [P, DC, FF]), sb("w2", [P, FC, D])
        w2_int = sb("w2_int", [P, FC, D], BF16)
        ident_b = sb("ident_bf16", [P, P], BF16)
        ones = sb("ones", [P, P])
        conv_w, conv_b = sb("conv_w", [P, FC, 3]), sb("conv_b", [P, FC])
        w_sum = sb("w_sum", [P, 2])
        w_mean, w_scale = sb("w_mean", [P, 2]), sb("w_scale", [P, 2])
        peak, scale, inv = sb("peak", [P, NT]), sb("scale", [P, NT]), sb("inv", [P, NT])
        hidden = sb("hidden", [P, FC, T])
        conv = sb("conv", [P, 2, HALF])
        h_peak, h_scale, h_inv = sb("h_peak", [P, NT]), sb("h_scale", [P, NT]), sb("h_inv", [P, NT])
        h_round = sb("h_round", [P, 2, FF])
        h_int = sb("h_int", [P, 2, FF], BF16)
        h_int_t = sb("h_int_t", [P, 2, FC, P], BF16)
        loads = [(w1[:, :, :], "l1f_w1"), (w2[:, :, :], "l1f_w2"), (conv_w[:, :, :], "l1f_conv_w"),
                 (conv_b[:, :], "l1f_conv_b")]

        def quantise_scale(chain, peak, scale, inv):
            chain(nc.vector.tensor_scalar(peak, peak, 1e-5, None, ALU.max))
            chain(nc.vector.reciprocal(scale, peak))
            chain(nc.vector.tensor_scalar(scale, scale, 127.0, None, ALU.mult))
            chain(nc.vector.tensor_scalar(inv, peak, 1.0 / 127.0, None, ALU.mult))

        with nc.Block() as block:

            @block.sync
            def _(sp):
                for dst, src in loads:
                    sp.dma_start(dst, env.dram[src]).then_inc(loaded, 16)

            @block.gpsimd
            def _(pool):
                nc.gpsimd.memset(ones[:, :], 1.0).then_inc(ones_ready, 1)
                nc.gpsimd.tensor_copy(ident_b[:, :], env.ident[:, :]).then_inc(ones_ready, 1)

            @block.vector
            def _(dve):
                chain = Chain(dve, chain_s)
                chain(nc.vector.tensor_reduce(peak[:, :], env.xn[:, :, :], AX.X, ALU.max, apply_absolute_value=True))
                quantise_scale(chain, peak[:, :], scale[:, :], inv[:, :])
                for step in range(3):
                    for t in range(NT):
                        row = env.xn[:, t, :]
                        if step == 0:
                            ins = nc.vector.tensor_scalar(row, row, scale[:, t:t + 1], MAGIC, ALU.mult, ALU.add)
                        elif step == 1:
                            ins = nc.vector.tensor_scalar(row, row, MAGIC + 127.0, MAGIC - 128.0, ALU.min, ALU.max)
                        else:
                            ins = nc.vector.tensor_scalar(row, row, MAGIC, inv[:, t:t + 1], ALU.subtract, ALU.mult)
                        ins.then_inc(chain_s if step < 2 else x_ready, 1)
                    if step < 2:
                        chain.n += NT
                        dve.wait_ge(chain_s, chain.n)
                dve.wait_ge(loaded, 16 * len(loads))
                for i, w in enumerate((w1, w2)):
                    nc.vector.tensor_reduce(w_sum[:, i:i + 1], w[:, :, :].rearrange("p a b -> p (a b)"), AX.X, ALU.add,
                                            apply_absolute_value=True).then_inc(summed, 1)
                dve.wait_ge(sum_filled, 1)
                chain(nc.vector.tensor_scalar(w_mean[:, :], env.psum[:, 7, 0:2], 1.0 / (D * FF), 1e-5, ALU.mult, ALU.max))
                chain(nc.vector.reciprocal(w_scale[:, :], w_mean[:, :]))
                for i, (w, out) in enumerate(((w1[:, :, :], w1[:, :, :]), (w2[:, :, :], w2_int[:, :, :]))):
                    chain(nc.vector.tensor_scalar(w, w, w_scale[:, i:i + 1], MAGIC, ALU.mult, ALU.add))
                    chain(nc.vector.tensor_scalar(w, w, MAGIC, 1.0, ALU.subtract, ALU.min))
                    nc.vector.tensor_scalar(out, w, -1.0, None, ALU.max).then_inc(w_ready, 1)
                nc.vector.tensor_scalar(conv_w[:, :, :], conv_w[:, :, :], w_mean[:, 0:1], None, ALU.mult
                                        ).then_inc(w_ready, 1)

            @block.tensor
            def _(pe):
                pe.wait_ge(summed, 2)
                pe.wait_ge(ones_ready, 2)
                nc.tensor.matmul(env.psum[:, 7, 0:2], ones[:, :], w_sum[:, :], start=True, stop=True
                                 ).then_inc(sum_filled, 1)
                for t in range(NT):
                    pe.wait_ge(x_ready, t + 1)
                    if t >= 4:
                        pe.wait_ge(x_taken, t - 3)
                    for c in range(DC):
                        mm = nc.tensor.transpose(env.psum[:, t % 4, c * P:(c + 1) * P], env.xn[:, t, c * P:(c + 1) * P],
                                                 env.ident[:, :])
                    mm.then_inc(x_turned, 1)

            @block.scalar
            def _(act):
                for t in range(NT):
                    act.wait_ge(x_turned, t + 1)
                    nc.scalar.copy(env.xt[:, :, t * P:(t + 1) * P],
                                   env.psum[:, t % 4, 0:D].rearrange("p (c n) -> p c n", c=DC)).then_inc(x_taken, 1)

        with nc.Block() as block:

            @block.tensor
            def _(pe):
                for n in range(2 * FC):
                    f, h = n // 2, n % 2
                    if n >= 4:
                        pe.wait_ge(conved, n - 3)
                    for k in range(DC):
                        mm = nc.tensor.matmul(env.bank(n % 4), w1[:, k, f * P:(f + 1) * P],
                                              env.xt[:, k, h * HALF:(h + 1) * HALF], start=(k == 0), stop=(k == DC - 1))
                    mm.then_inc(up_filled, 1)

            @block.vector
            def _(dve):
                chain = Chain(dve, conv_s)
                for n in range(2 * FC):
                    f = n // 2
                    rows = env.bank(n % 4).rearrange("p (b s) -> p b s", s=S)
                    out = conv[:, n % 2, :].rearrange("p (b s) -> p b s", s=S)
                    dve.wait_ge(up_filled, n + 1)
                    if n >= 2:
                        dve.wait_ge(h_ready, n - 1)
                    chain(nc.vector.tensor_scalar(out, rows, conv_w[:, f, 1:2], conv_b[:, f:f + 1], ALU.mult, ALU.add))
                    chain(nc.vector.scalar_tensor_tensor(out[:, :, 1:S], rows[:, :, 0:S - 1], conv_w[:, f, 0:1],
                                                         out[:, :, 1:S], ALU.mult, ALU.add))
                    nc.vector.scalar_tensor_tensor(out[:, :, 0:S - 1], rows[:, :, 1:S], conv_w[:, f, 2:3],
                                                   out[:, :, 0:S - 1], ALU.mult, ALU.add).then_inc(conved, 1)

            @block.scalar
            def _(act):
                for n in range(2 * FC):
                    act.wait_ge(conved, n + 1)
                    nc.scalar.activation(hidden[:, n // 2, n % 2 * HALF:(n % 2 + 1) * HALF], conv[:, n % 2, :],
                                         ACT.Silu).then_inc(h_ready, 1)

        with nc.Block() as block:

            @block.tensor
            def _(pe):
                def forth(t):
                    if t >= 2:
                        pe.wait_ge(quantised, 3 * (t - 1) - 2)
                    for f in range(FC):
                        mm = nc.tensor.transpose(env.psum[:, 2 * (t % 2) + f // 4, f % 4 * P:(f % 4 + 1) * P],
                                                 hidden[:, f, t * P:(t + 1) * P], env.ident[:, :])
                    mm.then_inc(turned, 1)

                forth(0)
                for t in range(NT):
                    if t + 1 < NT:
                        forth(t + 1)
                    pe.wait_ge(quantised, 3 * t + 3)
                    if t >= 2:
                        pe.wait_ge(int_taken, t - 1)
                    ints = env.psum[:, 4 + t % 2, :].bitcast(BF16)
                    for f in range(FC):
                        mm = nc.tensor.transpose(ints[:, f * P:(f + 1) * P], h_int[:, t % 2, f * P:(f + 1) * P],
                                                 ident_b[:, :])
                    mm.then_inc(int_turned, 1)
                    pe.wait_ge(int_taken, t + 1)
                    if t >= 2:
                        pe.wait_ge(added, t - 1)
                    for k in range(FC):
                        mm = nc.tensor.matmul(env.psum[:, 6 + t % 2, 0:D], h_int_t[:, t % 2, k, :], w2_int[:, k, :],
                                              start=(k == 0), stop=(k == FC - 1))
                    mm.then_inc(out_filled, 1)

            @block.scalar
            def _(act):
                for t in range(NT):
                    act.wait_ge(int_turned, t + 1)
                    if t >= 2:
                        act.wait_ge(out_filled, t - 1)
                    nc.scalar.copy(h_int_t[:, t % 2, :, :].rearrange("p f n -> p (f n)"),
                                   env.psum[:, 4 + t % 2, :].bitcast(BF16)).then_inc(int_taken, 1)

            @block.vector
            def _(dve):
                chain = Chain(dve, q_chain)

                def add(t):
                    dve.wait_ge(out_filled, t + 1)
                    nc.vector.scalar_tensor_tensor(env.x[:, t, :], env.psum[:, 6 + t % 2, 0:D], h_inv[:, t:t + 1],
                                                   env.x[:, t, :], ALU.mult, ALU.add).then_inc(added, 1)

                for t in range(NT):
                    one = slice(t, t + 1)
                    rows = env.psum[:, 2 * (t % 2):2 * (t % 2) + 2, :].rearrange("p k n -> p (k n)")
                    dve.wait_ge(turned, t + 1)
                    chain(nc.vector.tensor_reduce(h_peak[:, one], rows, AX.X, ALU.max, apply_absolute_value=True))
                    quantise_scale(chain, h_peak[:, one], h_scale[:, one], h_inv[:, one])
                    chain(nc.vector.tensor_scalar(h_inv[:, one], h_inv[:, one], w_mean[:, 1:2], None, ALU.mult))
                    if t >= 2:
                        dve.wait_ge(int_turned, t - 1)
                    buf = h_round[:, t % 2, :]
                    nc.vector.tensor_scalar(buf, rows, h_scale[:, one], MAGIC, ALU.mult, ALU.add).then_inc(quantised, 1)
                    dve.wait_ge(quantised, 3 * t + 1)
                    nc.vector.tensor_scalar(buf, buf, MAGIC + 127.0, MAGIC - 128.0, ALU.min, ALU.max
                                            ).then_inc(quantised, 1)
                    dve.wait_ge(quantised, 3 * t + 2)
                    nc.vector.tensor_scalar(h_int[:, t % 2, :], buf, MAGIC, None, ALU.subtract).then_inc(quantised, 1)
                    if t >= 1:
                        add(t - 1)
                add(NT - 1)


def l3_attn(env):
    nc = env.nc
    normalise(env, env.x)
    DI = 2 * D
    IC = DI // P
    N = 16
    TAPS = 4
    B_AT, C_AT, XD = 32, 64, 80
    sem = env.sem
    with ExitStack() as ctx:
        def sb(name, shape, dtype=F32, into=ctx):
            return env.sbuf(name, shape, dtype, into)

        u, gate, delta, du, y = (sb(n, [P, IC, T]) for n in ("u", "gate", "delta", "du", "y"))
        neg_a, neg_a_t = sb("neg_a", [P, IC, N]), sb("neg_a_t", [XD, DI])
        d_col = sb("d_col", [P, IC])
        x_dbl = sb("x_dbl", [XD, T])
        small_loaded, a_ready = sem("small_loaded"), sem("a_ready")

        with ExitStack() as inner:
            w_in = sb("w_in", [P, DC, 2 * DI], into=inner)
            conv_w, conv_b = sb("conv_w", [P, IC, TAPS], into=inner), sb("conv_b", [P, IC], into=inner)
            w_x = sb("w_x", [P, IC, XD], into=inner)
            conv = sb("conv", [P, 2, HALF], into=inner)
            w_dt, b_dt = sb("w_dt", [N, DI], into=inner), sb("b_dt", [P, IC], into=inner)
            loaded, filled, conv_s, conved, u_ready, gated = (
                sem(n) for n in ("loaded", "filled", "conv_chain", "conved", "u_ready", "gated"))
            dbl_filled, dbl_ready = sem("dbl_filled"), sem("dbl_ready")
            loads = [(w_in[:, :, :], "l3a_w_in"), (conv_w[:, :, :], "l3a_conv_w"), (conv_b[:, :], "l3a_conv_b"),
                     (w_x[:, :, :], "l3a_w_x"), (w_dt[:, :], "l3a_w_dt"), (b_dt[:, :], "l3a_b_dt"),
                     (d_col[:, :], "l3a_d"), (neg_a[:, :, :], "l3a_a"), (neg_a_t[C_AT:C_AT + N, :], "l3a_a_t")]
            with nc.Block() as block:

                @block.sync
                def _(sp):
                    for dst, src in loads:
                        sp.dma_start(dst, env.dram[src]).then_inc(loaded, 16)

                @block.tensor
                def _(pe):
                    pe.wait_ge(loaded, 16 * len(loads))
                    for n in range(2 * IC):
                        for part in range(2):
                            if n >= 4:
                                pe.wait_ge((conved, gated)[part], n - 3)
                            m, h = IC * part + n // 2, n % 2
                            for k in range(DC):
                                mm = nc.tensor.matmul(env.bank(4 * part + n % 4), w_in[:, k, m * P:(m + 1) * P],
                                                      env.xt[:, k, h * HALF:(h + 1) * HALF],
                                                      start=(k == 0), stop=(k == DC - 1))
                            mm.then_inc(filled, 1)
                    pe.wait_ge(gated, 2 * IC)
                    pe.wait_ge(u_ready, 2 * IC)
                    for h in range(2):
                        for k in range(IC):
                            mm = nc.tensor.matmul(env.psum[0:XD, 4 + h, :], w_x[:, k, :], u[:, k, h * HALF:(h + 1) * HALF],
                                                  start=(k == 0), stop=(k == IC - 1))
                        mm.then_inc(dbl_filled, 1)

                @block.vector
                def _(dve):
                    chain = Chain(dve, conv_s)
                    dve.wait_ge(loaded, 16 * len(loads))
                    for n in range(2 * IC):
                        f = n // 2
                        rows = env.bank(n % 4).rearrange("p (b s) -> p b s", s=S)
                        out = conv[:, n % 2, :].rearrange("p (b s) -> p b s", s=S)
                        dve.wait_ge(filled, 2 * n + 1)
                        if n >= 2:
                            dve.wait_ge(u_ready, n - 1)
                        chain(nc.vector.tensor_scalar(out, rows, conv_w[:, f, TAPS - 1:TAPS], conv_b[:, f:f + 1],
                                                      ALU.mult, ALU.add))
                        for back in range(1, TAPS):
                            ins = nc.vector.scalar_tensor_tensor(
                                out[:, :, back:S], rows[:, :, 0:S - back], conv_w[:, f, TAPS - 1 - back:TAPS - back],
                                out[:, :, back:S], ALU.mult, ALU.add)
                            if back < TAPS - 1:
                                chain(ins)
                        ins.then_inc(conved, 1)

                @block.scalar
                def _(act):
                    for n in range(2 * IC):
                        here = slice(n % 2 * HALF, (n % 2 + 1) * HALF)
                        act.wait_ge(filled, 2 * n + 2)
                        nc.scalar.activation(gate[:, n // 2, here], env.bank(4 + n % 4), ACT.Silu).then_inc(gated, 1)
                        act.wait_ge(conved, n + 1)
                        nc.scalar.activation(u[:, n // 2, here], conv[:, n % 2, :], ACT.Silu).then_inc(u_ready, 1)
                    for h in range(2):
                        act.wait_ge(dbl_filled, h + 1)
                        nc.scalar.copy(x_dbl[:, h * HALF:(h + 1) * HALF], env.psum[0:XD, 4 + h, :]
                                       ).then_inc(dbl_ready, 1)

            dt_filled, v_ready, abs_ready, e_ready, ln_ready, delta_ready, y_zero = (
                sem(n) for n in ("dt_filled", "v_ready", "abs_ready", "e_ready", "ln_ready", "delta_ready", "y_zero"))
            with nc.Block() as block:

                @block.tensor
                def _(pe):
                    for n in range(2 * IC):
                        nc.tensor.matmul(env.bank(n), w_dt[:, n // 2 * P:(n // 2 + 1) * P],
                                         x_dbl[0:N, n % 2 * HALF:(n % 2 + 1) * HALF], start=True, stop=True
                                         ).then_inc(dt_filled, 1)

                @block.scalar
                def _(act):
                    nc.scalar.activation(neg_a[:, :, :], neg_a[:, :, :], ACT.Exp).then_inc(a_ready, 1)
                    rows = slice(C_AT, C_AT + N)
                    nc.scalar.activation(neg_a_t[rows, :], neg_a_t[rows, :], ACT.Exp).then_inc(a_ready, 1)
                    for n in range(2 * IC):
                        here = slice(n % 2 * HALF, (n % 2 + 1) * HALF)
                        act.wait_ge(dt_filled, n + 1)
                        nc.scalar.activation(delta[:, n // 2, here], env.bank(n), ACT.Identity,
                                             bias=b_dt[:, n // 2:n // 2 + 1]).then_inc(v_ready, 1)
                        nc.scalar.activation(du[:, n // 2, here], env.bank(n), ACT.Abs,
                                             bias=b_dt[:, n // 2:n // 2 + 1]).then_inc(abs_ready, 1)
                    act.wait_ge(abs_ready, 2 * IC)
                    for c in range(IC):
                        nc.scalar.activation(du[:, c, :], du[:, c, :], ACT.Exp, scale=-1.0).then_inc(e_ready, 1)
                    act.wait_ge(e_ready, IC)
                    for c in range(IC):
                        nc.scalar.activation(du[:, c, :], du[:, c, :], ACT.Ln, bias=1.0).then_inc(ln_ready, 1)

                @block.vector
                def _(dve):
                    dve.wait_ge(a_ready, 2)
                    nc.vector.tensor_scalar(neg_a[:, :, :], neg_a[:, :, :], -1.0, None, ALU.mult)
                    rows = slice(C_AT, C_AT + N)
                    nc.vector.tensor_scalar(neg_a_t[rows, :], neg_a_t[rows, :], -1.0, None, ALU.mult)
                    dve.wait_ge(v_ready, 2 * IC)
                    for c in range(IC):
                        dve.wait_ge(ln_ready, c + 1)
                        nc.vector.scalar_tensor_tensor(delta[:, c, :], delta[:, c, :], 0.0, du[:, c, :],
                                                       ALU.max, ALU.add).then_inc(delta_ready, 1)
                        dve.wait_ge(delta_ready, c + 1)
                        nc.vector.tensor_tensor(du[:, c, :], delta[:, c, :], u[:, c, :], ALU.mult)

                @block.gpsimd
                def _(pool):
                    nc.gpsimd.memset(y[:, :, :], 0.0).then_inc(y_zero, 1)

        with ExitStack() as inner:
            eye = sb("eye", [XD, N], into=inner)
            zeros = sb("zeros", [P, B], into=inner)
            zeroed = sem("zeroed")
            pick = sb("pick", [XD, 2, P], into=inner)
            a_now = sb("a_now", [P, 2, IC], into=inner)
            decay = sb("state_decay", [P, 2, T], into=inner)
            grow = sb("state_input", [P, 2, T], into=inner)
            state = sb("state", [P, 2, T], into=inner)
            part = sb("part", [P, 2, T], into=inner)
            eye_loaded, picked, spread, decayed, reset, grown, stepped, parted, added = (
                sem(n) for n in ("eye_loaded", "picked", "spread", "decayed", "reset", "grown", "stepped", "parted",
                                 "added"))
            with nc.Block() as block:

                @block.sync
                def _(sp):
                    sp.dma_start(eye[:, :], env.dram["eye_rows"]).then_inc(eye_loaded, 16)

                @block.tensor
                def _(pe):
                    with pe.Fori(0, N // 2) as i:
                        for e in range(2):
                            pe.wait_ge(picked, 3 * (2 * i + e + 1))
                            pe.wait_ge(parted, i * (2 * IC))
                            for j, at in enumerate((B_AT, C_AT)):
                                for h in range(2):
                                    mm = nc.tensor.matmul(env.bank(4 * e + 2 * j + h), pick[at:at + N, e, :],
                                                          x_dbl[at:at + N, h * HALF:(h + 1) * HALF],
                                                          start=True, stop=True, tile_position=(at, 0))
                            mm.then_inc(spread, 1)

                @block.scalar
                def _(act):
                    with act.Fori(0, N // 2) as i:
                        for e in range(2):
                            act.wait_ge(picked, 3 * (2 * i + e + 1))
                            for c in range(IC):
                                n = e * IC + c
                                act.wait_ge(stepped, i * (2 * IC) + max(n - 1, 0))
                                nc.scalar.activation(decay[:, n % 2, :], delta[:, c, :], ACT.Exp,
                                                     scale=a_now[:, e, c:c + 1]).then_inc(decayed, 1)

                @block.gpsimd
                def _(pool):
                    nc.gpsimd.memset(zeros[:, :], 0.0).then_inc(zeroed, 1)
                    pool.wait_ge(zeroed, 1)
                    with pool.Fori(0, N // 2) as i:
                        for n in range(2 * IC):
                            pool.wait_ge(decayed, i * (2 * IC) + n + 1)
                            nc.gpsimd.tensor_tensor(decay[:, n % 2, 0:T:S], zeros[:, :], zeros[:, :], ALU.add
                                                    ).then_inc(reset, 1)
                            pool.wait_ge(parted, i * (2 * IC) + n + 1)
                            pool.wait_ge(added, i * (2 * IC) + max(n - IC + 1, 0))
                            nc.gpsimd.tensor_tensor(y[:, n % IC, :], y[:, n % IC, :], part[:, n % 2, :],
                                                    ALU.add).then_inc(added, 1)

                @block.vector
                def _(dve):
                    dve.wait_ge(eye_loaded, 16)
                    with dve.Fori(0, N // 2) as i:
                        for e in range(2):
                            dve.wait_ge(spread, 2 * i)
                            dve.wait_ge(decayed, i * (2 * IC))
                            nc.vector.tensor_copy(a_now[:, e, :], neg_a[:, :, bass.ds(2 * i + e, 1)].rearrange(
                                "p c o -> p (c o)")).then_inc(picked, 1)
                            for at in (B_AT, C_AT):
                                rows = slice(at, at + N)
                                nc.vector.tensor_copy(pick[rows, e, :], eye[rows, bass.ds(2 * i + e, 1)].to_broadcast(
                                    [N, P])).then_inc(picked, 1)
                        for e in range(2):
                            dve.wait_ge(spread, 2 * i + e + 1)
                            b_n = env.psum[:, 4 * e:4 * e + 2, :].rearrange("p k n -> p (k n)")
                            c_n = env.psum[:, 4 * e + 2:4 * e + 4, :].rearrange("p k n -> p (k n)")
                            for c in range(IC):
                                n = e * IC + c
                                k = n % 2
                                dve.wait_ge(stepped, i * (2 * IC) + max(n - 1, 0))
                                nc.vector.tensor_tensor(grow[:, k, :], du[:, c, :], b_n, ALU.mult).then_inc(grown, 1)
                                dve.wait_ge(grown, i * (2 * IC) + n + 1)
                                dve.wait_ge(reset, i * (2 * IC) + n + 1)
                                dve.wait_ge(parted, i * (2 * IC) + max(n - 1, 0))
                                nc.vector.tensor_tensor_scan(state[:, k, :], decay[:, k, :], grow[:, k, :], 0.0,
                                                             ALU.mult, ALU.add).then_inc(stepped, 1)
                                dve.wait_ge(stepped, i * (2 * IC) + n + 1)
                                dve.wait_ge(added, i * (2 * IC) + max(n - 1, 0))
                                nc.vector.tensor_tensor(part[:, k, :], state[:, k, :], c_n, ALU.mult
                                                        ).then_inc(parted, 1)

        w_out1, w_out2 = sb("w_out1", [P, 2 * IC, DI]), sb("w_out2", [P, IC, D])
        d_rep = sb("d_rep", [P, IC, P])
        loaded, rep_ready, mid, gated_y, t_filled, t_taken, h_filled, h_ready, out_filled, added = (
            sem(n) for n in ("loaded", "rep_ready", "mid", "gated_y", "t_filled", "t_taken", "h_filled", "h_ready",
                             "out_filled", "added"))
        y_t, h1 = delta, gate
        with nc.Block() as block:

            @block.sync
            def _(sp):
                sp.dma_start(w_out1[:, :, :], env.dram["l3a_w_out1"]).then_inc(loaded, 16)
                sp.dma_start(w_out2[:, :, :], env.dram["l3a_w_out2"]).then_inc(loaded, 16)

            @block.vector
            def _(dve):
                for c in range(IC):
                    nc.vector.tensor_copy(d_rep[:, c, :], d_col[:, c:c + 1].to_broadcast([P, P])).then_inc(rep_ready, 1)
                for c in range(IC):
                    nc.vector.scalar_tensor_tensor(y[:, c, :], u[:, c, :], d_col[:, c:c + 1], y[:, c, :],
                                                   ALU.mult, ALU.add).then_inc(mid, 1)
                    dve.wait_ge(mid, c + 1)
                    nc.vector.tensor_tensor(y[:, c, :], y[:, c, :], gate[:, c, :], ALU.mult).then_inc(gated_y, 1)
                for t in range(NT):
                    dve.wait_ge(out_filled, t + 1)
                    nc.vector.tensor_tensor(env.x[:, t, :], env.x[:, t, :], env.psum[:, 4 + t % 4, 0:D],
                                            ALU.add).then_inc(added, 1)

            @block.tensor
            def _(pe):
                pe.wait_ge(rep_ready, IC)
                for n in range(2 * IC):
                    m, here = n // 2, slice(n % 2 * HALF, (n % 2 + 1) * HALF)
                    for k in range(IC):
                        nc.tensor.matmul(env.bank(n), d_rep[:, k, :], u[:, k, here], start=(k == 0), stop=False)
                    nc.tensor.matmul(env.bank(n), neg_a_t[C_AT:C_AT + N, m * P:(m + 1) * P], x_dbl[C_AT:C_AT + N, here],
                                     start=False, stop=True, tile_position=(C_AT, 0)).then_inc(t_filled, 1)
                pe.wait_ge(loaded, 32)
                pe.wait_ge(gated_y, IC)
                pe.wait_ge(t_taken, 2 * IC)
                for n in range(2 * IC):
                    m, here = n // 2, slice(n % 2 * HALF, (n % 2 + 1) * HALF)
                    if n >= 4:
                        pe.wait_ge(h_ready, n - 3)
                    for k in range(2 * IC):
                        mm = nc.tensor.matmul(env.bank(n % 4), w_out1[:, k, m * P:(m + 1) * P],
                                              (y if k < IC else y_t)[:, k % IC, here],
                                              start=(k == 0), stop=(k == 2 * IC - 1))
                    mm.then_inc(h_filled, 1)
                pe.wait_ge(h_ready, 2 * IC)
                for t in range(NT):
                    if t >= 4:
                        pe.wait_ge(added, t - 3)
                    for k in range(IC):
                        mm = nc.tensor.matmul(env.psum[:, 4 + t % 4, 0:D], h1[:, k, t * P:(t + 1) * P], w_out2[:, k, :],
                                              start=(k == 0), stop=(k == IC - 1))
                    mm.then_inc(out_filled, 1)

            @block.scalar
            def _(act):
                for n in range(2 * IC):
                    act.wait_ge(t_filled, n + 1)
                    nc.scalar.copy(y_t[:, n // 2, n % 2 * HALF:(n % 2 + 1) * HALF], env.bank(n)).then_inc(t_taken, 1)
                act.wait_ge(gated_y, IC)
                for n in range(2 * IC):
                    act.wait_ge(h_filled, n + 1)
                    nc.scalar.activation(h1[:, n // 2, n % 2 * HALF:(n % 2 + 1) * HALF], env.bank(n % 4), ACT.Relu
                                         ).then_inc(h_ready, 1)


def l0_attn(env):
    nc = env.nc
    normalise(env, env.x, transpose=False)
    normalise(env, env.xn, gain="l0a_gain", shift="l0a_shift")
    SEG, DH = 32, 64
    PAIRS = HEADS // 2
    HT = 2 * NT
    sem = env.sem
    (consts_loaded, w_loaded, w_out_loaded, beta_ready, cleared) = (
        sem(n) for n in ("consts_loaded", "w_loaded", "w_out_loaded", "beta_ready", "cleared"))
    (projected, feature_ready, sin_ready, cos_ready, roped, elu_ready, v_filled, v_taken, s_filled, t_filled,
     z_filled, s_taken, t_taken, shifted, exp_done, weights_s, wt_ready, pv_filled, o_taken, chain_s,
     out_filled, added) = (
        sem(n) for n in ("projected", "feature_ready", "sin_ready", "cos_ready", "roped", "elu_ready", "v_filled",
                         "v_taken", "s_filled", "t_filled", "z_filled", "s_taken", "t_taken", "shifted", "exp_done",
                         "weights_chain", "wt_ready", "pv_filled", "o_taken", "chain", "out_filled", "added"))
    with ExitStack() as ctx:
        def sb(name, shape, dtype=F32):
            return env.sbuf(name, shape, dtype, ctx)

        w = sb("w_qkv", [P, DC, 5, P])
        w_out = sb("w_out", [P, PAIRS, D])
        cos, sin, causal = sb("cos", [P, S]), sb("sin", [P, S]), sb("causal", [P, SEG])
        z_col = sb("z_col", [P, 2])
        beta, rest = sb("beta", [P, HEADS]), sb("one_minus_beta", [P, HEADS])
        roped_t, sin_part, expo, relu, elu = (sb(n, [P, 2, T]) for n in ("roped", "sin_part", "expo", "relu", "elu"))
        v = sb("v", [P, NT, P])
        local, memory = sb("local", [P, HT, SEG]), sb("memory", [P, HT, SEG])
        peak, total, inverse, m_total, m_inverse = (sb(n, [P, HT]) for n in ("peak", "total", "inverse", "m_total",
                                                                            "m_inverse"))
        weight_t = sb("weight_t", [P, HT, P])
        o_t = sb("o_t", [P, PAIRS, T])
        loads = [(cos[:, :], "rope_cos"), (sin[:, :], "rope_sin"), (causal[:, :], "causal"), (z_col[:, :], "z_col")]

        def banks(k, n):
            return env.psum[:, k:k + n, :].rearrange("p k n -> p (k n)")

        with nc.Block() as block:

            @block.sync
            def _(sp):
                for dst, src in loads:
                    sp.dma_start(dst, env.dram[src]).then_inc(consts_loaded, 16)
                sp.dma_start(beta[:, :], env.dram["l0a_beta"].partition_broadcast(P)).then_inc(consts_loaded, 16)
                sp.dma_start(w[:, :, :, :], env.dram["l0a_w"][0]).then_inc(w_loaded, 16)
                sp.dma_start(w_out[:, :, :], env.dram["l0a_w_out"]).then_inc(w_out_loaded, 16)
                with sp.Fori(0, PAIRS - 1) as c:
                    sp.wait_ge(v_filled, c + 1)
                    sp.dma_start(w[:, :, :, :], env.dram["l0a_w"][bass.ds(c + 1, 1)].rearrange(
                        "o p k j n -> p (o k) j n")).then_inc(w_loaded, 16)

            @block.tensor
            def _(pe):
                pe.wait_ge(consts_loaded, 16 * (len(loads) + 1))
                with pe.Fori(0, PAIRS) as c:
                    pe.wait_ge(w_loaded, 16 * c + 16)
                    for j in range(4):
                        if j == 2:
                            pe.wait_ge(o_taken, c)
                        for h in range(2):
                            for k in range(DC):
                                mm = nc.tensor.matmul(env.bank(2 * j + h), w[:, k, j, :],
                                                      env.xt[:, k, h * HALF:(h + 1) * HALF],
                                                      start=(k == 0), stop=(k == DC - 1))
                        mm.then_inc(projected, 1)
                    pe.wait_ge(cos_ready, 2 * c + 1)
                    for t in range(NT):
                        for k in range(DC):
                            mm = nc.tensor.matmul(env.psum[:, t // 4, t % 4 * P:(t % 4 + 1) * P],
                                                  env.xt[:, k, t * P:(t + 1) * P], w[:, k, 4, :],
                                                  start=(k == 0), stop=(k == DC - 1))
                    mm.then_inc(v_filled, 1)
                    pe.wait_ge(v_taken, c + 1)
                    for part, (ready, x) in enumerate(((roped, roped_t), (elu_ready, elu))):
                        pe.wait_ge(ready, 2 * c + 2)
                        if part == 1:
                            pe.wait_ge(cos_ready, 2 * c + 2)
                        for h in range(2):
                            rows = slice(DH * h, DH * h + DH)
                            for t in range(NT):
                                here = slice(t * P, (t + 1) * P)
                                mm = nc.tensor.matmul(
                                    env.psum[:, 4 * part + 2 * h + t // 4, t % 4 * P:(t % 4 + 1) * P],
                                    x[rows, 0, here], x[rows, 1, here], start=True, stop=True,
                                    tile_position=(DH * h, 0))
                        mm.then_inc((s_filled, t_filled)[part], 1)
                    pe.wait_ge(s_taken, 4 * c + 4)
                    for t in range(NT):
                        mm = nc.tensor.matmul(env.psum[:, 0, 2 * t:2 * t + 2], elu[:, 0, t * P:(t + 1) * P], z_col[:, :],
                                              start=True, stop=True)
                    mm.then_inc(z_filled, 1)
                    pe.wait_ge(wt_ready, 6 * c + 6)
                    for h in range(2):
                        for t in range(NT):
                            mm = nc.tensor.matmul(
                                env.psum[DH * h:DH * h + DH, 4 + t // 4, t % 4 * P:(t % 4 + 1) * P],
                                v[:, t, DH * h:DH * h + DH], weight_t[:, NT * h + t, :], start=True, stop=True,
                                tile_position=(0, DH * h))
                    mm.then_inc(pv_filled, 1)
                pe.wait_ge(o_taken, PAIRS)
                pe.wait_ge(w_out_loaded, 16)
                for t in range(NT):
                    if t >= 4:
                        pe.wait_ge(added, t - 3)
                    for k in range(PAIRS):
                        mm = nc.tensor.matmul(env.psum[:, t % 4, 0:D], o_t[:, k, t * P:(t + 1) * P], w_out[:, k, :],
                                              start=(k == 0), stop=(k == PAIRS - 1))
                    mm.then_inc(out_filled, 1)

            @block.scalar
            def _(act):
                act.wait_ge(consts_loaded, 16 * (len(loads) + 1))
                nc.scalar.activation(beta[:, :], beta[:, :], ACT.Sigmoid).then_inc(beta_ready, 1)
                with act.Fori(0, PAIRS) as c:
                    for s in range(2):
                        act.wait_ge(projected, 4 * c + 2 * s + 1)
                        act.wait_ge(elu_ready, 2 * c)
                        nc.scalar.activation(expo[:, s, :], banks(4 * s, 2), ACT.Exp)
                        nc.scalar.activation(relu[:, s, :], banks(4 * s, 2), ACT.Relu).then_inc(feature_ready, 1)
                    act.wait_ge(v_filled, c + 1)
                    nc.scalar.copy(v[:, :, :].rearrange("p t n -> p (t n)"), banks(0, 2)).then_inc(v_taken, 1)
                    act.wait_ge(shifted, c + 1)
                    nc.scalar.activation(local[:, :, :], local[:, :, :], ACT.Exp).then_inc(exp_done, 1)
                    act.wait_ge(pv_filled, c + 1)
                    nc.scalar.copy(o_t[:, bass.ds(c, 1), :].rearrange("p o n -> p (o n)"), banks(4, 2)
                                   ).then_inc(o_taken, 1)

            @block.gpsimd
            def _(pool):
                nc.gpsimd.memset(weight_t[:, :, :], 0.0).then_inc(cleared, 1)
                nc.gpsimd.memset(memory[:, :, :], 0.0).then_inc(cleared, 1)
                with pool.Fori(0, PAIRS) as c:
                    for s in range(2):
                        pool.wait_ge(sin_ready, 2 * c + s + 1)
                        pool.wait_ge(cos_ready, 2 * c + s + 1)
                        nc.gpsimd.tensor_tensor(roped_t[:, s, :], roped_t[:, s, :], sin_part[:, s, :], ALU.add
                                                ).then_inc(roped, 1)

            @block.vector
            def _(dve):
                dve.wait_ge(beta_ready, 1)
                nc.vector.tensor_scalar(rest[:, :], beta[:, :], -1.0, 1.0, ALU.mult, ALU.add).then_inc(beta_ready, 1)
                dve.wait_ge(beta_ready, 2)
                dve.wait_ge(cleared, 2)
                L = 10
                with dve.Fori(0, PAIRS) as c:
                    chain = Chain(dve, chain_s, c * L)

                    def over_batches(x):
                        return x.rearrange("p (b s) -> p b s", s=S)

                    def table(x):
                        return x[:, None, :].to_broadcast([P, B, S])

                    for s in range(2):
                        dve.wait_ge(projected, 4 * c + 2 * s + 2)
                        nc.vector.tensor_tensor(over_batches(sin_part[:, s, :]), over_batches(banks(4 * s + 2, 2)),
                                                table(sin), ALU.mult).then_inc(sin_ready, 1)
                        dve.wait_ge(feature_ready, 2 * c + s + 1)
                        nc.vector.tensor_tensor(over_batches(roped_t[:, s, :]), over_batches(banks(4 * s, 2)),
                                                table(cos), ALU.mult).then_inc(cos_ready, 1)
                        nc.vector.scalar_tensor_tensor(elu[:, s, :], expo[:, s, :], 1.0, relu[:, s, :],
                                                       ALU.min, ALU.add).then_inc(elu_ready, 1)
                    full = [P, HT, SEG]
                    s_psum = banks(0, 4).rearrange("p (r n) -> p r n", n=P)
                    t_psum = banks(4, 4).rearrange("p (r n) -> p r n", n=P)
                    dve.wait_ge(s_filled, c + 1)
                    for g in range(4):
                        rows = slice(SEG * g, SEG * g + SEG)
                        nc.vector.scalar_tensor_tensor(local[rows, :, :], s_psum[rows, :, rows], DH ** -0.5,
                                                       causal[rows, None, :].to_broadcast([SEG, HT, SEG]),
                                                       ALU.mult, ALU.add).then_inc(s_taken, 1)
                    dve.wait_ge(s_taken, 4 * c + 4)
                    chain(nc.vector.tensor_reduce(peak[:, :], local[:, :, :], AX.X, ALU.max))
                    nc.vector.tensor_tensor(local[:, :, :], local[:, :, :], peak[:, :, None].to_broadcast(full),
                                            ALU.subtract).then_inc(shifted, 1)
                    dve.wait_ge(t_filled, c + 1)
                    for g in (1, 3):
                        rows = slice(SEG * g, SEG * g + SEG)
                        nc.vector.tensor_copy(memory[rows, :, :], t_psum[rows, :, SEG * (g - 1):SEG * g]
                                              ).then_inc(t_taken, 1)
                    dve.wait_ge(t_taken, 2 * c + 2)
                    chain(nc.vector.tensor_reduce(m_total[:, :], memory[:, :, :], AX.X, ALU.add))
                    dve.wait_ge(z_filled, c + 1)
                    by_head = [P, 2, NT]
                    chain(nc.vector.scalar_tensor_tensor(m_total[:, :].rearrange("p (h t) -> p h t", h=2),
                                                         env.psum[:, 0, 0:HT].rearrange("p (t h) -> p h t", h=2), 1e-6,
                                                         m_total[:, :].rearrange("p (h t) -> p h t", h=2),
                                                         ALU.add, ALU.add))
                    chain(nc.vector.reciprocal(m_inverse[:, :], m_total[:, :]))
                    chain(nc.vector.tensor_tensor(m_inverse[:, :].rearrange("p (h t) -> p h t", h=2),
                                                  m_inverse[:, :].rearrange("p (h t) -> p h t", h=2),
                                                  beta[:, bass.ds(2 * c, 2), None].to_broadcast(by_head), ALU.mult))
                    chain(nc.vector.tensor_tensor(memory[:, :, :], memory[:, :, :],
                                                  m_inverse[:, :, None].to_broadcast(full), ALU.mult))
                    dve.wait_ge(exp_done, c + 1)
                    chain(nc.vector.tensor_reduce(total[:, :], local[:, :, :], AX.X, ALU.add))
                    chain(nc.vector.reciprocal(inverse[:, :], total[:, :]))
                    chain(nc.vector.tensor_tensor(inverse[:, :].rearrange("p (h t) -> p h t", h=2),
                                                  inverse[:, :].rearrange("p (h t) -> p h t", h=2),
                                                  rest[:, bass.ds(2 * c, 2), None].to_broadcast(by_head), ALU.mult))
                    chain(nc.vector.tensor_tensor(local[:, :, :], local[:, :, :],
                                                  inverse[:, :, None].to_broadcast(full), ALU.mult))
                    dve.wait_ge(pv_filled, c)
                    for g in range(4):
                        rows = slice(SEG * g, SEG * g + SEG)
                        nc.vector.transpose(weight_t[rows, :, rows], local[rows, :, :]).then_inc(wt_ready, 1)
                    for g in (1, 3):
                        rows, before = slice(SEG * g, SEG * g + SEG), slice(SEG * (g - 1), SEG * g)
                        nc.vector.transpose(weight_t[before, :, rows], memory[rows, :, :]).then_inc(wt_ready, 1)
                    dve.wait_ge(wt_ready, 6 * c + 6)
                    assert chain.n == L
                for t in range(NT):
                    dve.wait_ge(out_filled, t + 1)
                    nc.vector.tensor_tensor(env.x[:, t, :], env.x[:, t, :], env.psum[:, t % 4, 0:D],
                                            ALU.add).then_inc(added, 1)


def more_layouts(a, out, rows, column):
    for n in ("q", "k", "v", "o"):
        out[f"l1a_w{n}"] = rows(a[f"L1_attn_W_{n}"])
    out["l1a_down"] = rows(a["L1_attn_W_down_kv"])
    out["l1a_up_k"], out["l1a_up_v"] = a["L1_attn_W_up_k"], a["L1_attn_W_up_v"]
    out["l2a_w_in"], out["l2a_w_out"] = rows(a["L2_attn_W_in"]), rows(a["L2_attn_W_out"])
    out["l2a_gamma"], out["l2a_beta"] = column(a["L2_attn_gamma"]), column(a["L2_attn_beta"])
    out["l2a_a"], out["l2a_b_in"] = column(a["L2_attn_A"]), column(a["L2_attn_b_in"])
    out["l2a_b_out"] = a["L2_attn_b_out"]
    out["l1f_w1"], out["l1f_w2"] = rows(a["L1_ffn_w1"].T), rows(a["L1_ffn_w2"].T)
    out["l1f_conv_w"] = a["L1_ffn_conv_w"].reshape(-1, P, 3).transpose(1, 0, 2)
    out["l1f_conv_b"] = column(a["L1_ffn_conv_b"])
    w = a["L3_attn_W_x"].T
    gap = np.zeros((w.shape[0], 16), w.dtype)
    out["l3a_w_x"] = rows(np.concatenate([w[:, 0:16], gap, w[:, 16:32], gap, w[:, 32:48]], axis=1))
    out["l3a_w_in"] = rows(a["L3_attn_W_in"].T)
    out["l3a_conv_w"] = a["L3_attn_conv_w"].reshape(-1, P, 4).transpose(1, 0, 2)
    out["l3a_conv_b"] = column(a["L3_attn_conv_b"])
    out["l3a_w_dt"], out["l3a_b_dt"] = a["L3_attn_W_dt"].T, column(a["L3_attn_b_dt"])
    out["l3a_d"], out["l3a_a"] = column(a["L3_attn_Dp"]), a["L3_attn_A_log"].reshape(-1, P, 16).transpose(1, 0, 2)
    out["l3a_a_t"] = a["L3_attn_A_log"].T
    out["l3a_w_out1"], out["l3a_w_out2"] = rows(a["L3_attn_W_out1"].T), rows(a["L3_attn_W_out2"].T)

    w = a["L0_attn_w_qkv"].reshape(D, 3, 8, P)
    swapped = w.reshape(D, 3, 8, P // 2, 2)[..., ::-1].reshape(w.shape)
    five = np.stack([w[:, 0], swapped[:, 0], w[:, 1], swapped[:, 1], w[:, 2]], axis=2)
    out["l0a_w"] = five.reshape(DC, P, 8, 5, P).transpose(2, 1, 0, 3, 4)
    out["l0a_w_out"] = rows(a["L0_attn_w_out"])
    out["l0a_gain"], out["l0a_shift"] = column(a["L0_attn_ln_g"]), column(a["L0_attn_ln_b"])
    out["l0a_beta"] = a["L0_attn_mem_beta"].reshape(HEADS)


def build(nc, dram, stages=None):
    with ExitStack() as ctx:
        env = Env(nc, ctx, dram)
        load_stream(env)
        for n, stage in enumerate(STAGES):
            if stages is None or n in stages:
                stage(env)
                env.end_stage()
        store_stream(env)


def l0_xattn(env):
    normalise(env, env.x)
    cross_attention(env, "l0x", "l0x_wq", "l0x_wk", "l0x_wv", "l0x_wo", "l0x_bq", "l0x_bk", "l0x_bv", "l0x_bo",
                    lambdas=[f"L0_xattn_lambda_{n}" for n in ("q1", "k1", "q2", "k2")])


def make_xattn(n, mask=None):
    def stage(env):
        normalise(env, env.x)
        cross_attention(env, f"l{n}x", *(f"l{n}x_{w}" for w in ("wq", "wk", "wv", "wo", "bq", "bk", "bv", "bo")),
                        mask=mask)
    return stage


STAGES = [l0_xattn, l0_attn, l0_ffn, make_xattn(1), l1_attn, l1_ffn,
          make_xattn(2, "mask"), l2_attn, l2_ffn, make_xattn(3), l3_attn, l3_ffn]


def constants():
    p = np.arange(P)
    out = {"identity": np.eye(P)}
    for subs, dim in ((2, HD), (4, HD // 2)):
        out[f"head_mask_{subs}"] = (p[:, None] % 32 // (32 // subs) == np.arange(subs)) / np.sqrt(dim)
    for n in (4, 8, 16):
        out[f"ties_{n}"] = np.broadcast_to(np.tril(np.ones((n, n)), -1), (P, n, n))
    out["pair_mask"] = p[:, None] // 16 == np.arange(8)
    distance = np.abs(np.arange(S)[:, None] - np.arange(S)[None, :])
    out["decay"] = np.tile(np.exp(-0.01 * distance) / np.sqrt(D), (2, 1))
    freqs = (10000.0 ** (-np.arange(0, 64, 2, dtype=np.float32) / 64)).astype(np.float32)
    angle = (np.arange(S, dtype=np.float32)[None, :] * np.repeat(freqs, 2)[:, None]).astype(np.float32)
    angle = np.tile(angle, (2, 1))
    out["rope_cos"] = np.cos(angle)
    out["rope_sin"] = np.sin(angle) * np.where(p % 2, 1.0, -1.0)[:, None]
    out["causal"] = np.where(np.arange(32)[None, :] <= p[:, None] % 32, 0.0, MASKED)
    out["z_col"] = 1e-6 * (p[:, None] // 64 == np.arange(2))
    out["eye_rows"] = np.arange(80)[:, None] % 32 == np.arange(16)
    return {k: np.ascontiguousarray(v, dtype=np.float32) for k, v in out.items()}


def lay_out(inputs):
    a = {k: np.asarray(v) for k, v in inputs.items()}
    out = constants()

    def rows(w):
        return np.moveaxis(w.reshape(*w.shape[:-2], -1, P, w.shape[-1]), -3, -2)

    def column(v):
        return np.moveaxis(v.reshape(*v.shape[:-1], -1, P), -1, -2)

    out["x"] = a["x"].reshape(T, D)
    out["ctx_t"] = rows(a["ctx_1024"].transpose(0, 2, 1))
    out["mask"] = a["mask_SxS2_ik0"]
    w, b = a["L0_xattn_in_proj_weight"], a["L0_xattn_in_proj_bias"]
    for i, n in enumerate("qkv"):
        out[f"l0x_w{n}"] = rows(w[i * D:(i + 1) * D].T)
        out[f"l0x_b{n}"] = b[i * D:(i + 1) * D]
    out["l0x_wo"] = rows(a["L0_xattn_out_proj_weight"].T)
    out["l0x_bo"] = a["L0_xattn_out_proj_bias"]
    for n in ("q1", "k1", "q2", "k2"):
        out[f"L0_xattn_lambda_{n}"] = a[f"L0_xattn_lambda_{n}"]
    for layer in (1, 2, 3):
        for n in "qkvo":
            w = a[f"L{layer}_xattn_W{n}"]
            out[f"l{layer}x_w{n}"] = rows(w if layer == 1 else w.T)
            out[f"l{layer}x_b{n}"] = a[f"L{layer}_xattn_b{n}"]
    for layer in range(4):
        for n in "qk":
            out[f"l{layer}x_b{n}"] = column(out[f"l{layer}x_b{n}"])

    def steps_up(name, shared):
        w = np.concatenate([a[name], a[shared].reshape(D, 2, P).transpose(1, 0, 2)])
        return rows(w.reshape(3, 6, D, P).transpose(0, 2, 1, 3).reshape(3, D, 6 * P))

    out["l0f_gate"] = steps_up("L0_ffn_w_gate", "L0_ffn_sw_gate")
    out["l0f_up"] = steps_up("L0_ffn_w_up", "L0_ffn_sw_up")
    w = np.concatenate([a["L0_ffn_w_down"], a["L0_ffn_sw_down"].reshape(2, P, D)])
    out["l0f_down"] = rows(w.reshape(3, 6 * P, D))
    out["l0f_router"] = rows(a["L0_ffn_gate_kernel"])
    out["l0f_bias"] = a["L0_ffn_gate_bias"]

    out["l2f_router"] = rows(a["L2_ffn_router_w"].T)
    out["l2f_w1"] = rows(a["L2_ffn_expert_w1"].transpose(0, 2, 1))
    out["l2f_w2"] = rows(a["L2_ffn_expert_w2"].transpose(0, 2, 1))
    out["l2f_b1"] = column(a["L2_ffn_expert_b1"])
    out["l2f_b2"] = a["L2_ffn_expert_b2"]

    out["l3f_ln_w"] = column(a["L3_ffn_ln_w"])
    out["l3f_router"] = rows(a["L3_ffn_Wg"])
    out["l3f_bias"] = a["L3_ffn_bg"]
    for n in "ab":
        out[f"l3f_w1{n}"] = rows(a[f"L3_ffn_W1{n}"])
        out[f"l3f_b1{n}"] = column(a[f"L3_ffn_b1{n}"])
    out["l3f_w2"] = rows(a["L3_ffn_W2"])
    out["l3f_b2"] = a["L3_ffn_b2"]
    more_layouts(a, out, rows, column)
    return {k: np.ascontiguousarray(v) for k, v in out.items()}


def kernel(**inputs):
    import concourse.bacc as bacc
    from concourse.bass_utils import run_bass_kernel_spmd

    arrays = lay_out(inputs)
    nc = bacc.Bacc("TRN2", target_bir_lowering=False, num_devices=1)
    dram = {k: nc.dram_tensor(f"in_{k}", v.shape, mybir.dt.from_np(v.dtype), kind="ExternalInput").ap()
            for k, v in arrays.items()}
    dram["out"] = nc.dram_tensor("out_x", (T, D), F32, kind="ExternalOutput").ap()
    build(nc, dram)
    result = run_bass_kernel_spmd(nc, [{f"in_{k}": v for k, v in arrays.items()}], core_ids=[0])
    return np.asarray(result.results[0]["out_x"]).reshape(B, S, D)
```

```python
from contextlib import ExitStack

import numpy as np

import concourse.bass as bass
from concourse import mybir

F32 = mybir.dt.float32
BF16 = mybir.dt.bfloat16
I32 = mybir.dt.int32
U32 = mybir.dt.uint32
ALU = mybir.AluOpType
ACT = mybir.ActivationFunctionType
AX = mybir.AxisListType

P = 128
B, S, D = 16, 64, 256
T = B * S
NT = T // P
DC = D // P
HALF = 512
NKEY = 1601
KT = -(-NKEY // P)
HEADS = 16
HD = D // HEADS
LAST_KEYS = NKEY - (KT - 1) * P
MASKED = -1e30


class Chain:

    def __init__(self, engine, sem, base=0):
        self.engine, self.sem, self.base, self.n = engine, sem, base, 0

    def __call__(self, instruction):
        self.n += 1
        instruction.then_inc(self.sem, 1)
        self.engine.wait_ge(self.sem, self.base + self.n)
        return instruction


class Env:

    def __init__(self, nc, ctx, dram):
        self.nc, self.ctx, self.dram = nc, ctx, dram
        self.serial = 0
        self.stage_sems = []
        self.x = self.sbuf("x_stream", [P, NT, D])
        self.xn = self.sbuf("x_normed", [P, NT, D])
        self.xt = self.sbuf("x_normed_T", [P, DC, T])
        self.ident = self.sbuf("identity", [P, P])
        self.psum = ctx.enter_context(nc.psum_tensor("psum_all", [P, 8, 512], F32))

    def sbuf(self, name, shape, dtype=F32, ctx=None):
        self.serial += 1
        return (ctx or self.ctx).enter_context(self.nc.sbuf_tensor(f"{name}_{self.serial}", shape, dtype))

    def sem(self, name):
        self.serial += 1
        handle = self.nc.alloc_semaphore(f"{name}_{self.serial}")
        self.stage_sems.append(handle)
        return handle

    def end_stage(self):
        nc, sems = self.nc, self.stage_sems
        with nc.Block() as block:

            @block.sync
            def _(sp):
                for handle in sems:
                    sp.sem_clear(handle)

        for handle in sems:
            nc.release_semaphore(handle)
        self.stage_sems = []

    def bank(self, k):
        return self.psum[:, k, :]


def load_stream(env):
    nc = env.nc
    loaded = env.sem("stream_loaded")
    with nc.Block() as block:

        @block.sync
        def _(sp):
            sp.dma_start(env.x[:, :, :], env.dram["x"].rearrange("(n p) d -> p n d", p=P)).then_inc(loaded, 16)
            sp.dma_start(env.ident[:, :], env.dram["identity"]).then_inc(loaded, 16)
            sp.wait_ge(loaded, 32)


def store_stream(env):
    nc = env.nc
    stored = env.sem("stream_stored")
    with nc.Block() as block:

        @block.sync
        def _(sp):
            sp.dma_start(env.dram["out"].rearrange("(n p) d -> p n d", p=P), env.x[:, :, :]).then_inc(stored, 16)
            sp.wait_ge(stored, 16)


def normalise(env, src, transpose=True, gain=None, shift=None, rms=False, eps=1e-5, early=None):
    nc = env.nc
    chain_s, normed, turned, loaded = (env.sem(n) for n in ("norm_chain", "tile_normed", "tile_turned", "gain_loaded"))
    var_ready, deviation_ready = env.sem("var_ready"), env.sem("deviation_ready")
    with ExitStack() as ctx:
        stats = env.sbuf("stats", [P, NT, 6], ctx=ctx)
        moments = env.sbuf("moments", [P, NT, 2], ctx=ctx)
        rstd = env.sbuf("rstd", [P, NT], ctx=ctx)
        deviation = env.sbuf("deviation", [P, NT], ctx=ctx)
        affine = env.sbuf("affine", [P, 2, DC], ctx=ctx)
        rows = (gain is not None) + (shift is not None)
        with nc.Block() as block:

            @block.sync
            def _(sp):
                for i, row in enumerate((gain, shift)):
                    if row is not None:
                        sp.dma_start(affine[:, i, :], env.dram[row]).then_inc(loaded, 16)
                if early:
                    early(sp)

            @block.vector
            def _(dve):
                chain = Chain(dve, chain_s)
                for t in range(NT):
                    nc.vector.bn_stats(stats[:, t, :], src[:, t, :]).then_inc(chain_s, 1)
                chain.n = NT
                dve.wait_ge(chain_s, NT)
                for t in range(NT):
                    nc.vector.bn_aggr(moments[:, t, :], stats[:, t, :]).then_inc(chain_s, 1)
                chain.n = 2 * NT
                dve.wait_ge(chain_s, 2 * NT)
                if rms:
                    chain(nc.vector.tensor_tensor(rstd[:, :], moments[:, :, 0], moments[:, :, 0], ALU.mult))
                    chain(nc.vector.tensor_tensor(moments[:, :, 1], moments[:, :, 1], rstd[:, :], ALU.add))
                    chain(nc.vector.memset(moments[:, :, 0], 0.0))
                nc.vector.tensor_scalar(rstd[:, :], moments[:, :, 1], eps, None, ALU.add).then_inc(var_ready, 1)
                dve.wait_ge(deviation_ready, 1)
                chain(nc.vector.reciprocal(rstd[:, :], deviation[:, :]))
                for t in range(NT):
                    nc.vector.tensor_scalar(env.xn[:, t, :], src[:, t, :], moments[:, t, 0:1], rstd[:, t:t + 1],
                                            ALU.subtract, ALU.mult).then_inc(normed, 1)

            if transpose:

                @block.tensor
                def _(pe):
                    for t in range(NT):
                        pe.wait_ge(normed, t + 1)
                        for c in range(DC):
                            mm = nc.tensor.transpose(env.psum[:, t, c * P:(c + 1) * P],
                                                     env.xn[:, t, c * P:(c + 1) * P], env.ident[:, :])
                        mm.then_inc(turned, 1)

            @block.scalar
            def _(act):
                act.wait_ge(var_ready, 1)
                nc.scalar.activation(deviation[:, :], rstd[:, :], ACT.Sqrt).then_inc(deviation_ready, 1)
                if not transpose:
                    return
                if rows:
                    act.wait_ge(loaded, 16 * rows)
                for t in range(NT):
                    act.wait_ge(turned, t + 1)
                    here = slice(t * P, (t + 1) * P)
                    if not rows:
                        nc.scalar.copy(env.xt[:, :, here],
                                       env.psum[:, t, 0:D].rearrange("p (c n) -> p c n", c=DC))
                        continue
                    for c in range(DC):
                        nc.scalar.activation(env.xt[:, c, here], env.psum[:, t, c * P:(c + 1) * P], ACT.Identity,
                                             scale=affine[:, 0, c:c + 1],
                                             bias=affine[:, 1, c:c + 1] if shift is not None else 0.0)


def add_projected(env, o_rows, w_o, scale=1.0):
    nc = env.nc
    o_turned, o_ready, out_filled, out_free = (env.sem(n) for n in ("o_turned", "o_ready", "out_filled", "out_free"))
    with ExitStack() as ctx:
        o_t = env.sbuf("o_t", [P, DC, T], ctx=ctx)
        with nc.Block() as block:

            @block.tensor
            def _(pe):
                for b in range(B):
                    if b >= 4:
                        pe.wait_ge(o_ready, b - 3)
                    for c in range(DC):
                        mm = nc.tensor.transpose(env.psum[:, b % 4, c * S:(c + 1) * S],
                                                 o_rows[:, b, c * P:(c + 1) * P], env.ident[0:S, 0:S])
                    mm.then_inc(o_turned, 1)
                for t in range(NT):
                    pe.wait_ge(o_ready, 2 * t + 2)
                    if t >= 4:
                        pe.wait_ge(out_free, t - 3)
                    for k in range(DC):
                        mm = nc.tensor.matmul(env.psum[:, 4 + t % 4, 0:D], o_t[:, k, t * P:(t + 1) * P], w_o[:, k, :],
                                              start=(k == 0), stop=(k == DC - 1))
                    mm.then_inc(out_filled, 1)

            @block.scalar
            def _(act):
                for b in range(B):
                    act.wait_ge(o_turned, b + 1)
                    nc.scalar.mul(o_t[:, :, b * S:(b + 1) * S],
                                  env.psum[:, b % 4, 0:DC * S].rearrange("p (c q) -> p c q", c=DC),
                                  scale).then_inc(o_ready, 1)

            @block.vector
            def _(dve):
                for t in range(NT):
                    dve.wait_ge(out_filled, t + 1)
                    nc.vector.tensor_tensor(env.x[:, t, :], env.x[:, t, :], env.psum[:, 4 + t % 4, 0:D],
                                            ALU.add).then_inc(out_free, 1)


class Step:

    def __init__(self, at, i=None):
        self.at, self.i = at, i

    def plus(self, n):
        return Step(self.at + n, self.i)

    def count(self, per_step, more=0):
        n = self.at * per_step + more
        return n if self.i is None else self.i * (4 * per_step) + n

    def batch(self, scale=1, more=0):
        n = self.at // 2 * scale + more
        return n if self.i is None else self.i * (2 * scale) + n


def at_least(engine, sem, value):
    if isinstance(value, int) and value <= 0:
        return
    engine.wait_ge(sem, value)


def add_token_rows(env, w_o, scale):
    nc = env.nc
    turned, o_ready, filled, free = (env.sem(n) for n in ("rows_turned", "rows_ready", "out_filled", "out_free"))
    with ExitStack() as ctx:
        o_t = env.sbuf("o_t", [P, DC, T], ctx=ctx)
        with nc.Block() as block:

            @block.tensor
            def _(pe):
                for t in range(NT):
                    if t >= 4:
                        pe.wait_ge(o_ready, t - 3)
                    for c in range(DC):
                        mm = nc.tensor.transpose(env.psum[:, t % 4, c * P:(c + 1) * P],
                                                 env.xn[:, t, c * P:(c + 1) * P], env.ident[:, :])
                    mm.then_inc(turned, 1)
                for t in range(NT):
                    pe.wait_ge(o_ready, t + 1)
                    if t >= 4:
                        pe.wait_ge(free, t - 3)
                    for k in range(DC):
                        mm = nc.tensor.matmul(env.psum[:, 4 + t % 4, 0:D], o_t[:, k, t * P:(t + 1) * P], w_o[:, k, :],
                                              start=(k == 0), stop=(k == DC - 1))
                    mm.then_inc(filled, 1)

            @block.scalar
            def _(act):
                for t in range(NT):
                    act.wait_ge(turned, t + 1)
                    nc.scalar.mul(o_t[:, :, t * P:(t + 1) * P],
                                  env.psum[:, t % 4, 0:DC * P].rearrange("p (c q) -> p c q", c=DC),
                                  scale).then_inc(o_ready, 1)

            @block.vector
            def _(dve):
                for t in range(NT):
                    dve.wait_ge(filled, t + 1)
                    nc.vector.tensor_tensor(env.x[:, t, :], env.x[:, t, :], env.psum[:, 4 + t % 4, 0:D],
                                            ALU.add).then_inc(free, 1)


def cross_attention(env, pre, wq, wk, wv, wo, bq, bk, bv, bo, lambdas=None, mask=None):
    nc = env.nc
    subs = 2 if lambdas is None else 4
    H2 = subs // 2
    PAIRS, CUTS = 4, 4
    ROUNDS = PAIRS * CUTS
    W = ROUNDS * H2
    OW = S * H2
    GV = -(-KT // 2)
    VW = HD + 1
    BLOCK = 2 * HD
    BLOCKS = (0, 1, 2, 0)
    Q_ROWS = 3 * BLOCK
    STEPS = 2 * B
    MAX = H2
    SCALE = 1.0 / np.sqrt(HD // H2)
    key_cut = [(k * 512, min(512, NKEY - k * 512)) for k in range(CUTS)]
    tiles_of = [min(4, KT - 4 * n) for n in range(CUTS)]
    rows_of = [P if n < CUTS - 1 else LAST_KEYS for n in range(CUTS)]
    K_ROUND = {0: 0, 2: 1, 4: 2, 6: 3}
    V_ROUND = [{8: 0, 10: 1, 12: 2}, {8: 4}]
    Q_ROUND = 6
    MOVES = len(BLOCKS) * PAIRS

    weights_loaded, const_ready = env.sem("weights_loaded"), env.sem("const_ready")
    ctx_loaded, k_stacked = env.sem("ctx_loaded"), env.sem("k_stacked")
    k_filled, k_high, k_rest, k_mid, k_low = (env.sem(n) for n in ("k_filled", "k_high_ready", "k_rest_ready",
                                                                  "k_mid_ready", "k_low_ready"))
    v_filled, v_ready = env.sem("v_filled"), env.sem("v_ready")
    q_filled, q_taken, q_ready = env.sem("q_filled"), env.sem("q_taken"), env.sem("q_ready")
    rows_scored, max_done = env.sem("rows_scored"), env.sem("max_done")
    keys_scored, exp_done, pv_done = env.sem("keys_scored"), env.sem("exp_done"), env.sem("pv_done")
    nm_split, nm_filled, nm_taken = env.sem("neg_max_split"), env.sem("neg_max_filled"), env.sem("neg_max_taken")
    o_copied, o_turned, o_taken = env.sem("o_copied"), env.sem("o_turned"), env.sem("o_taken")
    q_chain, nm_chain, o_chain, start_chain = (env.sem(n) for n in ("q_chain", "nm_chain", "o_chain", "start_chain"))
    waits_met, load_turn = env.sem("waits_met"), env.sem("load_turn")

    with ExitStack() as ctx:
        def sb(name, shape, dtype=F32):
            return env.sbuf(pre + name, shape, dtype, ctx)

        w_q = sb("wq", [P, DC, HEADS // 2, Q_ROWS])
        w_k, w_v, w_o = (sb(n, [P, DC, D]) for n in ("wk", "wv", "wo"))
        b_q, b_k = sb("bq", [Q_ROWS, HEADS // 2]), sb("bk", [P, DC])
        b_v, b_o = sb("bv", [P, D]), sb("bo", [P, D])
        owner_mask = sb("owner_mask", [Q_ROWS, subs])
        ones = sb("ones", [P, P], BF16)
        ident_bf = sb("ident_bf", [P, P], BF16)
        ctx_t = sb("ctx_t", [P, 2, DC, NKEY])
        k_parts = sb("k_parts", [P, 3, NKEY], BF16)
        k_left = sb("k_left", [P, 512])
        k_stack = sb("k_stack", [P, 4, PAIRS, NKEY], BF16)
        q_forms = sb("q_forms", [P, 4, 2, PAIRS, subs * S], BF16)
        nm_rows = sb("neg_max_rows", [P, 4, PAIRS, subs * S], BF16)
        q_scaled, q_left = sb("q_scaled", [Q_ROWS, PAIRS, S]), sb("q_left", [Q_ROWS, PAIRS, S])
        q_parts = sb("q_parts", [Q_ROWS, 3, PAIRS, S], BF16)
        v = sb("v", [P, 2, KT, HEADS, VW])
        probs_t = sb("probs_t", [P, 2, H2, 4, P])
        cut_max = sb("cut_max", [P, PAIRS, H2, CUTS])
        neg_max, nm_left = sb("neg_max", [P, H2]), sb("nm_left", [P, H2])
        nm_parts = sb("nm_parts", [P, H2, 3], BF16)
        o_t = sb("o_feature_major", [P, 4 * OW])
        inverse = sb("inverse", [P, HEADS])
        if lambdas:
            lam_in = sb("lam_in", [P, 4, 8])
            lam_prod = sb("lam_prod", [P, 2, 8])
            lam = sb("lam", [P, 4])
            o_second = sb("o_second", [S, HEADS, HD])
        if mask:
            mask_in = sb("mask_in", [S, NKEY], I32)
            mask_add = sb("mask_add", [P, NKEY], BF16)
            twice = sb("twice", [P, 2, S], BF16)
        loads = [(w_q[:, :, :, :], env.dram[wq]), (w_k[:, :, :], env.dram[wk]), (w_v[:, :, :], env.dram[wv]),
                 (w_o[:, :, :], env.dram[wo]), (b_q[:, :], env.dram[bq]), (b_k[:, :], env.dram[bk]),
                 (b_v[:, :], env.dram[bv].partition_broadcast(P)), (b_o[:, :], env.dram[bo].partition_broadcast(P)),
                 (owner_mask[:, :], env.dram[f"owner_mask_{subs}"])]
        if lambdas:
            loads += [(lam_in[:, i, :], env.dram[n].partition_broadcast(P)) for i, n in enumerate(lambdas)]
        if mask:
            loads += [(mask_in[:, :], env.dram[mask])]
        LOADED = 16 * len(loads)
        O_BANK, SMALL, K_BANK, V_BANK = 4, 5, 6, 7

        def first_loads(sp):
            for dst, src in loads:
                sp.dma_start(dst, src).then_inc(weights_loaded, 16)
            sp.dma_start(ctx_t[:, 0, :, :], env.dram["ctx_t"][0]).then_inc(ctx_loaded, 16)

        normalise(env, env.x, early=first_loads)

        def run_steps(engine, program):
            program(Step(-2), keys=True, maxima=False, outputs=False)
            program(Step(-1), keys=True, maxima=True, outputs=False)
            with engine.Fori(0, STEPS // 4 - 1) as i:
                for at in range(4):
                    program(Step(at, i), keys=True, maxima=True, outputs=True)
            for at in range(STEPS - 4, STEPS):
                program(Step(at), keys=at + 2 < STEPS, maxima=at + 1 < STEPS, outputs=True)

        with nc.Block() as block:

            @block.sync
            def _(sp):
                sp.wait_ge(ctx_loaded, 16)
                sp.dma_start(ctx_t[:, 1, :, :], env.dram["ctx_t"][1]).then_inc(ctx_loaded, 16)

                def step(s, keys, maxima, outputs):
                    if s.at % 2 == 0 and outputs and (s.i is not None):
                        source = env.dram["ctx_t"][bass.ds(s.batch(1, 2), 1)].rearrange("o p c n -> p (o c) n")
                        sp.wait_ge(v_filled, s.batch(GV, GV))
                        sp.sem_inc(load_turn, 1)
                        sp.wait_ge(ctx_loaded, s.batch(16, 32))
                        sp.dma_start(ctx_t[:, s.at // 2 % 2, :, :], source).then_inc(ctx_loaded, 16)
                    if keys:
                        sp.wait_ge(k_low, s.count(CUTS, 3 * CUTS))
                        for pair in range(PAIRS):
                            for block, part in enumerate(BLOCKS):
                                sp.dma_start(k_stack[block * BLOCK:(block + 1) * BLOCK, (s.at + 2) % 4, pair, :],
                                             k_parts[pair * BLOCK:(pair + 1) * BLOCK, part, :]
                                             ).then_inc(k_stacked, 16)

                run_steps(sp, step)

            @block.gpsimd
            def _(pool):
                pool.wait_ge(weights_loaded, LOADED)
                for t in range(NT):
                    nc.gpsimd.tensor_tensor(env.x[:, t, :], env.x[:, t, :], b_o[:, :], ALU.add)

            @block.tensor
            def _(pe):
                pe.wait_ge(weights_loaded, LOADED)

                def project_keys(s, cut):
                    if cut == 0:
                        pe.wait_ge(ctx_loaded, s.batch(16, 16))
                    at_least(pe, k_rest, s.count(CUTS, cut))
                    at, width = key_cut[cut]
                    for k in range(DC):
                        mm = nc.tensor.matmul(env.psum[:, K_BANK, 0:width],
                                              w_k[:, k, s.at % 2 * P:(s.at % 2 + 1) * P],
                                              ctx_t[:, s.at // 2 % 2, k, at:at + width],
                                              start=(k == 0), stop=(k == DC - 1))
                    mm.then_inc(k_filled, 1)

                def project_values(s, g):
                    at_least(pe, v_ready, s.batch(GV, g))
                    for j in range(2 * g, min(2 * g + 2, KT)):
                        rows = P if j < KT - 1 else LAST_KEYS
                        for k in range(DC):
                            mm = nc.tensor.matmul(env.psum[0:rows, V_BANK, (j % 2) * D:(j % 2 + 1) * D],
                                                  ctx_t[:, s.at // 2 % 2, k, j * P:j * P + rows], w_v[:, k, :],
                                                  start=(k == 0), stop=(k == DC - 1))
                    mm.then_inc(v_filled, 1)

                def project_queries(s):
                    at_least(pe, nm_taken, s.count(PAIRS, -3))
                    for pair in range(PAIRS):
                        for k in range(DC):
                            tokens = slice(s.batch(S), s.batch(S) + S) if s.i is None else bass.ds(s.batch(S), S)
                            mm = nc.tensor.matmul(env.psum[0:Q_ROWS, SMALL, pair * S:(pair + 1) * S],
                                                  w_q[:, k, s.at % 2 * PAIRS + pair, :], env.xt[:, k, tokens],
                                                  start=(k == 0), stop=(k == DC - 1))
                    mm.then_inc(q_filled, 1)

                def score_rows(s, pair, cut, h):
                    unit = (pair * CUTS + cut) * H2 + h
                    if unit == 0:
                        pe.wait_ge(q_ready, s.count(1, 1))
                        pe.wait_ge(k_stacked, s.count(16 * MOVES, 16 * MOVES))
                    pe.wait_ge(max_done, s.count(W * MAX, (unit + 1) * MAX))
                    at, width = key_cut[cut]
                    for form in range(2):
                        mm = nc.tensor.matmul(env.psum[:, unit % 2, 0:width],
                                              q_forms[:, s.at % 4, form, pair, h * P:(h + 1) * P],
                                              k_stack[:, s.at % 4, pair, at:at + width],
                                              start=(form == 0), stop=(form == 1 and mask is None))
                    if mask:
                        mm = nc.tensor.matmul(env.psum[:, unit % 2, 0:width],
                                              twice[:, :, :].rearrange("p s q -> p (s q)"),
                                              mask_add[:, at:at + width], start=False, stop=True)
                    mm.then_inc(rows_scored, 1)

                def score_keys(s, pair, cut, h):
                    unit = (pair * CUTS + cut) * H2 + h
                    if cut == 0 and h == 0:
                        pe.wait_ge(nm_taken, s.count(PAIRS, pair + 1))
                    pe.wait_ge(exp_done, s.count(W, unit + 1))
                    rows, tiles = rows_of[cut], tiles_of[cut]
                    nc.tensor.matmul(env.psum[0:rows, 2 + unit % 2, 0:tiles * P].rearrange("p (t n) -> p t n", n=P),
                                     ones[:, 0:rows],
                                     nm_rows[:, s.at % 4, pair, None, h * P:(h + 1) * P].to_broadcast([P, tiles, P]),
                                     start=True, stop=False)
                    for t in range(tiles):
                        at = (4 * cut + t) * P
                        out = env.psum[0:rows, 2 + unit % 2, t * P:(t + 1) * P]
                        last = t == tiles - 1
                        for form in range(2):
                            mm = nc.tensor.matmul(out, k_stack[:, s.at % 4, pair, at:at + rows],
                                                  q_forms[:, s.at % 4, form, pair, h * P:(h + 1) * P],
                                                  start=False, stop=(form == 1 and last and mask is None))
                        if mask:
                            mm = nc.tensor.matmul(out, mask_add[:, at:at + rows],
                                                  twice[:, :, :].rearrange("p s q -> p (s q)"), start=False, stop=last)
                    mm.then_inc(keys_scored, 1)

                def weigh(s, pair, cut):
                    r = pair * CUTS + cut
                    if r == 0 and s.at % 2 == 0:
                        pe.wait_ge(o_copied, s.batch(1, 1))
                    if r == 0:
                        pe.wait_ge(v_ready, s.batch(GV, GV))
                    pe.wait_ge(exp_done, s.count(W, (r + 1) * H2 + 2))
                    rows = rows_of[cut]
                    for t in range(tiles_of[cut]):
                        for h in range(2):
                            head = s.at % 2 * 8 + 2 * pair + h
                            j, g = head % 4, head // 4
                            cols = probs_t[0:rows, r % 2, 0, t, h * S:(h + 1) * S] if H2 == 1 else \
                                probs_t[0:rows, r % 2, h, t, :]
                            mm = nc.tensor.matmul(env.psum[32 * j:32 * j + VW, O_BANK, g * OW:(g + 1) * OW],
                                                  v[0:rows, s.at // 2 % 2, 4 * cut + t, head, :], cols,
                                                  start=(cut == 0 and t == 0), stop=(cut == CUTS - 1),
                                                  tile_position=(0, 32 * j))
                    mm.then_inc(pv_done, 1)

                def turn_max(s, pair):
                    pe.wait_ge(nm_split, s.count(PAIRS, pair + 1))
                    if pair == 3 and s.at % 2 == 0:
                        pe.wait_ge(o_taken, s.batch(1, 1))
                    if pair == 0:
                        pe.wait_ge(q_taken, s.count(1, 1))
                    if pair == 1:
                        pe.wait_ge(q_taken, s.count(1, 2) if s.at < STEPS - 1 or s.i is not None else STEPS)
                    at_least(pe, nm_taken, s.count(PAIRS, pair))
                    for h in range(H2):
                        mm = nc.tensor.matmul(env.psum[0:3, SMALL, h * P:(h + 1) * P], nm_parts[:, h, :],
                                              ident_bf[:, :], start=True, stop=True)
                    mm.then_inc(nm_filled, 1)

                def turn_outputs(s, maxima):
                    pe.wait_ge(o_copied, s.batch(1, 2))
                    pe.wait_ge(nm_taken, s.count(PAIRS, 2 * PAIRS - 1 if maxima else PAIRS))
                    pe.sem_inc(waits_met, 1)
                    for g in range(4):
                        mm = nc.tensor.transpose(env.psum[0:OW, SMALL, g * P:(g + 1) * P],
                                                 o_t[:, g * OW:(g + 1) * OW], env.ident[:, :])
                    mm.then_inc(o_turned, 1)

                def step(s, keys, maxima, outputs):
                    if s.at == -1:
                        pe.wait_ge(const_ready, 1)
                    for r in range(ROUNDS):
                        pair, cut = divmod(r, CUTS)
                        if maxima:
                            for h in range(H2):
                                score_rows(s.plus(1), pair, cut, h)
                        if outputs and r == 1:
                            turn_max(s, 3)
                        if maxima and r in (5, 9, 13):
                            turn_max(s.plus(1), (r - 5) // 4)
                        if keys and r in K_ROUND and H2 == 2:
                            project_keys(s.plus(2), K_ROUND[r])
                        if outputs:
                            for h in range(H2):
                                score_keys(s, pair, cut, h)
                            if r:
                                weigh(s, *divmod(r - 1, CUTS))
                        if keys and r in K_ROUND and H2 == 1:
                            project_keys(s.plus(2), K_ROUND[r])
                        if keys and r in V_ROUND[s.at % 2]:
                            project_values(s.plus(2), V_ROUND[s.at % 2][r])
                        if keys and r == Q_ROUND:
                            project_queries(s.plus(2))
                    if keys:
                        project_values(s.plus(2), GV - 2 if s.at % 2 else 3)
                    if outputs:
                        weigh(s, PAIRS - 1, CUTS - 1)
                    if keys and s.at % 2:
                        project_values(s.plus(2), GV - 1)
                    if outputs and s.at % 2:
                        turn_outputs(s, maxima)

                run_steps(pe, step)

            @block.scalar
            def _(act):
                act.wait_ge(weights_loaded, LOADED)
                act.sem_inc(exp_done, 2)
                if lambdas:
                    act.wait_ge(start_chain, 3)
                    nc.scalar.activation(lam[:, 2:4], lam[:, 0:2], ACT.Exp).then_inc(start_chain, 1)

                def step(s, keys, maxima, outputs):
                    for r in range(ROUNDS):
                        pair, cut = divmod(r, CUTS)
                        if outputs:
                            for h in range(H2):
                                unit = r * H2 + h
                                rows, tiles = rows_of[cut], tiles_of[cut]
                                act.wait_ge(keys_scored, s.count(W, unit + 1))
                                nc.scalar.activation(probs_t[0:rows, r % 2, h, 0:tiles, :],
                                                     env.psum[0:rows, 2 + unit % 2, 0:tiles * P].rearrange(
                                                         "p (t n) -> p t n", n=P), ACT.Exp).then_inc(exp_done, 1)
                        if keys:
                            for done, c in K_ROUND.items():
                                if done + 1 == r:
                                    at, width = key_cut[c]
                                    act.wait_ge(k_rest, s.count(CUTS, 2 * CUTS + c + 1))
                                    nc.scalar.copy(k_parts[:, 1, at:at + width], k_left[:, 0:width]).then_inc(k_mid, 1)
                            if r in K_ROUND:
                                c = K_ROUND[r]
                                at, width = key_cut[c]
                                act.wait_ge(k_filled, s.count(CUTS, 2 * CUTS + c + 1))
                                nc.scalar.activation(k_parts[:, 0, at:at + width], env.psum[:, K_BANK, 0:width],
                                                     ACT.Identity, bias=b_k[:, s.at % 2:s.at % 2 + 1]
                                                     ).then_inc(k_high, 1)
                    if outputs and s.at % 2:
                        act.wait_ge(pv_done, s.count(ROUNDS, ROUNDS))
                        nc.scalar.copy(o_t[:, :], env.psum[:, O_BANK, 0:4 * OW]).then_inc(o_copied, 1)

                run_steps(act, step)

            @block.vector
            def _(dve):
                start = Chain(dve, start_chain)
                start(nc.vector.memset(env.psum[:, O_BANK, 0:4 * OW], 0.0))
                dve.sem_inc(o_copied, 1)
                dve.sem_inc(o_taken, 1)
                dve.sem_inc(max_done, 2 * MAX)
                dve.wait_ge(weights_loaded, LOADED)
                if lambdas:
                    for i in range(2):
                        nc.vector.tensor_tensor(lam_prod[:, i, :], lam_in[:, 2 * i, :], lam_in[:, 2 * i + 1, :],
                                                ALU.mult).then_inc(q_chain, 1)
                    dve.wait_ge(q_chain, 2)
                    start(nc.vector.tensor_reduce(lam[:, 0:2], lam_prod[:, :, :], AX.X, ALU.add))
                    start(nc.vector.tensor_scalar(b_q[:, :], b_q[:, :], SCALE, None, ALU.mult))
                    dve.wait_ge(start_chain, 4)
                    start.n = 4
                    start(nc.vector.tensor_tensor(lam[:, 0:1], lam[:, 3:4], lam[:, 2:3], ALU.subtract))
                    start(nc.vector.tensor_scalar(lam[:, 0:1], lam[:, 0:1], -0.2, None, ALU.add))
                else:
                    start(nc.vector.tensor_scalar(b_q[:, :], b_q[:, :], SCALE, None, ALU.mult))
                if mask:
                    start(nc.vector.memset(twice[:, :, :], 0.0))
                    start(nc.vector.memset(mask_add[:, :], 0.0))
                    for s in range(2):
                        start(nc.vector.tensor_copy(twice[0:S, s, :], env.ident[0:S, 0:S]))
                    start(nc.vector.tensor_scalar(mask_add[0:S, :], mask_in[:, :], 0.0, MASKED, ALU.is_equal,
                                                  ALU.mult))
                start(nc.vector.memset(q_forms[2 * BLOCK:P, :, 1, :, :], 0.0))
                start(nc.vector.memset(nm_rows[:, :, :, :], 0.0))
                start(nc.vector.memset(ones[:, :], 1.0))
                for half in range(2):
                    start(nc.vector.memset(v[:, half, :, :, HD:VW], 1.0))
                nc.vector.tensor_copy(ident_bf[:, :], env.ident[:, :]).then_inc(const_ready, 1)
                Q_OPS, NM_OPS, O_OPS = 4, 4, 4 if lambdas else 1

                def key_rest(s, cut):
                    at, width = key_cut[cut]
                    dve.wait_ge(k_high, s.count(CUTS, cut + 1))
                    at_least(dve, k_low, s.count(CUTS, cut))
                    nc.vector.scalar_tensor_tensor(k_left[:, 0:width], env.psum[:, K_BANK, 0:width],
                                                   b_k[:, s.at % 2:s.at % 2 + 1], k_parts[:, 0, at:at + width],
                                                   ALU.add, ALU.subtract).then_inc(k_rest, 1)

                def key_low(s, cut):
                    at, width = key_cut[cut]
                    dve.wait_ge(k_mid, s.count(CUTS, cut + 1))
                    nc.vector.tensor_tensor(k_parts[:, 2, at:at + width], k_left[:, 0:width],
                                            k_parts[:, 1, at:at + width], ALU.subtract).then_inc(k_low, 1)

                def take_values(s, g):
                    tiles = min(2, KT - 2 * g)
                    rows = P if tiles == 2 else LAST_KEYS
                    dve.wait_ge(v_filled, s.batch(GV, g + 1))
                    nc.vector.tensor_tensor(v[0:rows, s.at // 2 % 2, 2 * g:2 * g + tiles, :, 0:HD],
                                            env.psum[0:rows, V_BANK, 0:tiles * D].rearrange(
                                                "p (j h w) -> p j h w", h=HEADS, w=HD),
                                            b_v[0:rows, :].rearrange("p (h w) -> p h w", w=HD)[:, None, :, :]
                                            .to_broadcast([rows, tiles, HEADS, HD]), ALU.add).then_inc(v_ready, 1)

                def take_max(s, pair):
                    dve.wait_ge(nm_filled, s.count(PAIRS, pair + 1))
                    nc.vector.tensor_copy(nm_rows[0:3, s.at % 4, pair, :],
                                          env.psum[0:3, SMALL, 0:subs * S]).then_inc(nm_taken, 1)

                def split_max(s, pair):
                    chain = Chain(dve, nm_chain, s.count(PAIRS * NM_OPS, pair * NM_OPS))
                    dve.wait_ge(max_done, s.count(W * MAX, ((pair + 1) * CUTS * H2 + 2) * MAX))
                    chain(nc.vector.tensor_reduce(neg_max[:, :], cut_max[:, pair, :, :], AX.X, ALU.max, negate=True))
                    chain(nc.vector.tensor_copy(nm_parts[:, :, 0], neg_max[:, :]))
                    chain(nc.vector.tensor_tensor(nm_left[:, :], neg_max[:, :], nm_parts[:, :, 0], ALU.subtract))
                    chain(nc.vector.tensor_copy(nm_parts[:, :, 1], nm_left[:, :]))
                    nc.vector.tensor_tensor(nm_parts[:, :, 2], nm_left[:, :], nm_parts[:, :, 1],
                                            ALU.subtract).then_inc(nm_split, 1)

                def take_queries(s, stage):
                    half = s.at % 2 * PAIRS
                    if stage == 0:
                        dve.wait_ge(q_filled, s.count(1, 1))
                        at_least(dve, q_ready, s.count(1))
                        nc.vector.scalar_tensor_tensor(
                            q_scaled[:, :, :], env.psum[0:Q_ROWS, SMALL, 0:PAIRS * S].rearrange("p (a q) -> p a q", q=S),
                            SCALE, b_q[:, half:half + PAIRS, None].to_broadcast([Q_ROWS, PAIRS, S]),
                            ALU.mult, ALU.add).then_inc(q_taken, 1)
                    if stage in (1, 2):
                        source, part = (q_scaled, 0) if stage == 1 else (q_left, 1)
                        if stage == 1:
                            dve.wait_ge(q_taken, s.count(1, 1))
                        chain = Chain(dve, q_chain, s.count(Q_OPS, 2 * part + (2 if lambdas else 0)))
                        chain(nc.vector.tensor_copy(q_parts[:, part, :, :], source[:, :, :]))
                        rest = q_left[:, :, :] if stage == 1 else q_parts[:, 2, :, :]
                        chain(nc.vector.tensor_tensor(rest, source[:, :, :], q_parts[:, part, :, :], ALU.subtract))
                    if stage >= 3:
                        form, at, blocks, part = ((0, 0, 3, 0), (0, 3, 1, 1), (1, 0, 1, 2), (1, 1, 1, 1))[stage - 3]
                        rows = slice(at * BLOCK, (at + blocks) * BLOCK)
                        source = slice(0, blocks * BLOCK)
                        full = [blocks * BLOCK, PAIRS, subs, S]
                        op = nc.vector.tensor_tensor(
                            q_forms[rows, s.at % 4, form, :, :].rearrange("p a (s q) -> p a s q", q=S),
                            q_parts[source, part, :, None, :].to_broadcast(full),
                            owner_mask[source, None, :, None].to_broadcast(full), ALU.mult)
                        if stage == 6:
                            op.then_inc(q_ready, 1)

                def take_outputs(s):
                    parity = s.at // 2 % 2
                    tile = bass.ds(s.i, 1) if s.i is not None else slice(s.at // 4, s.at // 4 + 1)
                    out = env.xn[parity * S:(parity + 1) * S, tile, :].rearrange("p o (h w) -> p (o h) w", w=HD)
                    turned = env.psum[:, SMALL, :].rearrange("p (h e) -> p h e", e=32)
                    dve.wait_ge(o_turned, s.batch(1, 1))
                    done = Chain(dve, o_chain, s.batch(O_OPS))
                    done(nc.vector.reciprocal(inverse[0:OW, :], turned[0:OW, :, HD]))
                    if lambdas:
                        done(nc.vector.tensor_scalar(inverse[S:P, :], inverse[S:P, :], lam[S:P, 0:1], None, ALU.mult))
                        done(nc.vector.tensor_tensor(o_second[:, :, :], turned[S:P, :, 0:HD],
                                                     inverse[S:P, :, None].to_broadcast([S, HEADS, HD]), ALU.mult))
                        done(nc.vector.tensor_tensor(out, turned[0:S, :, 0:HD],
                                                     inverse[0:S, :, None].to_broadcast([S, HEADS, HD]), ALU.mult))
                        nc.vector.tensor_tensor(out, out, o_second[:, :, :], ALU.add).then_inc(o_taken, 1)
                    else:
                        nc.vector.tensor_tensor(out, turned[0:S, :, 0:HD],
                                                inverse[0:S, :, None].to_broadcast([S, HEADS, HD]), ALU.mult
                                                ).then_inc(o_taken, 1)

                def step(s, keys, maxima, outputs):
                    for r in range(ROUNDS):
                        pair, cut = divmod(r, CUTS)
                        if maxima:
                            for h in range(H2):
                                unit = r * H2 + h
                                dve.wait_ge(rows_scored, s.plus(1).count(W, unit + 1))
                                nc.vector.tensor_reduce(cut_max[:, pair, h, cut:cut + 1],
                                                        env.psum[:, unit % 2, 0:key_cut[cut][1]], AX.X, ALU.max
                                                        ).then_inc(max_done, MAX)
                        if outputs and r == 1:
                            take_max(s, 3)
                        if maxima and r in (5, 9, 13):
                            take_max(s.plus(1), (r - 5) // 4)
                        if keys:
                            for done, c in K_ROUND.items():
                                if done + 1 == r:
                                    key_low(s.plus(2), c)
                            if r in K_ROUND:
                                key_rest(s.plus(2), K_ROUND[r])
                            if r in V_ROUND[s.at % 2]:
                                take_values(s.plus(2), V_ROUND[s.at % 2][r])
                            if Q_ROUND <= r <= Q_ROUND + 6:
                                take_queries(s.plus(2), r - Q_ROUND)
                        if maxima and cut == CUTS - 1:
                            split_max(s.plus(1), pair)
                    if keys:
                        for g in (GV - 2, GV - 1) if s.at % 2 else (3,):
                            take_values(s.plus(2), g)
                    if outputs and s.at % 2:
                        take_outputs(s)

                run_steps(dve, step)

        add_token_rows(env, w_o, 0.8 if lambdas else 1.0)




def rank_of(env, chain, values, ties, rank, scratch, shape):
    nc = env.nc
    rows, n = shape
    full = [P, rows, n, n]
    left = values[:, :, None, :].to_broadcast(full)
    own = values[:, :, :, None].to_broadcast(full)
    greater, equal = scratch
    chain(nc.vector.tensor_tensor(greater, left, own, ALU.is_gt))
    chain(nc.vector.tensor_tensor(equal, left, own, ALU.is_equal))
    chain(nc.vector.tensor_tensor(equal, equal, ties[:, None, :, :].to_broadcast(full), ALU.mult))
    chain(nc.vector.tensor_tensor(greater, greater, equal, ALU.add))
    chain(nc.vector.tensor_reduce(rank, greater, AX.X, ALU.add))


def route(env, ctx, kind, experts, weights, gate, add):
    nc = env.nc
    filled, loaded, chain_s = env.sem("logits_filled"), env.sem("gate_loaded"), env.sem("route_chain")
    scored, exp_ready = env.sem("scores_ready"), env.sem("exp_ready")
    n_all = weights.shape[2]
    def sb(name, shape):
        return env.sbuf(name, shape, ctx=ctx)

    w = sb("router_w", [P, DC, experts])
    ties = sb("ties", [P, experts, experts])
    ties4 = sb("ties4", [P, 4, 4])
    bias = sb("router_bias", [P, experts])
    score = sb("score", [P, NT, experts])
    prob = sb("prob", [P, NT, experts])
    rank = sb("rank", [P, NT, experts])
    big = [sb(f"pairs{i}", [P, NT * experts * experts]) for i in range(2)]
    row = sb("row", [P, NT * 4])
    group_rank = sb("group_rank", [P, NT * 4])
    total = sb("total", [P, NT])
    loads = [(w[:, :, :], env.dram[gate]), (ties[:, :, :], env.dram[f"ties_{experts}"]),
             (ties4[:, :, :], env.dram["ties_4"])]
    if add:
        loads.append((bias[:, :], env.dram[add].partition_broadcast(P)))
    logits = env.psum[:, 7, 0:NT * experts].rearrange("p (t e) -> p t e", t=NT)

    def pairs(rows, n):
        return [t[:, 0:rows * n * n].rearrange("p (r a b) -> p r a b", r=rows, a=n) for t in big]

    def wide(v):
        return v[:, :, None].to_broadcast([P, NT, experts])

    bias_all = bias[:, None, :].to_broadcast([P, NT, experts])

    def load(sp):
        for dst, src in loads:
            sp.dma_start(dst, src).then_inc(loaded, 16)

    def products(pe):
        pe.wait_ge(loaded, 16 * len(loads))
        for t in range(NT):
            for k in range(DC):
                mm = nc.tensor.matmul(logits[:, t, :], env.xt[:, k, t * P:(t + 1) * P], w[:, k, :],
                                      start=(k == 0), stop=(k == DC - 1))
        mm.then_inc(filled, 1)

    def exponentials(act):
        if kind == "groups":
            act.wait_ge(filled, 1)
            nc.scalar.activation(score[:, :, :], logits, ACT.Sigmoid).then_inc(exp_ready, 1)
        else:
            act.wait_ge(scored, 1)
            nc.scalar.activation(prob[:, :, :], prob[:, :, :], ACT.Exp).then_inc(exp_ready, 1)

    def choice(dve):
        chain = Chain(dve, chain_s)
        dve.wait_ge(loaded, 16 * len(loads))
        if n_all > experts:
            nc.vector.memset(weights[:, :, experts:n_all], 1.0)
        chosen = weights[:, :, 0:experts]
        if kind == "groups":
            dve.wait_ge(exp_ready, 1)
            chain(nc.vector.tensor_tensor(score[:, :, :], score[:, :, :], bias_all, ALU.add))
            quads = score[:, :, :].rearrange("p t (g j) -> p (t g) j", j=4)
            rank4 = rank[:, :, :].rearrange("p t (g j) -> p (t g) j", j=4)
            prob4 = prob[:, :, :].rearrange("p t (g j) -> p (t g) j", j=4)
            rank_of(env, chain, quads, ties4, rank4, pairs(NT * 4, 4), (NT * 4, 4))
            chain(nc.vector.scalar_tensor_tensor(prob4, rank4, 2.0, quads, ALU.is_lt, ALU.mult))
            chain(nc.vector.tensor_reduce(row[:, :], prob4, AX.X, ALU.add))
            sums = row[:, :].rearrange("p (t g) -> p t g", t=NT)
            ranks = group_rank[:, :].rearrange("p (t g) -> p t g", t=NT)
            rank_of(env, chain, sums, ties4, ranks, pairs(NT, 4), (NT, 4))
            chain(nc.vector.tensor_scalar(group_rank[:, :], group_rank[:, :], 2.0, None, ALU.is_lt))
            chain(nc.vector.tensor_tensor(quads, quads, group_rank[:, :, None].to_broadcast([P, NT * 4, 4]),
                                          ALU.mult))
            best, values = 4.0, score
        else:
            dve.wait_ge(filled, 1)
            if add:
                chain(nc.vector.tensor_tensor(score[:, :, :], logits, bias_all, ALU.add))
            else:
                chain(nc.vector.tensor_copy(score[:, :, :], logits))
            chain(nc.vector.tensor_reduce(total[:, :], score[:, :, :], AX.X, ALU.max))
            nc.vector.tensor_tensor(prob[:, :, :], score[:, :, :], wide(total),
                                    ALU.subtract).then_inc(scored, 1)
            dve.wait_ge(exp_ready, 1)
            best, values = 2.0, prob
            if kind == "probs":
                chain(nc.vector.tensor_reduce(total[:, :], prob[:, :, :], AX.X, ALU.add))
                chain(nc.vector.reciprocal(total[:, :], total[:, :]))
                chain(nc.vector.tensor_tensor(prob[:, :, :], prob[:, :, :], wide(total), ALU.mult))
        ranked = prob if kind == "probs" else score
        rank_of(env, chain, ranked[:, :, :], ties, rank[:, :, :], pairs(NT, experts), (NT, experts))
        chain(nc.vector.scalar_tensor_tensor(chosen, rank[:, :, :], best, values[:, :, :], ALU.is_lt, ALU.mult))
        chain(nc.vector.tensor_reduce(total[:, :], chosen, AX.X, ALU.add))
        tiny = {"groups": 1e-20, "probs": 1e-9, "logits": 0.0}[kind]
        chain(nc.vector.tensor_scalar(total[:, :], total[:, :], tiny, None, ALU.add))
        chain(nc.vector.reciprocal(total[:, :], total[:, :]))
        if kind == "groups":
            chain(nc.vector.tensor_scalar(total[:, :], total[:, :], 2.5, None, ALU.mult))
        chain(nc.vector.tensor_tensor(chosen, chosen, wide(total), ALU.mult))

    return load, products, exponentials, choice, exp_ready


def expert_ffn(env, norm, kind, routed, n_all, group, chunks, func, gate, add, up_a, up_b, down, bias_up, bias_down):
    nc = env.nc
    steps = n_all // group
    U = 2 * chunks
    DN = NT * group
    per = chunks // group
    gated = up_b is not None
    n_bias = (1 + gated) if bias_up else 0
    w1_loaded, w2_loaded, up_filled, act_ready = (env.sem(n) for n in ("up_loaded", "down_loaded", "up_filled",
                                                                      "act_ready"))
    h_ready, down_filled, down_free, column_s = (env.sem(n) for n in ("h_ready", "down_filled", "down_free", "column"))
    ones_ready = env.sem("ones_ready")
    with ExitStack() as ctx:
        def sb(name, shape):
            return env.sbuf(name, shape, ctx=ctx)

        combine = sb("combine", [P, NT, n_all])
        load_router, route_products, route_exponentials, choose, logits_gone = route(
            env, ctx, kind, routed, combine, gate, add)
        w_a = sb("w_a", [P, DC, chunks * P])
        w_b = sb("w_b", [P, DC, chunks * P]) if gated else None
        w_2 = sb("w_2", [P, chunks, D])
        b_up = sb("b_up", [P, 2, chunks])
        b_down = sb("b_down", [1, D])
        ones = sb("ones", [1, P])
        hidden = sb("hidden", [P, chunks, T])
        column = sb("column", [P, NT, group])

        def up_loads(e):
            one = bass.ds(e, 1)
            out = [(w_a[:, :, :], env.dram[up_a][one].rearrange("o p k n -> p (o k) n"))]
            if gated:
                out.append((w_b[:, :, :], env.dram[up_b][one].rearrange("o p k n -> p (o k) n")))
            for i in range(n_bias):
                out.append((b_up[:, i, :], env.dram[bias_up[i]][one].rearrange("o p n -> p (o n)")))
            return out

        def down_loads(e):
            one = bass.ds(e, 1)
            out = [(w_2[:, :, :], env.dram[down][one].rearrange("o p k n -> p (o k) n"))]
            if bias_down:
                out.append((b_down[:, :], env.dram[bias_down][one, :]))
            return out

        n_up, n_down = 1 + gated + n_bias, 1 + bool(bias_down)

        def first_loads(sp):
            load_router(sp)
            for dst, src in up_loads(0):
                sp.dma_start(dst, src).then_inc(w1_loaded, 16)
            for dst, src in down_loads(0):
                sp.dma_start(dst, src).then_inc(w2_loaded, 16)

        norm(first_loads)

        with nc.Block() as block:

            @block.sync
            def _(sp):
                with sp.Fori(0, steps - 1) as e:
                    sp.wait_ge(h_ready, e * U + U)
                    for dst, src in up_loads(e + 1):
                        sp.dma_start(dst, src).then_inc(w1_loaded, 16)
                    sp.wait_ge(down_filled, e * DN + DN)
                    for dst, src in down_loads(e + 1):
                        sp.dma_start(dst, src).then_inc(w2_loaded, 16)

            @block.tensor
            def _(pe):
                route_products(pe)
                pe.wait_ge(ones_ready, 1)
                with pe.Fori(0, steps) as e:
                    pe.wait_ge(w1_loaded, 16 * n_up * e + 16 * n_up)
                    for f in range(chunks):
                        for half in range(2):
                            u = 2 * f + half
                            depth = 2 if gated else 4
                            pe.wait_ge(h_ready, e * U + max(u - depth + 1, 0))
                            for i, w in enumerate((w_a, w_b) if gated else (w_a,)):
                                bank = 2 * (u % 2) + i if gated else u % 4
                                for k in range(DC):
                                    mm = nc.tensor.matmul(env.bank(bank), w[:, k, f * P:(f + 1) * P],
                                                          env.xt[:, k, half * HALF:(half + 1) * HALF],
                                                          start=(k == 0), stop=(k == DC - 1))
                            mm.then_inc(up_filled, 1)
                    pe.wait_ge(w2_loaded, 16 * n_down * e + 16 * n_down)
                    for g in range(group):
                        for t in range(NT):
                            d = NT * g + t
                            last = U if group == 1 else 2 * g + t // 4 + 1
                            pe.wait_ge(h_ready, e * U + last)
                            pe.wait_ge(down_free, e * DN + max(d - 3, 0))
                            if d == 3:
                                pe.wait_ge(logits_gone, 1)
                            out = env.psum[:, 4 + d % 4, 0:D]
                            for k in range(per):
                                mm = nc.tensor.matmul(out, hidden[:, g * per + k, t * P:(t + 1) * P],
                                                      w_2[:, g * per + k, :],
                                                      start=(k == 0), stop=(k == per - 1 and not bias_down))
                            if bias_down:
                                mm = nc.tensor.matmul(out, ones[:, :], b_down[:, :], start=False, stop=True)
                            mm.then_inc(down_filled, 1)

            @block.scalar
            def _(act):
                route_exponentials(act)
                with act.Fori(0, steps) as e:
                    if n_bias:
                        act.wait_ge(w1_loaded, 16 * n_up * e + 16 * n_up)
                    for f in range(chunks):
                        for half in range(2):
                            u = 2 * f + half
                            act.wait_ge(up_filled, e * U + u + 1)
                            bank = 2 * (u % 2) if gated else u % 4
                            nc.scalar.activation(hidden[:, f, half * HALF:(half + 1) * HALF], env.bank(bank), func,
                                                 bias=b_up[:, 0, f:f + 1] if n_bias else 0.0
                                                 ).then_inc(act_ready if gated else h_ready, 1)

            @block.vector
            def _(dve):
                nc.vector.memset(ones[:, :], 1.0).then_inc(ones_ready, 1)
                choose(dve)
                with dve.Fori(0, steps) as e:
                    if gated:
                        for f in range(chunks):
                            for half in range(2):
                                u = 2 * f + half
                                here = hidden[:, f, half * HALF:(half + 1) * HALF]
                                dve.wait_ge(act_ready, e * U + u + 1)
                                if n_bias:
                                    nc.vector.scalar_tensor_tensor(here, env.bank(2 * (u % 2) + 1),
                                                                   b_up[:, 1, f:f + 1], here,
                                                                   ALU.add, ALU.mult).then_inc(h_ready, 1)
                                else:
                                    nc.vector.tensor_tensor(here, env.bank(2 * (u % 2) + 1), here,
                                                            ALU.mult).then_inc(h_ready, 1)
                    dve.wait_ge(down_free, e * DN)
                    nc.vector.tensor_copy(column[:, :, :], combine[:, :, bass.ds(e * group, group)]
                                          ).then_inc(column_s, 1)
                    dve.wait_ge(column_s, e + 1)
                    for g in range(group):
                        dve.wait_ge(down_free, e * DN + NT * g)
                        for t in range(NT):
                            d = NT * g + t
                            dve.wait_ge(down_filled, e * DN + d + 1)
                            nc.vector.scalar_tensor_tensor(env.x[:, t, :], env.psum[:, 4 + d % 4, 0:D],
                                                           column[:, t, g:g + 1], env.x[:, t, :],
                                                           ALU.mult, ALU.add).then_inc(down_free, 1)


def l0_ffn(env):
    expert_ffn(env, lambda early: normalise(env, env.x, early=early), "groups", 16, 18, 6, 6, ACT.Silu,
               "l0f_router", "l0f_bias", "l0f_gate", "l0f_up", "l0f_down", None, None)


def l2_ffn(env):
    expert_ffn(env, lambda early: normalise(env, env.x, early=early), "probs", 8, 8, 1, 8, ACT.Gelu,
               "l2f_router", None, "l2f_w1", None, "l2f_w2", ["l2f_b1"], "l2f_b2")


def l3_ffn(env):

    def norm(early):
        normalise(env, env.x, transpose=False, early=early)
        normalise(env, env.xn, gain="l3f_ln_w", rms=True, eps=float(np.finfo(np.float32).eps))

    expert_ffn(env, norm, "logits", 8, 8, 1, 8, ACT.Silu, "l3f_router", "l3f_bias", "l3f_w1a", "l3f_w1b", "l3f_w2",
               ["l3f_b1a", "l3f_b1b"], "l3f_b2")


def l1_attn(env):
    nc = env.nc
    normalise(env, env.x)
    LAT = 64
    R = HEADS // 2
    filled, taken_a, taken_d, loaded = (env.sem(n) for n in ("filled", "taken_act", "taken_dve", "loaded"))
    lat_filled, lat_taken = env.sem("latent_filled"), env.sem("latent_taken")
    up_filled, up_a, up_d = env.sem("up_filled"), env.sem("up_taken_act"), env.sem("up_taken_dve")
    qd_ready, scored, decayed, shifted = (env.sem(n) for n in ("qd_ready", "scored", "decayed", "shifted"))
    turn_start = env.sem("turn_start")
    exp_done, turned, turned_taken, pv_done, o_taken, chain_s = (
        env.sem(n) for n in ("exp_done", "turned", "turned_taken", "pv_done", "o_taken", "chain"))
    with ExitStack() as ctx:
        def sb(name, shape, dtype=F32):
            return env.sbuf(name, shape, dtype, ctx)

        w_q, w_k, w_v, w_o = (sb(n, [P, DC, D]) for n in ("w_q", "w_k", "w_v", "w_o"))
        w_down = sb("w_down", [P, DC, LAT])
        w_up_k, w_up_v = sb("w_up_k", [LAT, D]), sb("w_up_v", [LAT, D])
        head_mask, decay = sb("head_mask", [P, 8]), sb("decay", [P, S])
        q_t, kv_t, k_t = (sb(n, [P, DC, T]) for n in ("q_t", "kv_t", "k_t"))
        lat_t = sb("lat_t", [LAT, T])
        v = sb("v", [S, B, D])
        q_diag = sb("q_diag", [P, 2, DC, 8, S])
        sc, probs = sb("sc", [P, 2, R, S]), sb("probs", [P, 2, R, S])
        probs_t = sb("probs_t", [S, 2, R, P])
        peak, total, inverse = (sb(n, [P, 2, R]) for n in ("peak", "total", "inverse"))
        o_rows = sb("o_rows", [S, B, D])
        loads = [(w_q[:, :, :], "l1a_wq"), (w_k[:, :, :], "l1a_wk"), (w_v[:, :, :], "l1a_wv"),
                 (w_down[:, :, :], "l1a_down"), (w_up_k[:, :], "l1a_up_k"), (w_up_v[:, :], "l1a_up_v"),
                 (head_mask[:, :], "pair_mask"), (decay[:, :], "decay"), (w_o[:, :, :], "l1a_wo")]

        with nc.Block() as block:

            @block.sync
            def _(sp):
                for dst, src in loads:
                    sp.dma_start(dst, env.dram[src]).then_inc(loaded, 16)

            @block.tensor
            def _(pe):
                pe.wait_ge(loaded, 16 * len(loads))
                for i, ws in enumerate(((w_q,), (w_k, w_v))):
                    for m in range(DC):
                        for h in range(2):
                            parts = [(w, k) for w in ws for k in range(DC)]
                            for n, (w, k) in enumerate(parts):
                                mm = nc.tensor.matmul(env.bank(4 * i + 2 * m + h), w[:, k, m * P:(m + 1) * P],
                                                      env.xt[:, k, h * HALF:(h + 1) * HALF],
                                                      start=(n == 0), stop=(n == len(parts) - 1))
                            mm.then_inc(filled, 1)
                pe.wait_ge(taken_d, 4)
                for h in range(2):
                    pe.wait_ge(taken_a, h + 1)
                    for k in range(DC):
                        mm = nc.tensor.matmul(env.psum[0:LAT, h, :], w_down[:, k, :], kv_t[:, k, h * HALF:(h + 1) * HALF],
                                              start=(k == 0), stop=(k == DC - 1))
                    mm.then_inc(lat_filled, 1)
                pe.wait_ge(taken_a, 4)
                pe.wait_ge(lat_taken, 2)
                for m in range(DC):
                    for h in range(2):
                        nc.tensor.matmul(env.bank(2 + 2 * m + h), w_up_k[:, m * P:(m + 1) * P],
                                         lat_t[:, h * HALF:(h + 1) * HALF], start=True, stop=True
                                         ).then_inc(up_filled, 1)
                for i in range(B // 2):
                    if i >= 4:
                        pe.wait_ge(up_d, i - 3)
                    for b in (2 * i, 2 * i + 1):
                        mm = nc.tensor.matmul(env.psum[0:S, (6 + i % 4) % 8, (b % 2) * D:(b % 2 + 1) * D],
                                              lat_t[:, b * S:(b + 1) * S], w_up_v[:, :], start=True, stop=True)
                    mm.then_inc(up_filled, 1)

            @block.scalar
            def _(act):
                for n in range(4):
                    act.wait_ge(filled, n + 1)
                    nc.scalar.copy(q_t[:, n // 2, n % 2 * HALF:(n % 2 + 1) * HALF], env.bank(n)).then_inc(taken_a, 1)
                for h in range(2):
                    act.wait_ge(lat_filled, h + 1)
                    nc.scalar.copy(lat_t[:, h * HALF:(h + 1) * HALF], env.psum[0:LAT, h, :]).then_inc(lat_taken, 1)
                for n in range(4):
                    act.wait_ge(up_filled, n + 1)
                    nc.scalar.copy(k_t[:, n // 2, n % 2 * HALF:(n % 2 + 1) * HALF], env.bank(2 + n)).then_inc(up_a, 1)

            @block.vector
            def _(dve):
                for n in range(4):
                    dve.wait_ge(filled, 4 + n + 1)
                    nc.vector.tensor_copy(kv_t[:, n // 2, n % 2 * HALF:(n % 2 + 1) * HALF],
                                          env.bank(4 + n)).then_inc(taken_d, 1)
                for i in range(B // 2):
                    dve.wait_ge(up_filled, 4 + i + 1)
                    nc.vector.tensor_copy(v[:, 2 * i:2 * i + 2, :],
                                          env.psum[0:S, (6 + i % 4) % 8, :].rearrange("p (b d) -> p b d", b=2)
                                          ).then_inc(up_d, 1)

        L = 3
        with nc.Block() as block:

            @block.gpsimd
            def _(pool):
                with pool.Fori(0, B // 2) as i:
                    for e in range(2):
                        pool.wait_ge(scored, 2 * i)
                        for c in range(DC):
                            now = q_t[:, c, bass.ds(i * (2 * S) + e * S, S)]
                            nc.gpsimd.tensor_tensor(q_diag[:, e, c, :, :], now[:, None, :].to_broadcast([P, 8, S]),
                                                    head_mask[:, :, None].to_broadcast([P, 8, S]), ALU.mult
                                                    ).then_inc(qd_ready, 1)

            @block.tensor
            def _(pe):
                with pe.Fori(0, B // 2) as i:
                    for e in range(2):
                        pe.wait_ge(qd_ready, i * 4 + 2 * e + 2)
                        pe.wait_ge(decayed, 2 * i)
                        for r in range(R):
                            pair = slice(2 * (r % 4), 2 * (r % 4) + 2)
                            mm = nc.tensor.matmul(env.psum[:, e, r * S:(r + 1) * S],
                                                  q_diag[:, e, r // 4, pair, :].rearrange("p s q -> p (s q)"),
                                                  k_t[:, r // 4, bass.ds(i * (2 * S) + e * S, S)],
                                                  start=True, stop=True)
                        mm.then_inc(scored, 1)
                    for e in range(2):
                        pe.wait_ge(exp_done, 2 * i + e + 1)
                        pe.wait_ge(turned_taken, 2 * i)
                        pe.sem_inc(turn_start, 1)
                        for r in range(R):
                            mm = nc.tensor.transpose(env.psum[0:S, 2 + 2 * e + r // 4, r % 4 * P:(r % 4 + 1) * P],
                                                     probs[:, e, r, :], env.ident[:, :])
                        mm.then_inc(turned, 1)
                    for e in range(2):
                        pe.wait_ge(turned_taken, 2 * i + e + 1)
                        pe.wait_ge(o_taken, 2 * i)
                        for r in range(R):
                            mm = nc.tensor.matmul(env.psum[:, 6 + e, r * 32:(r + 1) * 32], probs_t[:, e, r, :],
                                                  v[:, bass.ds(2 * i + e, 1), r * 32:(r + 1) * 32].rearrange(
                                                      "p o w -> p (o w)"), start=True, stop=True)
                        mm.then_inc(pv_done, 1)

            @block.scalar
            def _(act):
                with act.Fori(0, B // 2) as i:
                    for e in range(2):
                        act.wait_ge(shifted, 2 * i + e + 1)
                        act.wait_ge(turned, 2 * i)
                        nc.scalar.activation(probs[:, e, :, :], sc[:, e, :, :], ACT.Exp).then_inc(exp_done, 1)
                    for e in range(2):
                        act.wait_ge(turned, 2 * i + e + 1)
                        act.wait_ge(pv_done, 2 * i)
                        nc.scalar.copy(probs_t[:, e, :, :].rearrange("p r n -> p (r n)"),
                                       env.psum[0:S, 2 + 2 * e:4 + 2 * e, :].rearrange("p k n -> p (k n)")
                                       ).then_inc(turned_taken, 1)

            @block.vector
            def _(dve):
                with dve.Fori(0, B // 2) as i:
                    chain = Chain(dve, chain_s, i * (2 * L))
                    full = [P, R, S]
                    for e in range(2):
                        dve.wait_ge(scored, 2 * i + e + 1)
                        dve.wait_ge(exp_done, 2 * i)
                        nc.vector.tensor_tensor(sc[:, e, :, :], env.psum[:, e, :].rearrange("p (r m) -> p r m", r=R),
                                                decay[:, None, :].to_broadcast(full), ALU.mult).then_inc(decayed, 1)
                        dve.wait_ge(decayed, 2 * i + e + 1)
                        chain(nc.vector.tensor_reduce(peak[:, e, :], sc[:, e, :, :], AX.X, ALU.max))
                        nc.vector.tensor_tensor(sc[:, e, :, :], sc[:, e, :, :],
                                                peak[:, e, :, None].to_broadcast(full), ALU.subtract
                                                ).then_inc(shifted, 1)
                    for e in range(2):
                        dve.wait_ge(exp_done, 2 * i + e + 1)
                        dve.wait_ge(o_taken, 2 * i)
                        chain(nc.vector.tensor_reduce(total[:, e, :], probs[:, e, :, :], AX.X, ALU.add))
                        chain(nc.vector.reciprocal(inverse[:, e, :], total[:, e, :]))
                    for e in range(2):
                        dve.wait_ge(pv_done, 2 * i + e + 1)
                        out = o_rows[:, bass.ds(2 * i + e, 1), :].rearrange("p o (r s w) -> p (o r) s w", s=2, w=HD)
                        o_psum = env.psum[:, 6 + e, 0:D].rearrange("p (r w) -> p r w", r=R)
                        nc.vector.tensor_tensor(out[:, :, 0, :], o_psum[0:S, :, 0:HD],
                                                inverse[0:S, e, :, None].to_broadcast([S, R, HD]), ALU.mult)
                        nc.vector.tensor_tensor(out[:, :, 1, :], o_psum[S:P, :, HD:2 * HD],
                                                inverse[S:P, e, :, None].to_broadcast([S, R, HD]), ALU.mult
                                                ).then_inc(o_taken, 1)

        add_projected(env, o_rows, w_o)


def l2_attn(env):
    nc = env.nc
    normalise(env, env.x, transpose=False)
    base_loaded, loaded = env.sem("base_loaded"), env.sem("loaded")
    b_out_s, filled, u_ready, om_ready = (env.sem(n) for n in ("x_based", "filled", "gates_ready", "rest_ready"))
    summed, squashed, stepped, kept, mixed = (env.sem(n) for n in ("summed", "squashed", "stepped", "kept", "mixed"))
    out_filled, out_free = env.sem("out_filled"), env.sem("out_free")
    with ExitStack() as ctx:
        def sb(name, shape, dtype=F32):
            return env.sbuf(name, shape, dtype, ctx)

        b_out = sb("b_out", [P, D])
        with nc.Block() as block:

            @block.sync
            def _(sp):
                sp.dma_start(b_out[:, :], env.dram["l2a_b_out"].partition_broadcast(P)).then_inc(base_loaded, 16)

            @block.vector
            def _(dve):
                for t in range(NT):
                    nc.vector.tensor_tensor(env.x[:, t, :], env.x[:, t, :], env.xn[:, t, :],
                                            ALU.add).then_inc(b_out_s, 1)
                dve.wait_ge(base_loaded, 16)
                for t in range(NT):
                    dve.wait_ge(b_out_s, t + 1)
                    nc.vector.tensor_tensor(env.x[:, t, :], env.x[:, t, :], b_out[:, :], ALU.add)

        w_in, w_out = sb("w_in", [P, DC, 2 * D]), sb("w_out", [P, DC, D])
        b_in, a_col = sb("b_in", [P, 4]), sb("a_col", [P, DC])
        u, g, rest, hs = (sb(n, [P, DC, T]) for n in ("u", "g", "rest", "hs"))
        arg, squash, keep, mix = (sb(n, [P, DC, B]) for n in ("arg", "squash", "keep", "mix"))
        loads = [(w_in[:, :, :], "l2a_w_in"), (b_in[:, :], "l2a_b_in"), (a_col[:, :], "l2a_a"),
                 (w_out[:, :, :], "l2a_w_out")]

        def first_loads(sp):
            for dst, src in loads:
                sp.dma_start(dst, env.dram[src]).then_inc(loaded, 16)

        normalise(env, env.xn, gain="l2a_gamma", shift="l2a_beta", early=first_loads)

        def at(x, t):
            return x[:, :, :].rearrange("p c (b s) -> p c b s", s=S)[:, :, :, bass.ds(t, 1)].rearrange(
                "p c b o -> p c (b o)")

        with nc.Block() as block:

            @block.tensor
            def _(pe):
                pe.wait_ge(loaded, 16 * len(loads))
                for m in range(4):
                    for h in range(2):
                        for k in range(DC):
                            mm = nc.tensor.matmul(env.bank(2 * m + h), w_in[:, k, m * P:(m + 1) * P],
                                                  env.xt[:, k, h * HALF:(h + 1) * HALF],
                                                  start=(k == 0), stop=(k == DC - 1))
                        mm.then_inc(filled, 1)
                pe.wait_ge(stepped, S)
                for t in range(NT):
                    if t >= 4:
                        pe.wait_ge(out_free, t - 3)
                    for k in range(DC):
                        mm = nc.tensor.matmul(env.psum[:, t % 4, 0:D], hs[:, k, t * P:(t + 1) * P], w_out[:, k, :],
                                              start=(k == 0), stop=(k == DC - 1))
                    mm.then_inc(out_filled, 1)

            @block.scalar
            def _(act):
                act.wait_ge(loaded, 16 * len(loads))
                for m in range(4):
                    for h in range(2):
                        act.wait_ge(filled, 2 * m + h + 1)
                        dst = (u, g)[m // 2]
                        nc.scalar.activation(dst[:, m % 2, h * HALF:(h + 1) * HALF], env.bank(2 * m + h),
                                             (ACT.Identity, ACT.Sigmoid)[m // 2], bias=b_in[:, m:m + 1]
                                             ).then_inc(u_ready, 1)
                act.wait_ge(u_ready, 8)
                nc.scalar.activation(squash[:, :, :], at(u, 0), ACT.Tanh).then_inc(squashed, 1)
                with act.Fori(1, S) as t:
                    act.wait_ge(summed, 2 * t)
                    nc.scalar.activation(squash[:, :, :], arg[:, :, :], ACT.Tanh).then_inc(squashed, 1)

            @block.vector
            def _(dve):
                dve.wait_ge(u_ready, 8)
                for c in range(DC):
                    nc.vector.tensor_scalar(rest[:, c, :], g[:, c, :], -1.0, 1.0, ALU.mult, ALU.add
                                            ).then_inc(om_ready, 1)
                dve.wait_ge(om_ready, 2)
                dve.wait_ge(squashed, 1)
                nc.vector.tensor_tensor(at(hs, 0), at(rest, 0), squash[:, :, :], ALU.mult).then_inc(stepped, 1)
                with dve.Fori(1, S) as t:
                    dve.wait_ge(stepped, t)
                    for c in range(DC):
                        nc.vector.scalar_tensor_tensor(arg[:, c, :], at(hs, t - 1)[:, c, :], a_col[:, c:c + 1],
                                                       at(u, t)[:, c, :], ALU.mult, ALU.add).then_inc(summed, 1)
                    nc.vector.tensor_tensor(keep[:, :, :], at(g, t), at(hs, t - 1), ALU.mult).then_inc(kept, 1)
                    dve.wait_ge(squashed, t + 1)
                    nc.vector.tensor_tensor(mix[:, :, :], at(rest, t), squash[:, :, :], ALU.mult).then_inc(mixed, 1)
                    dve.wait_ge(mixed, t)
                    dve.wait_ge(kept, t)
                    nc.vector.tensor_tensor(at(hs, t), mix[:, :, :], keep[:, :, :], ALU.add).then_inc(stepped, 1)
                for t in range(NT):
                    dve.wait_ge(out_filled, t + 1)
                    nc.vector.tensor_tensor(env.x[:, t, :], env.x[:, t, :], env.psum[:, t % 4, 0:D],
                                            ALU.add).then_inc(out_free, 1)


def l1_ffn(env):
    nc = env.nc
    normalise(env, env.x, transpose=False)
    MAGIC = 1.5 * 2.0 ** 23
    FF = 4 * D
    FC = FF // P
    loaded, chain_s, w_chain = env.sem("loaded"), env.sem("chain"), env.sem("weight_chain")
    summed, sum_filled, w_ready, x_ready = (env.sem(n) for n in ("summed", "sum_filled", "weights_ready", "x_ready"))
    x_turned, x_taken, up_filled, scaled, conv_s, conved, h_ready, ones_ready = (
        env.sem(n) for n in ("x_turned", "x_taken", "up_filled", "scaled", "conv_step", "conved", "h_ready",
                             "ones_ready"))
    turned, quantised, int_turned, int_taken, out_filled, added, q_chain = (
        env.sem(n) for n in ("turned", "quantised", "int_turned", "int_taken", "out_filled", "added", "quant_chain"))
    with ExitStack() as ctx:
        def sb(name, shape, dtype=F32):
            return env.sbuf(name, shape, dtype, ctx)

        w1, w2 = sb("w1", [P, DC, FF]), sb("w2", [P, FC, D])
        w2_int = sb("w2_int", [P, FC, D], BF16)
        ident_b = sb("ident_bf16", [P, P], BF16)
        ones = sb("ones", [P, P])
        conv_w, conv_b = sb("conv_w", [P, FC, 3]), sb("conv_b", [P, FC])
        w_sum = sb("w_sum", [P, 2])
        w_mean, w_scale = sb("w_mean", [P, 2]), sb("w_scale", [P, 2])
        peak, scale, inv = sb("peak", [P, NT]), sb("scale", [P, NT]), sb("inv", [P, NT])
        hidden = sb("hidden", [P, FC, T])
        conv = sb("conv", [P, 2, HALF])
        h_peak, h_scale, h_inv = sb("h_peak", [P, NT]), sb("h_scale", [P, NT]), sb("h_inv", [P, NT])
        h_round = sb("h_round", [P, 2, FF])
        h_int = sb("h_int", [P, 2, FF], BF16)
        h_int_t = sb("h_int_t", [P, 2, FC, P], BF16)
        loads = [(w1[:, :, :], "l1f_w1"), (w2[:, :, :], "l1f_w2"), (conv_w[:, :, :], "l1f_conv_w"),
                 (conv_b[:, :], "l1f_conv_b")]

        def quantise_scale(chain, peak, scale, inv):
            chain(nc.vector.tensor_scalar(peak, peak, 1e-5, None, ALU.max))
            chain(nc.vector.reciprocal(scale, peak))
            chain(nc.vector.tensor_scalar(scale, scale, 127.0, None, ALU.mult))
            chain(nc.vector.tensor_scalar(inv, peak, 1.0 / 127.0, None, ALU.mult))

        with nc.Block() as block:

            @block.sync
            def _(sp):
                for dst, src in loads:
                    sp.dma_start(dst, env.dram[src]).then_inc(loaded, 16)

            @block.gpsimd
            def _(pool):
                nc.gpsimd.memset(ones[:, :], 1.0).then_inc(ones_ready, 1)
                nc.gpsimd.tensor_copy(ident_b[:, :], env.ident[:, :]).then_inc(ones_ready, 1)

            @block.vector
            def _(dve):
                chain = Chain(dve, chain_s)
                chain(nc.vector.tensor_reduce(peak[:, :], env.xn[:, :, :], AX.X, ALU.max, apply_absolute_value=True))
                quantise_scale(chain, peak[:, :], scale[:, :], inv[:, :])
                for step in range(3):
                    for t in range(NT):
                        row = env.xn[:, t, :]
                        if step == 0:
                            ins = nc.vector.tensor_scalar(row, row, scale[:, t:t + 1], MAGIC, ALU.mult, ALU.add)
                        elif step == 1:
                            ins = nc.vector.tensor_scalar(row, row, MAGIC + 127.0, MAGIC - 128.0, ALU.min, ALU.max)
                        else:
                            ins = nc.vector.tensor_scalar(row, row, MAGIC, inv[:, t:t + 1], ALU.subtract, ALU.mult)
                        ins.then_inc(chain_s if step < 2 else x_ready, 1)
                    if step < 2:
                        chain.n += NT
                        dve.wait_ge(chain_s, chain.n)
                dve.wait_ge(loaded, 16 * len(loads))
                for i, w in enumerate((w1, w2)):
                    nc.vector.tensor_reduce(w_sum[:, i:i + 1], w[:, :, :].rearrange("p a b -> p (a b)"), AX.X, ALU.add,
                                            apply_absolute_value=True).then_inc(summed, 1)
                dve.wait_ge(sum_filled, 1)
                chain(nc.vector.tensor_scalar(w_mean[:, :], env.psum[:, 7, 0:2], 1.0 / (D * FF), 1e-5, ALU.mult, ALU.max))
                chain(nc.vector.reciprocal(w_scale[:, :], w_mean[:, :]))
                for i, (w, out) in enumerate(((w1[:, :, :], w1[:, :, :]), (w2[:, :, :], w2_int[:, :, :]))):
                    chain(nc.vector.tensor_scalar(w, w, w_scale[:, i:i + 1], MAGIC, ALU.mult, ALU.add))
                    chain(nc.vector.tensor_scalar(w, w, MAGIC, 1.0, ALU.subtract, ALU.min))
                    nc.vector.tensor_scalar(out, w, -1.0, None, ALU.max).then_inc(w_ready, 1)
                nc.vector.tensor_scalar(conv_w[:, :, :], conv_w[:, :, :], w_mean[:, 0:1], None, ALU.mult
                                        ).then_inc(w_ready, 1)

            @block.tensor
            def _(pe):
                pe.wait_ge(summed, 2)
                pe.wait_ge(ones_ready, 2)
                nc.tensor.matmul(env.psum[:, 7, 0:2], ones[:, :], w_sum[:, :], start=True, stop=True
                                 ).then_inc(sum_filled, 1)
                for t in range(NT):
                    pe.wait_ge(x_ready, t + 1)
                    if t >= 4:
                        pe.wait_ge(x_taken, t - 3)
                    for c in range(DC):
                        mm = nc.tensor.transpose(env.psum[:, t % 4, c * P:(c + 1) * P], env.xn[:, t, c * P:(c + 1) * P],
                                                 env.ident[:, :])
                    mm.then_inc(x_turned, 1)

            @block.scalar
            def _(act):
                for t in range(NT):
                    act.wait_ge(x_turned, t + 1)
                    nc.scalar.copy(env.xt[:, :, t * P:(t + 1) * P],
                                   env.psum[:, t % 4, 0:D].rearrange("p (c n) -> p c n", c=DC)).then_inc(x_taken, 1)

        with nc.Block() as block:

            @block.tensor
            def _(pe):
                for n in range(2 * FC):
                    f, h = n // 2, n % 2
                    if n >= 4:
                        pe.wait_ge(conved, n - 3)
                    for k in range(DC):
                        mm = nc.tensor.matmul(env.bank(n % 4), w1[:, k, f * P:(f + 1) * P],
                                              env.xt[:, k, h * HALF:(h + 1) * HALF], start=(k == 0), stop=(k == DC - 1))
                    mm.then_inc(up_filled, 1)

            @block.vector
            def _(dve):
                chain = Chain(dve, conv_s)
                for n in range(2 * FC):
                    f = n // 2
                    rows = env.bank(n % 4).rearrange("p (b s) -> p b s", s=S)
                    out = conv[:, n % 2, :].rearrange("p (b s) -> p b s", s=S)
                    dve.wait_ge(up_filled, n + 1)
                    if n >= 2:
                        dve.wait_ge(h_ready, n - 1)
                    chain(nc.vector.tensor_scalar(out, rows, conv_w[:, f, 1:2], conv_b[:, f:f + 1], ALU.mult, ALU.add))
                    chain(nc.vector.scalar_tensor_tensor(out[:, :, 1:S], rows[:, :, 0:S - 1], conv_w[:, f, 0:1],
                                                         out[:, :, 1:S], ALU.mult, ALU.add))
                    nc.vector.scalar_tensor_tensor(out[:, :, 0:S - 1], rows[:, :, 1:S], conv_w[:, f, 2:3],
                                                   out[:, :, 0:S - 1], ALU.mult, ALU.add).then_inc(conved, 1)

            @block.scalar
            def _(act):
                for n in range(2 * FC):
                    act.wait_ge(conved, n + 1)
                    nc.scalar.activation(hidden[:, n // 2, n % 2 * HALF:(n % 2 + 1) * HALF], conv[:, n % 2, :],
                                         ACT.Silu).then_inc(h_ready, 1)

        with nc.Block() as block:

            @block.tensor
            def _(pe):
                def forth(t):
                    if t >= 2:
                        pe.wait_ge(quantised, 3 * (t - 1) - 2)
                    for f in range(FC):
                        mm = nc.tensor.transpose(env.psum[:, 2 * (t % 2) + f // 4, f % 4 * P:(f % 4 + 1) * P],
                                                 hidden[:, f, t * P:(t + 1) * P], env.ident[:, :])
                    mm.then_inc(turned, 1)

                forth(0)
                for t in range(NT):
                    if t + 1 < NT:
                        forth(t + 1)
                    pe.wait_ge(quantised, 3 * t + 3)
                    if t >= 2:
                        pe.wait_ge(int_taken, t - 1)
                    ints = env.psum[:, 4 + t % 2, :].bitcast(BF16)
                    for f in range(FC):
                        mm = nc.tensor.transpose(ints[:, f * P:(f + 1) * P], h_int[:, t % 2, f * P:(f + 1) * P],
                                                 ident_b[:, :])
                    mm.then_inc(int_turned, 1)
                    pe.wait_ge(int_taken, t + 1)
                    if t >= 2:
                        pe.wait_ge(added, t - 1)
                    for k in range(FC):
                        mm = nc.tensor.matmul(env.psum[:, 6 + t % 2, 0:D], h_int_t[:, t % 2, k, :], w2_int[:, k, :],
                                              start=(k == 0), stop=(k == FC - 1))
                    mm.then_inc(out_filled, 1)

            @block.scalar
            def _(act):
                for t in range(NT):
                    act.wait_ge(int_turned, t + 1)
                    if t >= 2:
                        act.wait_ge(out_filled, t - 1)
                    nc.scalar.copy(h_int_t[:, t % 2, :, :].rearrange("p f n -> p (f n)"),
                                   env.psum[:, 4 + t % 2, :].bitcast(BF16)).then_inc(int_taken, 1)

            @block.vector
            def _(dve):
                chain = Chain(dve, q_chain)

                def add(t):
                    dve.wait_ge(out_filled, t + 1)
                    nc.vector.scalar_tensor_tensor(env.x[:, t, :], env.psum[:, 6 + t % 2, 0:D], h_inv[:, t:t + 1],
                                                   env.x[:, t, :], ALU.mult, ALU.add).then_inc(added, 1)

                for t in range(NT):
                    one = slice(t, t + 1)
                    rows = env.psum[:, 2 * (t % 2):2 * (t % 2) + 2, :].rearrange("p k n -> p (k n)")
                    dve.wait_ge(turned, t + 1)
                    chain(nc.vector.tensor_reduce(h_peak[:, one], rows, AX.X, ALU.max, apply_absolute_value=True))
                    quantise_scale(chain, h_peak[:, one], h_scale[:, one], h_inv[:, one])
                    chain(nc.vector.tensor_scalar(h_inv[:, one], h_inv[:, one], w_mean[:, 1:2], None, ALU.mult))
                    if t >= 2:
                        dve.wait_ge(int_turned, t - 1)
                    buf = h_round[:, t % 2, :]
                    nc.vector.tensor_scalar(buf, rows, h_scale[:, one], MAGIC, ALU.mult, ALU.add).then_inc(quantised, 1)
                    dve.wait_ge(quantised, 3 * t + 1)
                    nc.vector.tensor_scalar(buf, buf, MAGIC + 127.0, MAGIC - 128.0, ALU.min, ALU.max
                                            ).then_inc(quantised, 1)
                    dve.wait_ge(quantised, 3 * t + 2)
                    nc.vector.tensor_scalar(h_int[:, t % 2, :], buf, MAGIC, None, ALU.subtract).then_inc(quantised, 1)
                    if t >= 1:
                        add(t - 1)
                add(NT - 1)


def l3_attn(env):
    nc = env.nc
    normalise(env, env.x)
    DI = 2 * D
    IC = DI // P
    N = 16
    TAPS = 4
    B_AT, C_AT, XD = 32, 64, 80
    sem = env.sem
    with ExitStack() as ctx:
        def sb(name, shape, dtype=F32, into=ctx):
            return env.sbuf(name, shape, dtype, into)

        u, gate, delta, du, y = (sb(n, [P, IC, T]) for n in ("u", "gate", "delta", "du", "y"))
        neg_a, neg_a_t = sb("neg_a", [P, IC, N]), sb("neg_a_t", [XD, DI])
        d_col = sb("d_col", [P, IC])
        x_dbl = sb("x_dbl", [XD, T])
        small_loaded, a_ready = sem("small_loaded"), sem("a_ready")

        with ExitStack() as inner:
            w_in = sb("w_in", [P, DC, 2 * DI], into=inner)
            conv_w, conv_b = sb("conv_w", [P, IC, TAPS], into=inner), sb("conv_b", [P, IC], into=inner)
            w_x = sb("w_x", [P, IC, XD], into=inner)
            conv = sb("conv", [P, 2, HALF], into=inner)
            w_dt, b_dt = sb("w_dt", [N, DI], into=inner), sb("b_dt", [P, IC], into=inner)
            loaded, filled, conv_s, conved, u_ready, gated = (
                sem(n) for n in ("loaded", "filled", "conv_chain", "conved", "u_ready", "gated"))
            dbl_filled, dbl_ready = sem("dbl_filled"), sem("dbl_ready")
            loads = [(w_in[:, :, :], "l3a_w_in"), (conv_w[:, :, :], "l3a_conv_w"), (conv_b[:, :], "l3a_conv_b"),
                     (w_x[:, :, :], "l3a_w_x"), (w_dt[:, :], "l3a_w_dt"), (b_dt[:, :], "l3a_b_dt"),
                     (d_col[:, :], "l3a_d"), (neg_a[:, :, :], "l3a_a"), (neg_a_t[C_AT:C_AT + N, :], "l3a_a_t")]
            with nc.Block() as block:

                @block.sync
                def _(sp):
                    for dst, src in loads:
                        sp.dma_start(dst, env.dram[src]).then_inc(loaded, 16)

                @block.tensor
                def _(pe):
                    pe.wait_ge(loaded, 16 * len(loads))
                    for n in range(2 * IC):
                        for part in range(2):
                            if n >= 4:
                                pe.wait_ge((conved, gated)[part], n - 3)
                            m, h = IC * part + n // 2, n % 2
                            for k in range(DC):
                                mm = nc.tensor.matmul(env.bank(4 * part + n % 4), w_in[:, k, m * P:(m + 1) * P],
                                                      env.xt[:, k, h * HALF:(h + 1) * HALF],
                                                      start=(k == 0), stop=(k == DC - 1))
                            mm.then_inc(filled, 1)
                    pe.wait_ge(gated, 2 * IC)
                    pe.wait_ge(u_ready, 2 * IC)
                    for h in range(2):
                        for k in range(IC):
                            mm = nc.tensor.matmul(env.psum[0:XD, 4 + h, :], w_x[:, k, :], u[:, k, h * HALF:(h + 1) * HALF],
                                                  start=(k == 0), stop=(k == IC - 1))
                        mm.then_inc(dbl_filled, 1)

                @block.vector
                def _(dve):
                    chain = Chain(dve, conv_s)
                    dve.wait_ge(loaded, 16 * len(loads))
                    for n in range(2 * IC):
                        f = n // 2
                        rows = env.bank(n % 4).rearrange("p (b s) -> p b s", s=S)
                        out = conv[:, n % 2, :].rearrange("p (b s) -> p b s", s=S)
                        dve.wait_ge(filled, 2 * n + 1)
                        if n >= 2:
                            dve.wait_ge(u_ready, n - 1)
                        chain(nc.vector.tensor_scalar(out, rows, conv_w[:, f, TAPS - 1:TAPS], conv_b[:, f:f + 1],
                                                      ALU.mult, ALU.add))
                        for back in range(1, TAPS):
                            ins = nc.vector.scalar_tensor_tensor(
                                out[:, :, back:S], rows[:, :, 0:S - back], conv_w[:, f, TAPS - 1 - back:TAPS - back],
                                out[:, :, back:S], ALU.mult, ALU.add)
                            if back < TAPS - 1:
                                chain(ins)
                        ins.then_inc(conved, 1)

                @block.scalar
                def _(act):
                    for n in range(2 * IC):
                        here = slice(n % 2 * HALF, (n % 2 + 1) * HALF)
                        act.wait_ge(filled, 2 * n + 2)
                        nc.scalar.activation(gate[:, n // 2, here], env.bank(4 + n % 4), ACT.Silu).then_inc(gated, 1)
                        act.wait_ge(conved, n + 1)
                        nc.scalar.activation(u[:, n // 2, here], conv[:, n % 2, :], ACT.Silu).then_inc(u_ready, 1)
                    for h in range(2):
                        act.wait_ge(dbl_filled, h + 1)
                        nc.scalar.copy(x_dbl[:, h * HALF:(h + 1) * HALF], env.psum[0:XD, 4 + h, :]
                                       ).then_inc(dbl_ready, 1)

            dt_filled, v_ready, abs_ready, e_ready, ln_ready, delta_ready, y_zero = (
                sem(n) for n in ("dt_filled", "v_ready", "abs_ready", "e_ready", "ln_ready", "delta_ready", "y_zero"))
            with nc.Block() as block:

                @block.tensor
                def _(pe):
                    for n in range(2 * IC):
                        nc.tensor.matmul(env.bank(n), w_dt[:, n // 2 * P:(n // 2 + 1) * P],
                                         x_dbl[0:N, n % 2 * HALF:(n % 2 + 1) * HALF], start=True, stop=True
                                         ).then_inc(dt_filled, 1)

                @block.scalar
                def _(act):
                    nc.scalar.activation(neg_a[:, :, :], neg_a[:, :, :], ACT.Exp).then_inc(a_ready, 1)
                    rows = slice(C_AT, C_AT + N)
                    nc.scalar.activation(neg_a_t[rows, :], neg_a_t[rows, :], ACT.Exp).then_inc(a_ready, 1)
                    for n in range(2 * IC):
                        here = slice(n % 2 * HALF, (n % 2 + 1) * HALF)
                        act.wait_ge(dt_filled, n + 1)
                        nc.scalar.activation(delta[:, n // 2, here], env.bank(n), ACT.Identity,
                                             bias=b_dt[:, n // 2:n // 2 + 1]).then_inc(v_ready, 1)
                        nc.scalar.activation(du[:, n // 2, here], env.bank(n), ACT.Abs,
                                             bias=b_dt[:, n // 2:n // 2 + 1]).then_inc(abs_ready, 1)
                    act.wait_ge(abs_ready, 2 * IC)
                    for c in range(IC):
                        nc.scalar.activation(du[:, c, :], du[:, c, :], ACT.Exp, scale=-1.0).then_inc(e_ready, 1)
                    act.wait_ge(e_ready, IC)
                    for c in range(IC):
                        nc.scalar.activation(du[:, c, :], du[:, c, :], ACT.Ln, bias=1.0).then_inc(ln_ready, 1)

                @block.vector
                def _(dve):
                    dve.wait_ge(a_ready, 2)
                    nc.vector.tensor_scalar(neg_a[:, :, :], neg_a[:, :, :], -1.0, None, ALU.mult)
                    rows = slice(C_AT, C_AT + N)
                    nc.vector.tensor_scalar(neg_a_t[rows, :], neg_a_t[rows, :], -1.0, None, ALU.mult)
                    dve.wait_ge(v_ready, 2 * IC)
                    for c in range(IC):
                        dve.wait_ge(ln_ready, c + 1)
                        nc.vector.scalar_tensor_tensor(delta[:, c, :], delta[:, c, :], 0.0, du[:, c, :],
                                                       ALU.max, ALU.add).then_inc(delta_ready, 1)
                        dve.wait_ge(delta_ready, c + 1)
                        nc.vector.tensor_tensor(du[:, c, :], delta[:, c, :], u[:, c, :], ALU.mult)

                @block.gpsimd
                def _(pool):
                    nc.gpsimd.memset(y[:, :, :], 0.0).then_inc(y_zero, 1)

        with ExitStack() as inner:
            eye = sb("eye", [XD, N], into=inner)
            zeros = sb("zeros", [P, B], into=inner)
            zeroed = sem("zeroed")
            pick = sb("pick", [XD, 2, P], into=inner)
            a_now = sb("a_now", [P, 2, IC], into=inner)
            decay = sb("state_decay", [P, 2, T], into=inner)
            grow = sb("state_input", [P, 2, T], into=inner)
            state = sb("state", [P, 2, T], into=inner)
            part = sb("part", [P, 2, T], into=inner)
            eye_loaded, picked, spread, decayed, reset, grown, stepped, parted, added = (
                sem(n) for n in ("eye_loaded", "picked", "spread", "decayed", "reset", "grown", "stepped", "parted",
                                 "added"))
            with nc.Block() as block:

                @block.sync
                def _(sp):
                    sp.dma_start(eye[:, :], env.dram["eye_rows"]).then_inc(eye_loaded, 16)

                UNITS = 2 * IC

                @block.tensor
                def _(pe):

                    def spread_rows(i, e):
                        pe.wait_ge(picked, i * 6 + (3 * e + 3))
                        if not isinstance(i, int):
                            pe.wait_ge(parted, i * UNITS + (e * IC - IC))
                        for j, at in enumerate((B_AT, C_AT)):
                            for h in range(2):
                                mm = nc.tensor.matmul(env.bank(4 * e + 2 * j + h), pick[at:at + N, e, :],
                                                      x_dbl[at:at + N, h * HALF:(h + 1) * HALF],
                                                      start=True, stop=True, tile_position=(at, 0))
                        mm.then_inc(spread, 1)

                    for e in range(2):
                        spread_rows(0, e)
                    with pe.Fori(0, N // 2 - 1) as i:
                        for e in range(2):
                            spread_rows(i + 1, e)

                @block.scalar
                def _(act):
                    act.wait_ge(zeroed, 1)
                    with act.Fori(0, N // 2) as i:
                        for e in range(2):
                            act.wait_ge(picked, i * 6 + (3 * e + 3))
                            for c in range(IC):
                                n = e * IC + c
                                act.wait_ge(stepped, i * UNITS + max(n - 1, 0))
                                nc.scalar.activation(decay[:, n % 2, :], delta[:, c, :], ACT.Exp,
                                                     scale=a_now[:, e, c:c + 1]).then_inc(decayed, 1)
                                act.wait_ge(decayed, i * UNITS + n + 1)
                                nc.scalar.copy(decay[:, n % 2, 0:T:S], zeros[:, :]).then_inc(reset, 1)

                @block.gpsimd
                def _(pool):
                    nc.gpsimd.memset(zeros[:, :], 0.0).then_inc(zeroed, 1)
                    pool.wait_ge(zeroed, 1)
                    with pool.Fori(0, N // 2) as i:
                        for n in range(UNITS):
                            pool.wait_ge(parted, i * UNITS + n + 1)
                            pool.wait_ge(added, i * UNITS + max(n - IC + 1, 0))
                            nc.gpsimd.tensor_tensor(y[:, n % IC, :], y[:, n % IC, :], part[:, n % 2, :],
                                                    ALU.add).then_inc(added, 1)

                @block.vector
                def _(dve):

                    def pick_state(i, e):
                        at_least(dve, spread, i * 2 + (e - 1))
                        at_least(dve, decayed, i * UNITS + (e * IC - IC))
                        state_at = slice(2 * i + e, 2 * i + e + 1) if isinstance(i, int) else bass.ds(2 * i + e, 1)
                        nc.vector.tensor_copy(a_now[:, e, :], neg_a[:, :, state_at].rearrange(
                            "p c o -> p (c o)")).then_inc(picked, 1)
                        for at in (B_AT, C_AT):
                            rows = slice(at, at + N)
                            nc.vector.tensor_copy(pick[rows, e, :], eye[rows, state_at].to_broadcast([N, P])
                                                  ).then_inc(picked, 1)

                    def scan_state(i, e):
                        dve.wait_ge(spread, i * 2 + (e + 1))
                        b_n = env.psum[:, 4 * e:4 * e + 2, :].rearrange("p k n -> p (k n)")
                        c_n = env.psum[:, 4 * e + 2:4 * e + 4, :].rearrange("p k n -> p (k n)")

                        def feed(n):
                            at_least(dve, stepped, i * UNITS + max(n - 1, 0))
                            nc.vector.tensor_tensor(grow[:, n % 2, :], du[:, n % IC, :], b_n, ALU.mult
                                                    ).then_inc(grown, 1)

                        feed(e * IC)
                        for n in range(e * IC, (e + 1) * IC):
                            k = n % 2
                            dve.wait_ge(grown, i * UNITS + n + 1)
                            dve.wait_ge(reset, i * UNITS + n + 1)
                            at_least(dve, parted, i * UNITS + max(n - 1, 0))
                            nc.vector.tensor_tensor_scan(state[:, k, :], decay[:, k, :], grow[:, k, :], 0.0,
                                                         ALU.mult, ALU.add).then_inc(stepped, 1)
                            if n + 1 < (e + 1) * IC:
                                feed(n + 1)
                            dve.wait_ge(stepped, i * UNITS + n + 1)
                            at_least(dve, added, i * UNITS + max(n - 1, 0))
                            nc.vector.tensor_tensor(part[:, k, :], state[:, k, :], c_n, ALU.mult
                                                    ).then_inc(parted, 1)

                    dve.wait_ge(eye_loaded, 16)
                    for e in range(2):
                        pick_state(0, e)
                    with dve.Fori(0, N // 2 - 1) as i:
                        for e in range(2):
                            scan_state(i, e)
                            pick_state(i + 1, e)
                    for e in range(2):
                        scan_state(N // 2 - 1, e)

        w_out1, w_out2 = sb("w_out1", [P, 2 * IC, DI]), sb("w_out2", [P, IC, D])
        d_rep = sb("d_rep", [P, IC, P])
        loaded, rep_ready, mid, gated_y, t_filled, t_taken, h_filled, h_ready, out_filled, added = (
            sem(n) for n in ("loaded", "rep_ready", "mid", "gated_y", "t_filled", "t_taken", "h_filled", "h_ready",
                             "out_filled", "added"))
        y_t, h1 = delta, gate
        with nc.Block() as block:

            @block.sync
            def _(sp):
                sp.dma_start(w_out1[:, :, :], env.dram["l3a_w_out1"]).then_inc(loaded, 16)
                sp.dma_start(w_out2[:, :, :], env.dram["l3a_w_out2"]).then_inc(loaded, 16)

            @block.vector
            def _(dve):
                for c in range(IC):
                    nc.vector.tensor_copy(d_rep[:, c, :], d_col[:, c:c + 1].to_broadcast([P, P])).then_inc(rep_ready, 1)
                for c in range(IC):
                    nc.vector.scalar_tensor_tensor(y[:, c, :], u[:, c, :], d_col[:, c:c + 1], y[:, c, :],
                                                   ALU.mult, ALU.add).then_inc(mid, 1)
                    dve.wait_ge(mid, c + 1)
                    nc.vector.tensor_tensor(y[:, c, :], y[:, c, :], gate[:, c, :], ALU.mult).then_inc(gated_y, 1)
                for t in range(NT):
                    dve.wait_ge(out_filled, t + 1)
                    nc.vector.tensor_tensor(env.x[:, t, :], env.x[:, t, :], env.psum[:, 4 + t % 4, 0:D],
                                            ALU.add).then_inc(added, 1)

            @block.tensor
            def _(pe):
                pe.wait_ge(rep_ready, IC)
                for n in range(2 * IC):
                    m, here = n // 2, slice(n % 2 * HALF, (n % 2 + 1) * HALF)
                    for k in range(IC):
                        nc.tensor.matmul(env.bank(n), d_rep[:, k, :], u[:, k, here], start=(k == 0), stop=False)
                    nc.tensor.matmul(env.bank(n), neg_a_t[C_AT:C_AT + N, m * P:(m + 1) * P], x_dbl[C_AT:C_AT + N, here],
                                     start=False, stop=True, tile_position=(C_AT, 0)).then_inc(t_filled, 1)
                pe.wait_ge(loaded, 32)
                pe.wait_ge(gated_y, IC)
                pe.wait_ge(t_taken, 2 * IC)
                for n in range(2 * IC):
                    m, here = n // 2, slice(n % 2 * HALF, (n % 2 + 1) * HALF)
                    if n >= 4:
                        pe.wait_ge(h_ready, n - 3)
                    for k in range(2 * IC):
                        mm = nc.tensor.matmul(env.bank(n % 4), w_out1[:, k, m * P:(m + 1) * P],
                                              (y if k < IC else y_t)[:, k % IC, here],
                                              start=(k == 0), stop=(k == 2 * IC - 1))
                    mm.then_inc(h_filled, 1)
                pe.wait_ge(h_ready, 2 * IC)
                for t in range(NT):
                    if t >= 4:
                        pe.wait_ge(added, t - 3)
                    for k in range(IC):
                        mm = nc.tensor.matmul(env.psum[:, 4 + t % 4, 0:D], h1[:, k, t * P:(t + 1) * P], w_out2[:, k, :],
                                              start=(k == 0), stop=(k == IC - 1))
                    mm.then_inc(out_filled, 1)

            @block.scalar
            def _(act):
                for n in range(2 * IC):
                    act.wait_ge(t_filled, n + 1)
                    nc.scalar.copy(y_t[:, n // 2, n % 2 * HALF:(n % 2 + 1) * HALF], env.bank(n)).then_inc(t_taken, 1)
                act.wait_ge(gated_y, IC)
                for n in range(2 * IC):
                    act.wait_ge(h_filled, n + 1)
                    nc.scalar.activation(h1[:, n // 2, n % 2 * HALF:(n % 2 + 1) * HALF], env.bank(n % 4), ACT.Relu
                                         ).then_inc(h_ready, 1)


def l0_attn(env):
    nc = env.nc
    normalise(env, env.x, transpose=False)
    SEG, DH = 32, 64
    PAIRS = HEADS // 2
    HT = 2 * NT
    sem = env.sem
    (consts_loaded, w_loaded, w_out_loaded, beta_ready, cleared) = (
        sem(n) for n in ("consts_loaded", "w_loaded", "w_out_loaded", "beta_ready", "cleared"))
    (projected, feature_ready, sin_ready, cos_ready, roped, elu_ready, v_filled, v_taken, s_filled, t_filled,
     z_filled, s_taken, t_taken, shifted, exp_done, weights_s, wt_ready, pv_filled, o_taken, chain_s,
     out_filled, added) = (
        sem(n) for n in ("projected", "feature_ready", "sin_ready", "cos_ready", "roped", "elu_ready", "v_filled",
                         "v_taken", "s_filled", "t_filled", "z_filled", "s_taken", "t_taken", "shifted", "exp_done",
                         "weights_chain", "wt_ready", "pv_filled", "o_taken", "chain", "out_filled", "added"))
    with ExitStack() as ctx:
        def sb(name, shape, dtype=F32):
            return env.sbuf(name, shape, dtype, ctx)

        w = sb("w_qkv", [P, DC, 5, P])
        w_out = sb("w_out", [P, PAIRS, D])
        cos, sin, causal = sb("cos", [P, S]), sb("sin", [P, S]), sb("causal", [P, SEG])
        z_col = sb("z_col", [P, 2])
        beta, rest = sb("beta", [P, HEADS]), sb("one_minus_beta", [P, HEADS])
        roped_t, sin_part, expo, relu, elu = (sb(n, [P, 2, T]) for n in ("roped", "sin_part", "expo", "relu", "elu"))
        v = sb("v", [P, NT, P])
        local, memory = sb("local", [P, HT, SEG]), sb("memory", [P, HT, SEG])
        peak, total, inverse, m_total, m_inverse = (sb(n, [P, HT]) for n in ("peak", "total", "inverse", "m_total",
                                                                            "m_inverse"))
        weight_t = sb("weight_t", [P, HT, P])
        o_t = sb("o_t", [P, PAIRS, T])
        loads = [(cos[:, :], "rope_cos"), (sin[:, :], "rope_sin"), (causal[:, :], "causal"), (z_col[:, :], "z_col")]

        L = 10

        def banks(k, n):
            return env.psum[:, k:k + n, :].rearrange("p k n -> p (k n)")

        def first_loads(sp):
            for dst, src in loads:
                sp.dma_start(dst, env.dram[src]).then_inc(consts_loaded, 16)
            sp.dma_start(beta[:, :], env.dram["l0a_beta"].partition_broadcast(P)).then_inc(consts_loaded, 16)
            sp.dma_start(w[:, :, :, :], env.dram["l0a_w"][0]).then_inc(w_loaded, 16)
            sp.dma_start(w_out[:, :, :], env.dram["l0a_w_out"]).then_inc(w_out_loaded, 16)

        normalise(env, env.xn, gain="l0a_gain", shift="l0a_shift", early=first_loads)

        with nc.Block() as block:

            @block.sync
            def _(sp):
                with sp.Fori(0, PAIRS - 1) as c:
                    sp.wait_ge(v_filled, c + 1)
                    sp.dma_start(w[:, :, :, :], env.dram["l0a_w"][bass.ds(c + 1, 1)].rearrange(
                        "o p k j n -> p (o k) j n")).then_inc(w_loaded, 16)

            @block.tensor
            def _(pe):
                pe.wait_ge(consts_loaded, 16 * (len(loads) + 1))

                def project(j):
                    for h in range(2):
                        for k in range(DC):
                            mm = nc.tensor.matmul(env.bank(2 * j + h), w[:, k, j, :],
                                                  env.xt[:, k, h * HALF:(h + 1) * HALF],
                                                  start=(k == 0), stop=(k == DC - 1))
                    mm.then_inc(projected, 1)

                def project_values(c):
                    pe.wait_ge(cos_ready, c * 2 + 1)
                    for t in range(NT):
                        for k in range(DC):
                            mm = nc.tensor.matmul(env.psum[:, t // 4, t % 4 * P:(t % 4 + 1) * P],
                                                  env.xt[:, k, t * P:(t + 1) * P], w[:, k, 4, :],
                                                  start=(k == 0), stop=(k == DC - 1))
                    mm.then_inc(v_filled, 1)

                def attend(c, more):
                    pe.wait_ge(v_taken, c + 1)
                    for part, (ready, x) in enumerate(((roped, roped_t), (elu_ready, elu))):
                        pe.wait_ge(ready, c * 2 + 2)
                        if part == 1:
                            pe.wait_ge(cos_ready, c * 2 + 2)
                        for h in range(2):
                            rows = slice(DH * h, DH * h + DH)
                            for t in range(NT):
                                here = slice(t * P, (t + 1) * P)
                                mm = nc.tensor.matmul(
                                    env.psum[:, 4 * part + 2 * h + t // 4, t % 4 * P:(t % 4 + 1) * P],
                                    x[rows, 0, here], x[rows, 1, here], start=True, stop=True,
                                    tile_position=(DH * h, 0))
                        mm.then_inc((s_filled, t_filled)[part], 1)
                    pe.wait_ge(s_taken, c * 4 + 4)
                    for t in range(NT):
                        mm = nc.tensor.matmul(env.psum[:, 0, 2 * t:2 * t + 2], elu[:, 0, t * P:(t + 1) * P], z_col[:, :],
                                              start=True, stop=True)
                    mm.then_inc(z_filled, 1)
                    if more:
                        pe.wait_ge(w_loaded, c * 16 + 32)
                        project(1)
                        pe.wait_ge(chain_s, c * L + 3)
                        project(0)
                        pe.wait_ge(t_taken, c * 2 + 2)
                        project(2)
                    pe.wait_ge(wt_ready, c * 6 + 6)
                    for h in range(2):
                        for t in range(NT):
                            mm = nc.tensor.matmul(
                                env.psum[DH * h:DH * h + DH, 6 + t // 4, t % 4 * P:(t % 4 + 1) * P],
                                v[:, t, DH * h:DH * h + DH], weight_t[:, NT * h + t, :], start=True, stop=True,
                                tile_position=(0, DH * h))
                    mm.then_inc(pv_filled, 1)
                    if more:
                        pe.wait_ge(o_taken, c + 1)
                        project(3)
                        project_values(c + 1)

                pe.wait_ge(w_loaded, 16)
                for j in (1, 0, 2, 3):
                    project(j)
                project_values(0)
                with pe.Fori(0, PAIRS - 1) as c:
                    attend(c, more=True)
                attend(PAIRS - 1, more=False)
                pe.wait_ge(o_taken, PAIRS)
                pe.wait_ge(w_out_loaded, 16)
                for t in range(NT):
                    if t >= 4:
                        pe.wait_ge(added, t - 3)
                    for k in range(PAIRS):
                        mm = nc.tensor.matmul(env.psum[:, t % 4, 0:D], o_t[:, k, t * P:(t + 1) * P], w_out[:, k, :],
                                              start=(k == 0), stop=(k == PAIRS - 1))
                    mm.then_inc(out_filled, 1)

            @block.scalar
            def _(act):
                act.wait_ge(consts_loaded, 16 * (len(loads) + 1))
                nc.scalar.activation(beta[:, :], beta[:, :], ACT.Sigmoid).then_inc(beta_ready, 1)

                def features(c, s):
                    act.wait_ge(projected, c * 4 + (s + 2))
                    at_least(act, elu_ready, c * 2)
                    nc.scalar.activation(expo[:, s, :], banks(4 * s, 2), ACT.Exp)
                    nc.scalar.activation(relu[:, s, :], banks(4 * s, 2), ACT.Relu).then_inc(feature_ready, 1)

                def take_values(c):
                    act.wait_ge(v_filled, c + 1)
                    nc.scalar.copy(v[:, :, :].rearrange("p t n -> p (t n)"), banks(0, 2)).then_inc(v_taken, 1)

                def finish(c, more):
                    act.wait_ge(shifted, c + 1)
                    nc.scalar.activation(local[:, :, :], local[:, :, :], ACT.Exp).then_inc(exp_done, 1)
                    if more:
                        features(c + 1, 0)
                        features(c + 1, 1)
                    pair = slice(c, c + 1) if isinstance(c, int) else bass.ds(c, 1)
                    act.wait_ge(pv_filled, c + 1)
                    nc.scalar.copy(o_t[:, pair, :].rearrange("p o n -> p (o n)"), banks(6, 2)).then_inc(o_taken, 1)
                    if more:
                        take_values(c + 1)

                features(0, 0)
                features(0, 1)
                take_values(0)
                with act.Fori(0, PAIRS - 1) as c:
                    finish(c, more=True)
                finish(PAIRS - 1, more=False)

            @block.gpsimd
            def _(pool):
                nc.gpsimd.memset(weight_t[:, :, :], 0.0).then_inc(cleared, 1)
                nc.gpsimd.memset(memory[:, :, :], 0.0).then_inc(cleared, 1)
                with pool.Fori(0, PAIRS) as c:
                    pool.wait_ge(sin_ready, 2 * c + 1)
                    pool.wait_ge(cos_ready, 2 * c + 1)
                    nc.gpsimd.tensor_tensor(roped_t[:, 0, :], roped_t[:, 0, :], sin_part[:, 0, :], ALU.add
                                            ).then_inc(roped, 1)

            @block.vector
            def _(dve):
                dve.wait_ge(beta_ready, 1)
                nc.vector.tensor_scalar(rest[:, :], beta[:, :], -1.0, 1.0, ALU.mult, ALU.add).then_inc(beta_ready, 1)
                dve.wait_ge(beta_ready, 2)
                dve.wait_ge(cleared, 2)
                with dve.Fori(0, PAIRS) as c:
                    chain = Chain(dve, chain_s, c * L)

                    def over_batches(x):
                        return x.rearrange("p (b s) -> p b s", s=S)

                    def table(x):
                        return x[:, None, :].to_broadcast([P, B, S])

                    def times_sin(s):
                        dve.wait_ge(projected, 4 * c + (4 if s else 1))
                        nc.vector.tensor_tensor(over_batches(sin_part[:, s, :]), over_batches(banks(4 * s + 2, 2)),
                                                table(sin), ALU.mult).then_inc(sin_ready, 1)

                    def times_cos(s):
                        dve.wait_ge(feature_ready, 2 * c + s + 1)
                        nc.vector.tensor_tensor(over_batches(roped_t[:, s, :]), over_batches(banks(4 * s, 2)),
                                                table(cos), ALU.mult).then_inc(cos_ready, 1)
                        nc.vector.scalar_tensor_tensor(elu[:, s, :], expo[:, s, :], 1.0, relu[:, s, :],
                                                       ALU.min, ALU.add).then_inc(elu_ready, 1)

                    times_sin(0)
                    times_cos(0)
                    times_cos(1)
                    times_sin(1)
                    dve.wait_ge(sin_ready, 2 * c + 2)
                    dve.wait_ge(cos_ready, 2 * c + 2)
                    nc.vector.tensor_tensor(roped_t[:, 1, :], roped_t[:, 1, :], sin_part[:, 1, :], ALU.add
                                            ).then_inc(roped, 1)
                    full = [P, HT, SEG]
                    s_psum = banks(0, 4).rearrange("p (r n) -> p r n", n=P)
                    t_psum = banks(4, 4).rearrange("p (r n) -> p r n", n=P)
                    dve.wait_ge(s_filled, c + 1)
                    for g in range(4):
                        rows = slice(SEG * g, SEG * g + SEG)
                        nc.vector.scalar_tensor_tensor(local[rows, :, :], s_psum[rows, :, rows], DH ** -0.5,
                                                       causal[rows, None, :].to_broadcast([SEG, HT, SEG]),
                                                       ALU.mult, ALU.add).then_inc(s_taken, 1)
                    dve.wait_ge(s_taken, 4 * c + 4)
                    chain(nc.vector.tensor_reduce(peak[:, :], local[:, :, :], AX.X, ALU.max))
                    nc.vector.tensor_tensor(local[:, :, :], local[:, :, :], peak[:, :, None].to_broadcast(full),
                                            ALU.subtract).then_inc(shifted, 1)
                    dve.wait_ge(t_filled, c + 1)
                    for g in (1, 3):
                        rows = slice(SEG * g, SEG * g + SEG)
                        nc.vector.tensor_copy(memory[rows, :, :], t_psum[rows, :, SEG * (g - 1):SEG * g]
                                              ).then_inc(t_taken, 1)
                    dve.wait_ge(t_taken, 2 * c + 2)
                    chain(nc.vector.tensor_reduce(m_total[:, :], memory[:, :, :], AX.X, ALU.add))
                    dve.wait_ge(z_filled, c + 1)
                    by_head = [P, 2, NT]
                    chain(nc.vector.scalar_tensor_tensor(m_total[:, :].rearrange("p (h t) -> p h t", h=2),
                                                         env.psum[:, 0, 0:HT].rearrange("p (t h) -> p h t", h=2), 1e-6,
                                                         m_total[:, :].rearrange("p (h t) -> p h t", h=2),
                                                         ALU.add, ALU.add))
                    chain(nc.vector.reciprocal(m_inverse[:, :], m_total[:, :]))
                    chain(nc.vector.tensor_tensor(m_inverse[:, :].rearrange("p (h t) -> p h t", h=2),
                                                  m_inverse[:, :].rearrange("p (h t) -> p h t", h=2),
                                                  beta[:, bass.ds(2 * c, 2), None].to_broadcast(by_head), ALU.mult))
                    chain(nc.vector.tensor_tensor(memory[:, :, :], memory[:, :, :],
                                                  m_inverse[:, :, None].to_broadcast(full), ALU.mult))
                    dve.wait_ge(exp_done, c + 1)
                    chain(nc.vector.tensor_reduce(total[:, :], local[:, :, :], AX.X, ALU.add))
                    chain(nc.vector.reciprocal(inverse[:, :], total[:, :]))
                    chain(nc.vector.tensor_tensor(inverse[:, :].rearrange("p (h t) -> p h t", h=2),
                                                  inverse[:, :].rearrange("p (h t) -> p h t", h=2),
                                                  rest[:, bass.ds(2 * c, 2), None].to_broadcast(by_head), ALU.mult))
                    chain(nc.vector.tensor_tensor(local[:, :, :], local[:, :, :],
                                                  inverse[:, :, None].to_broadcast(full), ALU.mult))
                    dve.wait_ge(pv_filled, c)
                    for g in range(4):
                        rows = slice(SEG * g, SEG * g + SEG)
                        nc.vector.transpose(weight_t[rows, :, rows], local[rows, :, :]).then_inc(wt_ready, 1)
                    for g in (1, 3):
                        rows, before = slice(SEG * g, SEG * g + SEG), slice(SEG * (g - 1), SEG * g)
                        nc.vector.transpose(weight_t[before, :, rows], memory[rows, :, :]).then_inc(wt_ready, 1)
                    dve.wait_ge(wt_ready, 6 * c + 6)
                    assert chain.n == L
                for t in range(NT):
                    dve.wait_ge(out_filled, t + 1)
                    nc.vector.tensor_tensor(env.x[:, t, :], env.x[:, t, :], env.psum[:, t % 4, 0:D],
                                            ALU.add).then_inc(added, 1)


def more_layouts(a, out, rows, column):
    for n in ("q", "k", "v", "o"):
        out[f"l1a_w{n}"] = rows(a[f"L1_attn_W_{n}"])
    out["l1a_down"] = rows(a["L1_attn_W_down_kv"])
    out["l1a_up_k"], out["l1a_up_v"] = a["L1_attn_W_up_k"], a["L1_attn_W_up_v"]
    out["l2a_w_in"], out["l2a_w_out"] = rows(a["L2_attn_W_in"]), rows(a["L2_attn_W_out"])
    out["l2a_gamma"], out["l2a_beta"] = column(a["L2_attn_gamma"]), column(a["L2_attn_beta"])
    out["l2a_a"], out["l2a_b_in"] = column(a["L2_attn_A"]), column(a["L2_attn_b_in"])
    out["l2a_b_out"] = a["L2_attn_b_out"]
    out["l1f_w1"], out["l1f_w2"] = rows(a["L1_ffn_w1"].T), rows(a["L1_ffn_w2"].T)
    out["l1f_conv_w"] = a["L1_ffn_conv_w"].reshape(-1, P, 3).transpose(1, 0, 2)
    out["l1f_conv_b"] = column(a["L1_ffn_conv_b"])
    w = a["L3_attn_W_x"].T
    gap = np.zeros((w.shape[0], 16), w.dtype)
    out["l3a_w_x"] = rows(np.concatenate([w[:, 0:16], gap, w[:, 16:32], gap, w[:, 32:48]], axis=1))
    out["l3a_w_in"] = rows(a["L3_attn_W_in"].T)
    out["l3a_conv_w"] = a["L3_attn_conv_w"].reshape(-1, P, 4).transpose(1, 0, 2)
    out["l3a_conv_b"] = column(a["L3_attn_conv_b"])
    out["l3a_w_dt"], out["l3a_b_dt"] = a["L3_attn_W_dt"].T, column(a["L3_attn_b_dt"])
    out["l3a_d"], out["l3a_a"] = column(a["L3_attn_Dp"]), a["L3_attn_A_log"].reshape(-1, P, 16).transpose(1, 0, 2)
    out["l3a_a_t"] = a["L3_attn_A_log"].T
    out["l3a_w_out1"], out["l3a_w_out2"] = rows(a["L3_attn_W_out1"].T), rows(a["L3_attn_W_out2"].T)

    w = a["L0_attn_w_qkv"].reshape(D, 3, 8, P)
    swapped = w.reshape(D, 3, 8, P // 2, 2)[..., ::-1].reshape(w.shape)
    five = np.stack([w[:, 0], swapped[:, 0], w[:, 1], swapped[:, 1], w[:, 2]], axis=2)
    out["l0a_w"] = five.reshape(DC, P, 8, 5, P).transpose(2, 1, 0, 3, 4)
    out["l0a_w_out"] = rows(a["L0_attn_w_out"])
    out["l0a_gain"], out["l0a_shift"] = column(a["L0_attn_ln_g"]), column(a["L0_attn_ln_b"])
    out["l0a_beta"] = a["L0_attn_mem_beta"].reshape(HEADS)


def build(nc, dram, stages=None):
    with ExitStack() as ctx:
        env = Env(nc, ctx, dram)
        load_stream(env)
        for n, stage in enumerate(STAGES):
            if stages is None or n in stages:
                stage(env)
                env.end_stage()
        store_stream(env)


def l0_xattn(env):
    cross_attention(env, "l0x", "l0x_wq", "l0x_wk", "l0x_wv", "l0x_wo", "l0x_bq", "l0x_bk", "l0x_bv", "l0x_bo",
                    lambdas=[f"L0_xattn_lambda_{n}" for n in ("q1", "k1", "q2", "k2")])


def make_xattn(n, mask=None):
    def stage(env):
        cross_attention(env, f"l{n}x", *(f"l{n}x_{w}" for w in ("wq", "wk", "wv", "wo", "bq", "bk", "bv", "bo")),
                        mask=mask)
    return stage


STAGES = [l0_xattn, l0_attn, l0_ffn, make_xattn(1), l1_attn, l1_ffn,
          make_xattn(2, "mask"), l2_attn, l2_ffn, make_xattn(3), l3_attn, l3_ffn]


def constants():
    p = np.arange(P)
    out = {"identity": np.eye(P)}
    for subs in (2, 4):
        out[f"owner_mask_{subs}"] = np.arange(6 * HD)[:, None] % (2 * HD) // (2 * HD // subs) == np.arange(subs)
    for n in (4, 8, 16):
        out[f"ties_{n}"] = np.broadcast_to(np.tril(np.ones((n, n)), -1), (P, n, n))
    out["pair_mask"] = p[:, None] // 16 == np.arange(8)
    distance = np.abs(np.arange(S)[:, None] - np.arange(S)[None, :])
    out["decay"] = np.tile(np.exp(-0.01 * distance) / np.sqrt(D), (2, 1))
    freqs = (10000.0 ** (-np.arange(0, 64, 2, dtype=np.float32) / 64)).astype(np.float32)
    angle = (np.arange(S, dtype=np.float32)[None, :] * np.repeat(freqs, 2)[:, None]).astype(np.float32)
    angle = np.tile(angle, (2, 1))
    out["rope_cos"] = np.cos(angle)
    out["rope_sin"] = np.sin(angle) * np.where(p % 2, 1.0, -1.0)[:, None]
    out["causal"] = np.where(np.arange(32)[None, :] <= p[:, None] % 32, 0.0, MASKED)
    out["z_col"] = 1e-6 * (p[:, None] // 64 == np.arange(2))
    out["eye_rows"] = np.arange(80)[:, None] % 32 == np.arange(16)
    return {k: np.ascontiguousarray(v, dtype=np.float32) for k, v in out.items()}


def lay_out(inputs):
    a = {k: np.asarray(v) for k, v in inputs.items()}
    out = constants()

    def rows(w):
        return np.moveaxis(w.reshape(*w.shape[:-2], -1, P, w.shape[-1]), -3, -2)

    def column(v):
        return np.moveaxis(v.reshape(*v.shape[:-1], -1, P), -1, -2)

    out["x"] = a["x"].reshape(T, D)
    out["ctx_t"] = rows(a["ctx_1024"].transpose(0, 2, 1))
    out["mask"] = a["mask_SxS2_ik0"]
    w, b = a["L0_xattn_in_proj_weight"], a["L0_xattn_in_proj_bias"]
    for i, n in enumerate("qkv"):
        out[f"l0x_w{n}"] = rows(w[i * D:(i + 1) * D].T)
        out[f"l0x_b{n}"] = b[i * D:(i + 1) * D]
    out["l0x_wo"] = rows(a["L0_xattn_out_proj_weight"].T)
    out["l0x_bo"] = a["L0_xattn_out_proj_bias"]
    for n in ("q1", "k1", "q2", "k2"):
        out[f"L0_xattn_lambda_{n}"] = a[f"L0_xattn_lambda_{n}"]
    for layer in (1, 2, 3):
        for n in "qkvo":
            w = a[f"L{layer}_xattn_W{n}"]
            out[f"l{layer}x_w{n}"] = rows(w if layer == 1 else w.T)
            out[f"l{layer}x_b{n}"] = a[f"L{layer}_xattn_b{n}"]
    for layer in range(4):
        out[f"l{layer}x_bk"] = column(out[f"l{layer}x_bk"])
        w = out[f"l{layer}x_wq"].reshape(P, DC, HEADS // 2, 1, 2 * HD)
        out[f"l{layer}x_wq"] = np.broadcast_to(w, (P, DC, HEADS // 2, 3, 2 * HD)).reshape(P, DC, HEADS // 2, 6 * HD)
        b = out[f"l{layer}x_bq"].reshape(HEADS // 2, 1, 2 * HD)
        out[f"l{layer}x_bq"] = np.broadcast_to(b, (HEADS // 2, 3, 2 * HD)).reshape(HEADS // 2, 6 * HD).T

    def steps_up(name, shared):
        w = np.concatenate([a[name], a[shared].reshape(D, 2, P).transpose(1, 0, 2)])
        return rows(w.reshape(3, 6, D, P).transpose(0, 2, 1, 3).reshape(3, D, 6 * P))

    out["l0f_gate"] = steps_up("L0_ffn_w_gate", "L0_ffn_sw_gate")
    out["l0f_up"] = steps_up("L0_ffn_w_up", "L0_ffn_sw_up")
    w = np.concatenate([a["L0_ffn_w_down"], a["L0_ffn_sw_down"].reshape(2, P, D)])
    out["l0f_down"] = rows(w.reshape(3, 6 * P, D))
    out["l0f_router"] = rows(a["L0_ffn_gate_kernel"])
    out["l0f_bias"] = a["L0_ffn_gate_bias"]

    out["l2f_router"] = rows(a["L2_ffn_router_w"].T)
    out["l2f_w1"] = rows(a["L2_ffn_expert_w1"].transpose(0, 2, 1))
    out["l2f_w2"] = rows(a["L2_ffn_expert_w2"].transpose(0, 2, 1))
    out["l2f_b1"] = column(a["L2_ffn_expert_b1"])
    out["l2f_b2"] = a["L2_ffn_expert_b2"]

    out["l3f_ln_w"] = column(a["L3_ffn_ln_w"])
    out["l3f_router"] = rows(a["L3_ffn_Wg"])
    out["l3f_bias"] = a["L3_ffn_bg"]
    for n in "ab":
        out[f"l3f_w1{n}"] = rows(a[f"L3_ffn_W1{n}"])
        out[f"l3f_b1{n}"] = column(a[f"L3_ffn_b1{n}"])
    out["l3f_w2"] = rows(a["L3_ffn_W2"])
    out["l3f_b2"] = a["L3_ffn_b2"]
    more_layouts(a, out, rows, column)
    return {k: np.ascontiguousarray(v) for k, v in out.items()}


def kernel(**inputs):
    import concourse.bacc as bacc
    from concourse.bass_utils import run_bass_kernel_spmd

    arrays = lay_out(inputs)
    nc = bacc.Bacc("TRN2", target_bir_lowering=False, num_devices=1)
    dram = {k: nc.dram_tensor(f"in_{k}", v.shape, mybir.dt.from_np(v.dtype), kind="ExternalInput").ap()
            for k, v in arrays.items()}
    dram["out"] = nc.dram_tensor("out_x", (T, D), F32, kind="ExternalOutput").ap()
    build(nc, dram)
    result = run_bass_kernel_spmd(nc, [{f"in_{k}": v for k, v in arrays.items()}], core_ids=[0])
    return np.asarray(result.results[0]["out_x"]).reshape(B, S, D)
```
